# Optimizing a Trainium2 kernel written in Bass

```python
import numpy as np
import jax
import jax.numpy as jnp

def _softmax(x, axis=-1):
    return jax.nn.softmax(x, axis=axis)

def _gelu(x):
    return jax.nn.gelu(x, approximate=True)

def _silu(x):
    return jax.nn.silu(x)

def _sigmoid(x):
    return jax.nn.sigmoid(x)

def _layernorm(x, axis=-1, eps=1e-05):
    m = jnp.mean(x, axis=axis, keepdims=True)
    v = jnp.var(x, axis=axis, keepdims=True)
    return (x - m) / jnp.sqrt(v + eps)

def _scatter_add(tgt, idx, src, axis=0):
    return tgt.at[idx].add(src)

def _segment_sum(src, seg, n):
    return jax.ops.segment_sum(src, seg, n)
kernel_name = 'mk_flamingo_gated_d2_seqx_r4_841d1a'

def setup_inputs(seed: int=0):
    np.random.seed(seed)
    _w = jnp.asarray

    def _rec_inputs():
        import jax
        import jax.numpy as jnp
        _rk = jax.random.key(seed)
        x = -0.0002928 + 1 * jax.random.normal(jax.random.fold_in(_rk, 1), (16, 256, 256), jnp.float32)
        _lenS = 256 - jax.random.randint(jax.random.fold_in(_rk, 7), (16,), 0, max(1, 256 // 4) + 1, jnp.int32)
        _lenS2 = 77 - jax.random.randint(jax.random.fold_in(_rk, 8), (16,), 0, max(1, 77 // 4) + 1, jnp.int32)
        _ctx_1024P = jax.random.normal(jax.random.fold_in(_rk, 11), (16, 16, 256), jnp.float32)
        _ctx_1024c = jax.random.dirichlet(jax.random.fold_in(_rk, 511), 0.3 * jnp.ones((16,), jnp.float32), (16, 77))
        _ctx_1024t = jnp.einsum('bsk,bkd->bsd', _ctx_1024c, _ctx_1024P)
        _ctx_1024t = _ctx_1024t * jax.lax.rsqrt(jnp.mean(jnp.square(_ctx_1024t)) + 1e-12) * 0.953939
        ctx_1024 = -1.39393e-06 + 0.999914 * (_ctx_1024t + 0.3 * jax.random.normal(jax.random.fold_in(_rk, 611), (16, 77, 256), jnp.float32))
        _g = jax.random.normal(jax.random.fold_in(_rk, 9001), (2, 2), jnp.float32)
        _g = jnp.sign(_g) * jnp.maximum(jnp.abs(_g), 1.0) + (_g == 0) * 1.0
        g_xattn = _g[0]
        g_ffn = _g[1]
        return (x, ctx_1024, g_xattn, g_ffn)
    x, ctx_1024, g_xattn, g_ffn = _rec_inputs()

    def _L0_xattn_setup():
        import jax, jax.numpy as jnp
        import numpy as np
        import math
        NUM_HEADS = 16
        key = jax.random.key(seed)
        ks = jax.random.split(key, 9)
        B, S, D = (2, 512, 256)
        hd = D // NUM_HEADS
        s_in = 1.0 / math.sqrt(D)
        return {'q': jax.random.normal(ks[0], (B, S, D), jnp.float32), 'k': jax.random.normal(ks[1], (B, S, D), jnp.float32), 'v': jax.random.normal(ks[2], (B, S, D), jnp.float32), 'Wq': jax.random.normal(ks[3], (D, D), jnp.float32) * s_in, 'bq': jnp.zeros((D,), jnp.float32), 'Wk': jax.random.normal(ks[4], (D, hd), jnp.float32) * s_in, 'bk': jnp.zeros((hd,), jnp.float32), 'Wv': jax.random.normal(ks[5], (D, hd), jnp.float32) * s_in, 'bv': jnp.zeros((hd,), jnp.float32)}
    _L0_xattn_all = _L0_xattn_setup()
    _L0_xattn_in = {k: v for k, v in _L0_xattn_all.items() if k in ('Wq', 'bq', 'Wk', 'bk', 'Wv', 'bv')}
    del _L0_xattn_all

    def _L0_ffn_setup():
        import jax, jax.numpy as jnp
        import numpy as np
        LN_EPS = 1e-05
        NORM_EPS = 1e-12

        def _layernorm(x, gamma, beta):
            mu = x.mean(axis=-1, keepdims=True)
            var = ((x - mu) ** 2).mean(axis=-1, keepdims=True)
            return (x - mu) * jax.lax.rsqrt(var + LN_EPS) * gamma + beta

        def _l2norm(x, axis):
            n = jnp.sqrt((x ** 2).sum(axis=axis, keepdims=True))
            return x / jnp.maximum(n, NORM_EPS)
        key = jax.random.key(seed)
        ks = jax.random.split(key, 4)
        B, N, D, E, S, H = (64, 64, 256, 16, 16, 64)
        x = jax.random.normal(ks[0], (B, N, D), dtype=jnp.float32)
        mu = jax.random.normal(ks[1], (D, E, S), dtype=jnp.float32) / np.sqrt(D)
        w1 = jax.random.normal(ks[2], (E, D, H), dtype=jnp.float32) * np.sqrt(2.0 / D)
        w2 = jax.random.normal(ks[3], (E, H, D), dtype=jnp.float32) * np.sqrt(2.0 / (H + D))
        return {'x': x, 'ln_gamma': jnp.ones((D,), jnp.float32), 'ln_beta': jnp.zeros((D,), jnp.float32), 'mu': mu, 'scale': jnp.ones((1,), jnp.float32), 'w1': w1, 'b1': jnp.zeros((E, H), jnp.float32), 'w2': w2, 'b2': jnp.zeros((E, D), jnp.float32)}
    _L0_ffn_all = _L0_ffn_setup()
    _L0_ffn_in = {k: v for k, v in _L0_ffn_all.items() if k in ('ln_gamma', 'ln_beta', 'mu', 'scale', 'w1', 'b1', 'w2', 'b2')}
    del _L0_ffn_all

    def _L1_xattn_setup():
        import jax, jax.numpy as jnp
        import numpy as np
        B, S, D, DFF = (4, 512, 256, 1024)
        EPS = 1e-05

        def layernorm(x, gamma, beta):
            mu = jnp.mean(x, axis=-1, keepdims=True)
            var = jnp.var(x, axis=-1, keepdims=True)
            return (x - mu) * jax.lax.rsqrt(var + EPS) * gamma + beta

        def attention(Q, K, V, causal):
            d_k = Q.shape[-1]
            scores = jnp.einsum('bqd,bkd->bqk', Q, K) / jnp.sqrt(jnp.asarray(d_k, Q.dtype))
            if causal:
                q_len, k_len = (scores.shape[-2], scores.shape[-1])
                mask = jnp.tril(jnp.ones((q_len, k_len), dtype=bool))
                scores = jnp.where(mask[None], scores, jnp.asarray(-jnp.inf, scores.dtype))
            w = jax.nn.softmax(scores, axis=-1)
            return jnp.einsum('bqk,bkd->bqd', w, V)
        key = jax.random.key(seed)
        ks = jax.random.split(key, 12)
        sd = 0.02
        return {'y': jax.random.normal(ks[0], (B, S, D), jnp.float32), 'Z': jax.random.normal(ks[1], (B, S, D), jnp.float32), 'w1': jax.random.normal(ks[2], (D, DFF), jnp.float32) * sd, 'b1': jnp.zeros((DFF,), jnp.float32), 'w2': jax.random.normal(ks[3], (DFF, D), jnp.float32) * sd, 'b2': jnp.zeros((D,), jnp.float32), 'g1': jnp.ones((D,), jnp.float32), 'beta1': jnp.zeros((D,), jnp.float32), 'g2': jnp.ones((D,), jnp.float32), 'beta2': jnp.zeros((D,), jnp.float32), 'g3': jnp.ones((D,), jnp.float32), 'beta3': jnp.zeros((D,), jnp.float32)}
    _L1_xattn_all = _L1_xattn_setup()
    _L1_xattn_in = {k: v for k, v in _L1_xattn_all.items() if k in ('w1', 'b1', 'w2', 'b2', 'g1', 'beta1', 'g2', 'beta2', 'g3', 'beta3')}
    del _L1_xattn_all

    def _L1_ffn_setup():
        import jax, jax.numpy as jnp
        import numpy as np
        D = 256
        H = 192
        E = 8
        K = 2
        NS = 2
        ROUTE_SCALE = 1.0

        def _gated_mlp(x, w1, w2):
            h = x @ w1.T
            y, g = jnp.split(h, 2, axis=-1)
            return y * jax.nn.silu(g) @ w2.T
        key = jax.random.key(seed)
        ks = jax.random.split(key, 6)
        s = 0.02
        return {'x': jax.random.normal(ks[0], (2, 256, D), jnp.float32), 'gate_w': jax.random.normal(ks[1], (E, D), jnp.float32) * s, 'W1': jax.random.normal(ks[2], (E, 2 * H, D), jnp.float32) * s, 'W2': jax.random.normal(ks[3], (E, D, H), jnp.float32) * s, 'Ws1': jax.random.normal(ks[4], (2 * NS * H, D), jnp.float32) * s, 'Ws2': jax.random.normal(ks[5], (D, NS * H), jnp.float32) * s}
    _L1_ffn_all = _L1_ffn_setup()
    _L1_ffn_in = {k: v for k, v in _L1_ffn_all.items() if k in ('gate_w', 'W1', 'W2', 'Ws1', 'Ws2')}
    del _L1_ffn_all
    return {'x': x, 'ctx_1024': ctx_1024, 'g_xattn': g_xattn, 'g_ffn': g_ffn, 'L0_xattn_Wq': _L0_xattn_in['Wq'], 'L0_xattn_bq': _L0_xattn_in['bq'], 'L0_xattn_Wk': _L0_xattn_in['Wk'], 'L0_xattn_bk': _L0_xattn_in['bk'], 'L0_xattn_Wv': _L0_xattn_in['Wv'], 'L0_xattn_bv': _L0_xattn_in['bv'], 'L0_ffn_ln_gamma': _L0_ffn_in['ln_gamma'], 'L0_ffn_ln_beta': _L0_ffn_in['ln_beta'], 'L0_ffn_mu': _L0_ffn_in['mu'], 'L0_ffn_scale': _L0_ffn_in['scale'], 'L0_ffn_w1': _L0_ffn_in['w1'], 'L0_ffn_b1': _L0_ffn_in['b1'], 'L0_ffn_w2': _L0_ffn_in['w2'], 'L0_ffn_b2': _L0_ffn_in['b2'], 'L1_xattn_w1': _L1_xattn_in['w1'], 'L1_xattn_b1': _L1_xattn_in['b1'], 'L1_xattn_w2': _L1_xattn_in['w2'], 'L1_xattn_b2': _L1_xattn_in['b2'], 'L1_xattn_g1': _L1_xattn_in['g1'], 'L1_xattn_beta1': _L1_xattn_in['beta1'], 'L1_xattn_g2': _L1_xattn_in['g2'], 'L1_xattn_beta2': _L1_xattn_in['beta2'], 'L1_xattn_g3': _L1_xattn_in['g3'], 'L1_xattn_beta3': _L1_xattn_in['beta3'], 'L1_ffn_gate_w': _L1_ffn_in['gate_w'], 'L1_ffn_W1': _L1_ffn_in['W1'], 'L1_ffn_W2': _L1_ffn_in['W2'], 'L1_ffn_Ws1': _L1_ffn_in['Ws1'], 'L1_ffn_Ws2': _L1_ffn_in['Ws2']}

def reference(x, ctx_1024, g_xattn, g_ffn, L0_xattn_Wq, L0_xattn_bq, L0_xattn_Wk, L0_xattn_bk, L0_xattn_Wv, L0_xattn_bv, L0_ffn_ln_gamma, L0_ffn_ln_beta, L0_ffn_mu, L0_ffn_scale, L0_ffn_w1, L0_ffn_b1, L0_ffn_w2, L0_ffn_b2, L1_xattn_w1, L1_xattn_b1, L1_xattn_w2, L1_xattn_b2, L1_xattn_g1, L1_xattn_beta1, L1_xattn_g2, L1_xattn_beta2, L1_xattn_g3, L1_xattn_beta3, L1_ffn_gate_w, L1_ffn_W1, L1_ffn_W2, L1_ffn_Ws1, L1_ffn_Ws2):
    import jax
    import jax.numpy as jnp

    def _L0_xattn_ref(q, k, v, Wq, bq, Wk, bk, Wv, bv):
        import jax, jax.numpy as jnp
        import numpy as np
        import math
        NUM_HEADS = 16
        B, S, D = q.shape
        H = NUM_HEADS
        hd = D // H
        qp = (q @ Wq + bq).reshape(B, H, S, hd)
        kp = k @ Wk + bk
        vp = v @ Wv + bv
        scale = 1.0 / math.sqrt(D)
        att = jnp.einsum('bhsd,btd->bhst', qp, kp) * scale
        att = jax.nn.softmax(att, axis=-1)
        out = jnp.einsum('bhst,btd->bhsd', att, vp)
        out = out.transpose(0, 2, 1, 3).reshape(B, S, D)
        return out

    def _L0_ffn_ref(x, ln_gamma, ln_beta, mu, scale, w1, b1, w2, b2):
        import jax, jax.numpy as jnp
        import numpy as np
        LN_EPS = 1e-05
        NORM_EPS = 1e-12

        def _layernorm(x, gamma, beta):
            mu = x.mean(axis=-1, keepdims=True)
            var = ((x - mu) ** 2).mean(axis=-1, keepdims=True)
            return (x - mu) * jax.lax.rsqrt(var + LN_EPS) * gamma + beta

        def _l2norm(x, axis):
            n = jnp.sqrt((x ** 2).sum(axis=axis, keepdims=True))
            return x / jnp.maximum(n, NORM_EPS)
        B, N, D = x.shape
        _, E, S = mu.shape
        xn = _layernorm(x, ln_gamma, ln_beta)
        x_unit = _l2norm(xn, axis=-1)
        mu_unit = _l2norm(mu, axis=0)
        logits = jnp.einsum('bnd,des->bnes', x_unit * scale, mu_unit)
        dispatch = jax.nn.softmax(logits, axis=1)
        combine = jax.nn.softmax(logits.reshape(B, N, E * S), axis=-1).reshape(B, N, E, S)
        slot_in = jnp.einsum('bnd,bnes->besd', xn, dispatch)
        h = jax.nn.gelu(jnp.einsum('besd,edh->besh', slot_in, w1) + b1[None, :, None, :], approximate=False)
        slot_out = jnp.einsum('besh,ehd->besd', h, w2) + b2[None, :, None, :]
        out = jnp.einsum('besd,bnes->bnd', slot_out, combine)
        return out

    def _L1_xattn_ref(y, Z, w1, b1, w2, b2, g1, beta1, g2, beta2, g3, beta3):
        import jax, jax.numpy as jnp
        import numpy as np
        B, S, D, DFF = (4, 512, 256, 1024)
        EPS = 1e-05

        def layernorm(x, gamma, beta):
            mu = jnp.mean(x, axis=-1, keepdims=True)
            var = jnp.var(x, axis=-1, keepdims=True)
            return (x - mu) * jax.lax.rsqrt(var + EPS) * gamma + beta

        def attention(Q, K, V, causal):
            d_k = Q.shape[-1]
            scores = jnp.einsum('bqd,bkd->bqk', Q, K) / jnp.sqrt(jnp.asarray(d_k, Q.dtype))
            if causal:
                q_len, k_len = (scores.shape[-2], scores.shape[-1])
                mask = jnp.tril(jnp.ones((q_len, k_len), dtype=bool))
                scores = jnp.where(mask[None], scores, jnp.asarray(-jnp.inf, scores.dtype))
            w = jax.nn.softmax(scores, axis=-1)
            return jnp.einsum('bqk,bkd->bqd', w, V)
        sa = attention(y, y, y, causal=True)
        y = layernorm(y + sa, g1, beta1)
        ca = attention(y, Z, Z, causal=False)
        y = layernorm(y + ca, g2, beta2)
        h = jax.nn.relu(jnp.einsum('bsd,df->bsf', y, w1) + b1)
        ff = jnp.einsum('bsf,fd->bsd', h, w2) + b2
        y = layernorm(y + ff, g3, beta3)
        return y

    def _L1_ffn_ref(x, gate_w, W1, W2, Ws1, Ws2):
        import jax, jax.numpy as jnp
        import numpy as np
        D = 256
        H = 192
        E = 8
        K = 2
        NS = 2
        ROUTE_SCALE = 1.0

        def _gated_mlp(x, w1, w2):
            h = x @ w1.T
            y, g = jnp.split(h, 2, axis=-1)
            return y * jax.nn.silu(g) @ w2.T
        x_shape = x.shape
        xf = x.reshape(-1, D)
        T = xf.shape[0]
        scores = jax.nn.softmax((xf @ gate_w.T).astype(jnp.float32), axis=-1)
        top_vals, top_idx = jax.lax.top_k(scores, K)
        weights = (top_vals * ROUTE_SCALE).astype(x.dtype)
        w_dense = jnp.zeros((T, E), x.dtype).at[jnp.arange(T)[:, None], top_idx].set(weights)
        h = jnp.einsum('td,ehd->teh', xf, W1)
        y, g = jnp.split(h, 2, axis=-1)
        eo = jnp.einsum('teh,edh->ted', y * jax.nn.silu(g), W2)
        z = jnp.einsum('te,ted->td', w_dense, eo)
        z = z + _gated_mlp(xf, Ws1, Ws2)
        return z.reshape(x_shape)
    x = x + jnp.tanh(g_xattn[0]) * _L0_xattn_ref(_layernorm(x, axis=-1), ctx_1024, ctx_1024, L0_xattn_Wq, L0_xattn_bq, L0_xattn_Wk, L0_xattn_bk, L0_xattn_Wv, L0_xattn_bv)
    x = x + jnp.tanh(g_ffn[0]) * _L0_ffn_ref(_layernorm(x, axis=-1), L0_ffn_ln_gamma, L0_ffn_ln_beta, L0_ffn_mu, L0_ffn_scale, L0_ffn_w1, L0_ffn_b1, L0_ffn_w2, L0_ffn_b2)
    x = x + jnp.tanh(g_xattn[1]) * _L1_xattn_ref(_layernorm(x, axis=-1), ctx_1024, L1_xattn_w1, L1_xattn_b1, L1_xattn_w2, L1_xattn_b2, L1_xattn_g1, L1_xattn_beta1, L1_xattn_g2, L1_xattn_beta2, L1_xattn_g3, L1_xattn_beta3)
    x = x + jnp.tanh(g_ffn[1]) * _L1_ffn_ref(_layernorm(x, axis=-1), L1_ffn_gate_w, L1_ffn_W1, L1_ffn_W2, L1_ffn_Ws1, L1_ffn_Ws2)
    return x

_drawn_inputs = setup_inputs


def setup_inputs(seed=0):
    import zlib

    import numpy as np

    out = dict(_drawn_inputs(seed))
    spreads = {'g_ffn': (-1.0, 0.6),
     'L0_xattn_bq': (0.0, 0.8),
     'L0_xattn_bk': (0.0, 2.0),
     'L0_xattn_bv': (0.0, 0.1),
     'L0_ffn_ln_gamma': (1.0, 0.6),
     'L0_ffn_ln_beta': (0.0, 0.8),
     'L0_ffn_b1': (0.0, 0.8),
     'L0_ffn_b2': (0.0, 0.655),
     'L1_xattn_b1': (0.0, 0.1),
     'L1_xattn_b2': (0.0, 0.1),
     'L1_xattn_g1': (1.0, 0.2),
     'L1_xattn_beta1': (0.0, 0.1),
     'L1_xattn_g2': (1.0, 0.2),
     'L1_xattn_beta2': (0.0, 0.1),
     'L1_xattn_g3': (1.0, 0.2),
     'L1_xattn_beta3': (0.0, 0.1)}
    factors = {'L0_ffn_mu': 45.222,
     'L1_ffn_gate_w': 8.0,
     'L1_ffn_W1': 8.0,
     'L1_ffn_W2': 8.0,
     'L1_ffn_Ws1': 8.0,
     'L1_ffn_Ws2': 8.0}
    for name, (base, spread) in spreads.items():
        noise = np.random.default_rng([zlib.crc32(name.encode()), seed]).standard_normal(out[name].shape)
        drawn = base * np.exp(spread * noise) if base else spread * noise
        out[name] = jnp.asarray(drawn.astype(out[name].dtype))
    for name, factor in factors.items():
        out[name] = (out[name] * factor).astype(out[name].dtype)
    return out
```

```python
from contextlib import ExitStack

import concourse.bass as bass
from concourse import mybir

F32 = mybir.dt.float32
F32R = mybir.dt.float32r
F16 = mybir.dt.float16
BF16 = mybir.dt.bfloat16
U32 = mybir.dt.uint32
ALU = mybir.AluOpType
ACT = mybir.ActivationFunctionType
AX = mybir.AxisListType

P = 128
NB, S, D = 16, 256, 256
TT = S // P
KD = D // P
L = 77
G, HD = 16, 16
UG = 8
NE0, NS0, H0 = 16, 16, 64
SLOTS = NE0 * NS0
FF = 1024
FC = FF // P
NE1, H1 = 8, 192
SH = 384
HC = (NE1 * H1 + SH) // P
EC = NE1 * H1 // P
TB = 512
NBLK = NB * S // TB
BT = TB // P
LN_EPS = 1e-5
L2_EPS = 1e-12


class Signal:

    def __init__(self, sem, per=1, step=1):
        self.sem, self.per, self.step = sem, per, step


def need(eng, sig, b, count=None):
    count = sig.per if count is None else count
    eng.wait_ge(sig.sem, (b * sig.per + count) * sig.step)


def alone(eng):
    eng.nop(nofuse=True)


def reuse(eng, sig, b, count=None):
    if isinstance(b, int) and b == 0:
        return
    count = sig.per if count is None else count
    eng.wait_ge(sig.sem, (b * sig.per + (count - sig.per)) * sig.step)


def at(tensor, b):
    if isinstance(b, int):
        return tensor[:, b]
    part = tensor[:, bass.ds(b, 1)]
    names = " ".join("wxyz"[: len(part.shape) - 2])
    first = names.split()[0]
    return part.rearrange(f"p a {names} -> p (a {first}) {names[2:]}")


def turns(eng, schedule, n):
    schedule(0, None)
    schedule(1, 0)
    with eng.Fori(1, n - 1) as i:
        schedule(i + 1, i)
    schedule(None, n - 1)


class Kernel:
    def __init__(self, nc, ins, out, stop=None):
        self.nc, self.ins, self.out, self.stop = nc, ins, out, stop
        self.used = []

    def sb(self, ctx, name, shape, dt=F32):
        return ctx.enter_context(self.nc.sbuf_tensor(name, shape, dt))

    def ps(self, ctx, name, shape, dt=F32):
        return ctx.enter_context(self.nc.psum_tensor(name, shape, dt))

    def sig(self, ctx, name, per=1, step=1):
        sem = ctx.enter_context(self.nc.semaphore(name))
        self.used.append(sem.num)
        return Signal(sem, per, step)

    def clear_signals(self):
        used, self.used = sorted(set(self.used)), []
        starts = [n for n in used if n - 1 not in used]
        ends = [n + 1 for n in used if n + 1 not in used]
        with self.nc.Block() as block:
            @block.gpsimd
            def _(pool):
                for a, b in zip(starts, ends):
                    pool.sem_clear(range(a, b))

    def build(self):
        nc = self.nc
        self.routes = nc.dram_tensor("routes", [NE1 * BT, P], F32, kind="Internal").ap()
        with ExitStack() as whole:
            self.X = self.sb(whole, "x_all", [P, NB, TT, D])
            self.ident = self.sb(whole, "ident", [P, P])
            self.gates = self.sb(whole, "gates", [P, 4])
            self.minus_half = self.sb(whole, "minus_half", [P, 4])
            with ExitStack() as moe:
                self.CT = self.sb(moe, "combineT_all", [P, NB, TT, S])
                self.SL = self.sb(moe, "slots_all", [P, KD, NB, SLOTS])
                self.rcomb = self.sb(moe, "combine_scale_all", [P, NB, TT])
                with ExitStack() as c:
                    self.phase_a(c)
                if self.stop == "a":
                    return self.dump(self.X)
                self.clear_signals()
                with ExitStack() as c:
                    self.phase_b(c)
                if self.stop == "b":
                    return self.dump(self.X)
                with ExitStack() as c:
                    self.phase_c(c)
                if self.stop == "c":
                    return self.dump(self.X)
            self.clear_signals()
            with ExitStack() as c:
                self.phase_d(c)

    def dump(self, X):
        with ExitStack() as c:
            done = self.sig(c, "dumped", 1, 16)
            block = c.enter_context(self.nc.Block())

            @block.sync
            def _(sp):
                sp.dma_start(self.out.rearrange("b (t p) d -> p b t d", p=P), X[:]).then_inc(done.sem, 16)
                sp.wait_ge(done.sem, 16)

    def phase_a(self, c):
        nc, ins = self.nc, self.ins
        X, CT, SL, ident = self.X, self.CT, self.SL, self.ident
        sb = lambda n, s, d=F32: self.sb(c, n, s, d)
        sig = lambda n, per=1, step=1: self.sig(c, n, per, step)

        wq = sb("wq", [P, KD, D])
        wk = sb("wk", [P, KD, P])
        wv = sb("wv", [P, KD, P])
        bq = sb("bq", [P, KD])
        bk = sb("bk", [P, 1])
        bvt = sb("bv_gated", [P, G, HD])
        scale0 = sb("scale0", [P, 1])
        gam0 = sb("gamma0", [P, D])
        bet0 = sb("beta0", [P, D])
        ones = sb("ones", [P, P])
        gmask = sb("group_mask", [P, UG])
        mu = sb("mu", [P, KD, SLOTS])
        mu_sq = sb("mu_sq", [P, KD, SLOTS])
        mu_ss = sb("mu_ss", [P, KD])
        mu_rn = sb("mu_rn", [P, KD])
        mu_diag = sb("mu_diag", [P, KD, P])
        mu_unit = sb("mu_unit", [P, KD, SLOTS])
        ctxT = sb("ctx_turned", [P, KD, P])
        kblock = sb("kblock", [P, UG, L])
        vpart = sb("vpart", [L, 3, HD + 1], BF16)
        vres = sb("vres", [L, 2, HD])
        z = sb("z", [P, TT, D])
        zT = sb("zT", [P, KD, S])
        qT = sb("qT", [P, KD, S])
        mx = sb("mx", [P, UG])
        prob = sb("prob", [P, 2, UG, L])
        prob2 = sb("prob_lo_hi", [P, 2, UG, L, 2], F16)
        probT = sb("probT", [L, G, G, G], U32)
        osum = sb("osum", [P, TT, G, HD + 1])
        orec = sb("orec", [P, TT, G])
        ogate = sb("ogate", [P, TT, G])
        oprod = sb("oprod", [P, TT, G, HD])
        mv1 = sb("mv1", [P, TT, 2])
        bs1 = sb("bs1", [P, TT, 6])
        rs1 = sb("rs1", [P, TT])
        bs2 = sb("bs2", [P, TT, 6])
        mv2 = sb("mv2", [P, TT, 2])
        small = sb("ln2_small", [P, 8, TT])
        xg = sb("xg", [P, TT, D])
        xn = sb("xn", [P, TT, D])
        sq = sb("sq", [P, TT, D])
        ss = sb("ss", [P, TT])
        ru = sb("ru", [P, TT])
        xu = sb("xu", [P, TT, D])
        xuT = sb("xuT", [P, KD, S])
        negmax = sb("negmax", [P, 2, TT])
        esum = sb("esum", [P, 2, TT])
        erec = sb("erec", [P, 2, TT])
        comb = sb("comb", [P, TT, SLOTS])
        dispT = sb("dispT", [P, TT, S])
        disp = sb("disp", [P, TT, SLOTS])

        psA = self.ps(c, "ps_small_a", [P, 512])
        psB = self.ps(c, "ps_small_b", [P, 512])
        psS = self.ps(c, "ps_scores", [P, 2, 512])
        psT = self.ps(c, "ps_probT", [P, 4, P])
        psR = self.ps(c, "ps_turned", [P, 512])
        psL = self.ps(c, "ps_logits", [P, 2, 256])
        psM = self.ps(c, "ps_logitsT", [P, 2, 256])

        const_in = sig("const_in", 1, 16)
        x_in, ctx_in = sig("x_in", 1, 16), sig("ctx_in", 1, 16)
        filled, id_done, gate_done, bv_done = sig("filled"), sig("id_done"), sig("gate_done"), sig("bv_done")
        mu_sq_done, mu_ss_mm, mu_ss_ev, mu_rn_done = sig("mu_sq_done"), sig("mu_ss_mm"), sig("mu_ss_ev"), sig("mu_rn_done")
        mu_diag_done, mu_bc_mm, mu_done = sig("mu_diag_done"), sig("mu_bc_mm"), sig("mu_done")
        kv_mm, kb_done, v_step = sig("kv_mm"), sig("kb_done"), sig("v_step", 5)
        st1, mv1_done, rs1_step, z_done = sig("st1"), sig("mv1_done"), sig("rs1_step", 2), sig("z_done")
        zt_mm, zt_ev, q_mm, q_ev = sig("zt_mm"), sig("zt_ev"), sig("q_mm"), sig("q_ev")
        sc_mm, mx_done, sub_done, exp_done = sig("sc_mm", 4), sig("mx_done", 4), sig("sub_done", 4), sig("exp_done", 4)
        hi_done, lo_done, pt_mm, pt_ev = sig("hi_done", 4), sig("lo_done", 4), sig("pt_mm", 8), sig("pt_ev", 8)
        pv_mm, osum_done = sig("pv_mm", 4), sig("osum_done", 4)
        xb_done, o_step, x1_done = sig("xb_done"), sig("o_step", 3), sig("x1_done")
        st2, mv2_done, rs2_step, xg_done, xn_done = sig("st2"), sig("mv2_done"), sig("rs2_step", 8), sig("xg_done"), sig("xn_done")
        ss_done, ru_step, xu_done = sig("ss_done"), sig("ru_step", 3), sig("xu_done")
        xut_mm, xut_ev, lg_mm, lt_mm = sig("xut_mm"), sig("xut_ev"), sig("lg_mm"), sig("lt_mm")
        nm_done, ce_done, de_done = sig("nm_done", 2), sig("ce_done"), sig("de_done")
        rec_done, dn_done = sig("rec_done", 2), sig("dn_done")
        ct_mm, ct_ev, dt_mm, dt_ev, sl_mm, sl_ev = sig("ct_mm"), sig("ct_ev"), sig("dt_mm"), sig("dt_ev"), sig("sl_mm"), sig("sl_ev")

        row = lambda ap, n: spread(ap.rearrange("(a d) -> a d", a=1), 0, n)
        const_loads = [
            (wq[:], ins["L0_xattn_Wq"].rearrange("(k p) f -> p k f", p=P)),
            (wk[:], ins["wk8"].rearrange("(k p) f -> p k f", p=P)),
            (wv[:, :, 0:HD], ins["L0_xattn_Wv"].rearrange("(k p) f -> p k f", p=P)),
            (bq[:], ins["bq_cols"]),
            (bk[:], ins["bk8"].rearrange("(p a) -> p a", a=1)),
            (bvt[:], spread(spread(ins["L0_xattn_bv"].rearrange("(a b d) -> a b d", a=1, b=1), 0, P), 1, G)),
            (scale0[:], row(ins["L0_ffn_scale"], P)),
            (gam0[:], row(ins["L0_ffn_ln_gamma"], P)),
            (bet0[:], row(ins["L0_ffn_ln_beta"], P)),
            (self.gates[:, 0:2], row(ins["g_xattn"], P)),
            (self.gates[:, 2:4], row(ins["g_ffn"], P)),
            (mu[:], ins["L0_ffn_mu"].rearrange("(k p) e s -> p k (e s)", p=P)),
        ]
        block = c.enter_context(nc.Block())

        @block.sync
        def _(sp):
            def load_x(b):
                sp.dma_start(at(X, b), ins["x"].rearrange("b (t p) d -> p b t d", p=P)[:, b] if isinstance(b, int)
                             else at(ins["x"].rearrange("b (t p) d -> p b t d", p=P), b)).then_inc(x_in.sem, 16)

            def load_ctx(b):
                reuse(sp, kv_mm, b)
                src = ins["ctxT"].rearrange("b (k p) l -> p b k l", p=P)
                sp.dma_start(ctxT[:, :, 0:L], at(src, b)).then_inc(ctx_in.sem, 16)

            load_x(0)
            sp.wait_ge(filled.sem, 1)
            load_ctx(0)
            for dst, src in const_loads:
                sp.dma_start(dst, src).then_inc(const_in.sem, 16)
            with sp.Fori(1, NB) as b:
                sp.wait_ge(x_in.sem, b * 16)
                load_x(b)
                load_ctx(b)

        all_const = 16 * len(const_loads)

        @block.gpsimd
        def _(pool):
            pool.memset(ident[:], 0.0)
            pool.memset(gmask[:], 1.0)
            pool.memset(ones[:], 1.0)
            pool.memset(self.minus_half[:], -0.5)
            pool.memset(wv[:, :, HD:P], 0.0)
            pool.memset(vpart[:, 0, HD:HD + 1], 1.0)
            pool.memset(vpart[:, 1:3, HD:HD + 1], 0.0)
            pool.memset(ctxT[:], 0.0).then_inc(filled.sem, 1)
            pool.wait_ge(filled.sem, 1)
            pool.affine_select(out=ident[:], in_=ident[:], compare_op=ALU.not_equal, fill=1.0, base=0,
                               pattern=[[-1, P]], channel_multiplier=1).then_inc(id_done.sem, 1)
            pool.affine_select(out=gmask[:], in_=gmask[:], compare_op=ALU.is_ge, fill=0.0, base=0,
                               pattern=[[-HD, UG]], channel_multiplier=1).then_inc(id_done.sem, 1)
            pool.wait_ge(id_done.sem, 2)
            pool.affine_select(out=gmask[:], in_=gmask[:], compare_op=ALU.is_ge, fill=0.0, base=HD - 1,
                               pattern=[[HD, UG]], channel_multiplier=-1).then_inc(id_done.sem, 1)
            pool.wait_ge(mu_ss_ev.sem, 1)
            pool.tensor_tensor(mu_rn[:], mu_ss[:], self.minus_half[:, 0:KD], ALU.pow).then_inc(mu_rn_done.sem, 1)
            pool.wait_ge(gate_done.sem, 1)
            alone(pool)
            pool.tensor_scalar(bvt[:], bvt[:], self.gates[:, 0:1], None, ALU.mult).then_inc(bv_done.sem, 1)
            pool.wait_ge(bv_done.sem, 1)

            def rstd1(b):
                need(pool, mv1_done, b)
                alone(pool)
                pool.tensor_scalar(rs1[:], mv1[:, :, 1], LN_EPS, None, ALU.add).then_inc(rs1_step.sem, 1)
                need(pool, rs1_step, b, 1)
                pool.tensor_tensor(rs1[:], rs1[:], self.minus_half[:, 0:TT], ALU.pow).then_inc(rs1_step.sem, 1)

            def add_bv(b):
                need(pool, z_done, b)
                pool.tensor_tensor(at(X, b), at(X, b), spread(bvt[:].rearrange("p (a g) d -> p a (g d)", a=1), 1, TT),
                                   ALU.add).then_inc(xb_done.sem, 1)

            def split(b, u):
                need(pool, exp_done, b, u + 1)
                if u < 2:
                    reuse(pool, pt_mm, b, 4 + 2 * (u + 1))
                else:
                    need(pool, pt_mm, b, 2 * (u - 1))
                alone(pool)
                pool.tensor_copy(prob2[:, u % 2, :, :, 1], prob[:, u % 2]).then_inc(hi_done.sem, 1)
                need(pool, hi_done, b, u + 1)
                pool.tensor_tensor(prob2[:, u % 2, :, :, 0], prob[:, u % 2], prob2[:, u % 2, :, :, 1],
                                   ALU.subtract).then_inc(lo_done.sem, 1)

            def rstd2(b):
                need(pool, mv2_done, b)
                steps = [
                    lambda: pool.tensor_scalar(small[:, 0, :], mv2[:, :, 1], LN_EPS, None, ALU.add),
                    lambda: pool.tensor_tensor(small[:, 1, :], small[:, 0, :], self.minus_half[:, 0:TT], ALU.pow),
                    lambda: pool.tensor_tensor(small[:, 2, :], small[:, 1, :], small[:, 1, :], ALU.mult),
                    lambda: pool.tensor_tensor(small[:, 3, :], small[:, 2, :], mv2[:, :, 1], ALU.mult),
                    lambda: pool.tensor_scalar(small[:, 4, :], small[:, 3, :], LN_EPS, None, ALU.add),
                    lambda: pool.tensor_tensor(small[:, 5, :], small[:, 4, :], self.minus_half[:, 0:TT], ALU.pow),
                    lambda: pool.tensor_tensor(small[:, 6, :], small[:, 5, :], small[:, 1, :], ALU.mult),
                    lambda: pool.tensor_copy(small[:, 7, :], small[:, 6, :]),
                ]
                for n, step in enumerate(steps):
                    if n:
                        need(pool, rs2_step, b, n)
                    alone(pool)
                    step().then_inc(rs2_step.sem, 1)

            def runit(b):
                need(pool, ss_done, b)
                reuse(pool, xu_done, b)
                alone(pool)
                pool.tensor_scalar(ru[:], ss[:], L2_EPS * L2_EPS, None, ALU.max).then_inc(ru_step.sem, 1)
                need(pool, ru_step, b, 1)
                pool.tensor_tensor(ru[:], ru[:], self.minus_half[:, 0:TT], ALU.pow).then_inc(ru_step.sem, 1)
                need(pool, ru_step, b, 2)
                alone(pool)
                pool.tensor_scalar(ru[:], ru[:], scale0[:, 0:1], None, ALU.mult).then_inc(ru_step.sem, 1)

            def schedule(f, k):
                if f is not None:
                    rstd1(f)
                    add_bv(f)
                if k is not None:
                    rstd2(k)
                for u in range(4):
                    if f is not None:
                        split(f, u)
                    if k is not None and u == 0:
                        runit(k)

            turns(pool, schedule, NB)

        @block.scalar
        def _(act):
            act.wait_ge(const_in.sem, all_const)
            act.activation(self.gates[:], self.gates[:], ACT.Tanh).then_inc(gate_done.sem, 1)

            def zT_out(b):
                need(act, zt_mm, b)
                reuse(act, q_mm, b)
                act.copy(zT[:].rearrange("p k s -> p (k s)"), psA[:]).then_inc(zt_ev.sem, 1)

            def q_out(b):
                need(act, q_mm, b)
                reuse(act, sc_mm, b)
                for k in range(KD):
                    ins_ = act.activation(qT[:, k, :], psB[:, k * S:(k + 1) * S], ACT.Identity, bias=bq[:, k:k + 1])
                ins_.then_inc(q_ev.sem, 1)

            def exps(b, u):
                need(act, sub_done, b, u + 1)
                act.activation(prob[:, u % 2], prob[:, u % 2], ACT.Exp, scale=float(D) ** -0.5).then_inc(exp_done.sem, 1)

            def squares(b):
                need(act, xn_done, b)
                reuse(act, ss_done, b)
                reuse(act, ru_step, b, 1)
                for t in range(TT):
                    ins_ = act.activation(sq[:, t, :], xn[:, t, :], ACT.Square, accum_out=ss[:, t:t + 1])
                ins_.then_inc(ss_done.sem, 1)

            def xuT_out(b):
                need(act, xut_mm, b)
                reuse(act, lt_mm, b)
                act.copy(xuT[:].rearrange("p k s -> p (k s)"), psR[:]).then_inc(xut_ev.sem, 1)

            def combine(b):
                need(act, nm_done, b, 1)
                reuse(act, ct_mm, b)
                reuse(act, rec_done, b, 1)
                for t in range(TT):
                    ins_ = act.activation(comb[:, t, :], psL[:, t, :], ACT.Exp, bias=negmax[:, 0, t:t + 1],
                                          accum_out=esum[:, 0, t:t + 1])
                ins_.then_inc(ce_done.sem, 1)

            def dispatch(b):
                need(act, nm_done, b, 2)
                reuse(act, dt_mm, b)
                reuse(act, rec_done, b, 2)
                for t in range(TT):
                    ins_ = act.activation(dispT[:, t, :], psM[:, t, :], ACT.Exp, bias=negmax[:, 1, t:t + 1],
                                          accum_out=esum[:, 1, t:t + 1])
                ins_.then_inc(de_done.sem, 1)

            def combineT_out(b):
                need(act, ct_mm, b)
                act.copy(at(CT, b), psR[:].rearrange("p (k s) -> p k s", k=TT)).then_inc(ct_ev.sem, 1)

            def disp_out(b):
                need(act, dt_mm, b)
                reuse(act, sl_mm, b)
                act.copy(disp[:].rearrange("p k s -> p (k s)"), psR[:]).then_inc(dt_ev.sem, 1)

            def slots_out(b):
                need(act, sl_mm, b)
                for k in range(KD):
                    dst = SL[:, k, b, :] if isinstance(b, int) else SL[:, k, bass.ds(b, 1), :].rearrange("p a s -> p (a s)")
                    ins_ = act.copy(dst, psL[:, k, :])
                ins_.then_inc(sl_ev.sem, 1)

            def schedule(f, k):
                if f is not None:
                    zT_out(f)
                    q_out(f)
                    exps(f, 0)
                if k is not None:
                    squares(k)
                    xuT_out(k)
                if f is not None:
                    exps(f, 1)
                if k is not None:
                    combine(k)
                if f is not None:
                    exps(f, 2)
                if k is not None:
                    dispatch(k)
                    combineT_out(k)
                if f is not None:
                    exps(f, 3)
                if k is not None:
                    disp_out(k)
                    slots_out(k)

            turns(act, schedule, NB)

        @block.vector
        def _(dve):
            dve.wait_ge(const_in.sem, all_const)
            dve.tensor_tensor(mu_sq[:], mu[:], mu[:], ALU.mult).then_inc(mu_sq_done.sem, 1)
            dve.wait_ge(mu_ss_mm.sem, 1)
            dve.tensor_scalar(mu_ss[:], psA[:].rearrange("p (k s) -> p k s", k=KD)[:, :, 0], L2_EPS * L2_EPS, None, ALU.max)\
               .then_inc(mu_ss_ev.sem, 1)
            dve.wait_ge(mu_rn_done.sem, 1)
            dve.wait_ge(id_done.sem, 3)
            for k in range(KD):
                last = dve.tensor_scalar(mu_diag[:, k, :], ident[:], mu_rn[:, k:k + 1], None, ALU.mult)
            last.then_inc(mu_diag_done.sem, 1)
            dve.wait_ge(mu_bc_mm.sem, 1)
            dve.tensor_tensor(mu_unit[:], mu[:], spread(psB[:, 0:SLOTS].rearrange("p (a s) -> p a s", a=1), 1, KD), ALU.mult)\
               .then_inc(mu_done.sem, 1)

            def kv_out(b):
                need(dve, kv_mm, b)
                reuse(dve, sc_mm, b)
                dve.scalar_tensor_tensor(out=kblock[:], in0=spread(psA[:, 0:L].rearrange("p (a l) -> p a l", a=1), 1, UG),
                                         scalar=bk[:, 0:1], in1=spread(gmask[:].rearrange("p (g a) -> p g a", a=1), 2, L),
                                         op0=ALU.add, op1=ALU.mult).then_inc(kb_done.sem, 1)
                reuse(dve, pv_mm, b)
                v = psA[0:L, P:P + HD]
                dve.tensor_copy(vpart[:, 0, 0:HD], v).then_inc(v_step.sem, 1)
                need(dve, v_step, b, 1)
                dve.tensor_tensor(vres[:, 0, :], v, vpart[:, 0, 0:HD], ALU.subtract).then_inc(v_step.sem, 1)
                need(dve, v_step, b, 2)
                dve.tensor_copy(vpart[:, 1, 0:HD], vres[:, 0, :]).then_inc(v_step.sem, 1)
                need(dve, v_step, b, 3)
                dve.tensor_tensor(vres[:, 1, :], vres[:, 0, :], vpart[:, 1, 0:HD], ALU.subtract).then_inc(v_step.sem, 1)
                need(dve, v_step, b, 4)
                dve.tensor_copy(vpart[:, 2, 0:HD], vres[:, 1, :]).then_inc(v_step.sem, 1)

            def stats(b, src, bs, mv, st, done, readers):
                reuse(dve, readers, b)
                alone(dve)
                for t in range(TT):
                    last = dve.bn_stats(bs[:, t, :], src[:, t, :])
                last.then_inc(st.sem, 1)
                need(dve, st, b)
                alone(dve)
                for t in range(TT):
                    last = dve.bn_aggr(mv[:, t, :], bs[:, t, :])
                last.then_inc(done.sem, 1)

            def ln1_stats(b):
                need(dve, x_in, b)
                stats(b, at(X, b), bs1, mv1, st1, mv1_done, z_done)

            def ln1_apply(b):
                need(dve, rs1_step, b)
                reuse(dve, zt_mm, b)
                x = at(X, b)
                for t in range(TT):
                    last = dve.tensor_scalar(z[:, t, :], x[:, t, :], mv1[:, t, 0:1], rs1[:, t:t + 1], ALU.subtract, ALU.mult)
                last.then_inc(z_done.sem, 1)

            def scores_out(b, u):
                need(dve, sc_mm, b, u + 1)
                s = psS[:, :, 0:UG // 2 * L].rearrange("p c (g l) -> p c g l", l=L)
                m = mx[:].rearrange("p (c g) -> p c g", c=2)
                dve.tensor_reduce(m, s, AX.X, ALU.max).then_inc(mx_done.sem, 1)
                need(dve, mx_done, b, u + 1)
                if u < 2:
                    reuse(dve, lo_done, b, 3 + u)
                else:
                    need(dve, lo_done, b, u - 1)
                dve.tensor_tensor(prob[:, u % 2].rearrange("p (c g) l -> p c g l", c=2), s,
                                  spread(mx[:].rearrange("p (c g a) -> p c g a", c=2, a=1), 3, L),
                                  ALU.subtract).then_inc(sub_done.sem, 1)

            def probT_out(b, u):
                for n in (2 * u, 2 * u + 1):
                    need(dve, pt_mm, b, n + 1)
                    if n == 0:
                        reuse(dve, pv_mm, b)
                    tile, g0 = n // 4, (n % 4) * 4
                    dst = probT[:, tile * UG:(tile + 1) * UG, :, g0:g0 + 4].rearrange("k h t g -> k (h t) g")
                    src = psT[0:L].bitcast(U32).rearrange("k g q -> k q g")
                    dve.tensor_copy(dst, src).then_inc(pt_ev.sem, 1)

            def out_sum(b, w):
                need(dve, pv_mm, b, w + 1)
                bank = (psA, psB)[w % 2]
                dve.tensor_reduce(osum[:, w // 2, (w % 2) * 8:(w % 2) * 8 + 8, :],
                                  bank[:, 0:8 * 3 * (HD + 1)].rearrange("p (h c d) -> p h d c", h=8, c=3),
                                  AX.X, ALU.add).then_inc(osum_done.sem, 1)

            def x1(b):
                need(dve, osum_done, b)
                dve.reciprocal(orec[:], osum[:, :, :, HD]).then_inc(o_step.sem, 1)
                need(dve, o_step, b, 1)
                dve.tensor_scalar(ogate[:], orec[:], self.gates[:, 0:1], None, ALU.mult).then_inc(o_step.sem, 1)
                need(dve, o_step, b, 2)
                dve.tensor_tensor(oprod[:], osum[:, :, :, 0:HD],
                                  spread(ogate[:].rearrange("p t (g a) -> p t g a", a=1), 3, HD), ALU.mult).then_inc(o_step.sem, 1)
                need(dve, o_step, b, 3)
                need(dve, xb_done, b)
                dve.tensor_tensor(at(X, b), at(X, b), oprod[:].rearrange("p t g d -> p t (g d)"), ALU.add).then_inc(x1_done.sem, 1)

            def ln2_stats(b):
                need(dve, x1_done, b)
                stats(b, at(X, b), bs2, mv2, st2, mv2_done, xn_done)

            def ln2_apply(b):
                x = at(X, b)
                need(dve, mv2_done, b)
                for t in range(TT):
                    last = dve.scalar_tensor_tensor(out=xg[:, t, :], in0=x[:, t, :], scalar=mv2[:, t, 0:1], in1=gam0[:],
                                                    op0=ALU.subtract, op1=ALU.mult)
                last.then_inc(xg_done.sem, 1)
                need(dve, rs2_step, b)
                need(dve, xg_done, b)
                reuse(dve, sl_mm, b)
                reuse(dve, ss_done, b)
                for t in range(TT):
                    last = dve.scalar_tensor_tensor(out=xn[:, t, :], in0=xg[:, t, :], scalar=small[:, 7, t:t + 1], in1=bet0[:],
                                                    op0=ALU.mult, op1=ALU.add)
                last.then_inc(xn_done.sem, 1)

            def unit(b):
                need(dve, ru_step, b)
                reuse(dve, xut_mm, b)
                for t in range(TT):
                    last = dve.tensor_scalar(xu[:, t, :], xn[:, t, :], ru[:, t:t + 1], None, ALU.mult)
                last.then_inc(xu_done.sem, 1)

            def neg_max(b):
                need(dve, lg_mm, b)
                reuse(dve, ce_done, b)
                dve.tensor_reduce(negmax[:, 0, :], psL[:], AX.X, ALU.max, negate=True).then_inc(nm_done.sem, 1)
                need(dve, lt_mm, b)
                reuse(dve, de_done, b)
                dve.tensor_reduce(negmax[:, 1, :], psM[:], AX.X, ALU.max, negate=True).then_inc(nm_done.sem, 1)

            def normalise(b):
                need(dve, ce_done, b)
                dve.reciprocal(erec[:, 0, :], esum[:, 0, :]).then_inc(rec_done.sem, 1)
                need(dve, de_done, b)
                dve.reciprocal(erec[:, 1, :], esum[:, 1, :]).then_inc(rec_done.sem, 1)
                need(dve, rec_done, b)
                dve.tensor_scalar(at2(self.rcomb, b), erec[:, 0, :], self.gates[:, 2:3], None, ALU.mult)
                for t in range(TT):
                    last = dve.tensor_scalar(dispT[:, t, :], dispT[:, t, :], erec[:, 1, t:t + 1], None, ALU.mult)
                last.then_inc(dn_done.sem, 1)

            def schedule(f, k):
                if f is not None:
                    kv_out(f)
                    ln1_stats(f)
                    ln1_apply(f)
                if k is not None:
                    ln2_stats(k)
                    ln2_apply(k)
                if f is not None:
                    scores_out(f, 0)
                if k is not None:
                    unit(k)
                if f is not None:
                    scores_out(f, 1)
                    probT_out(f, 0)
                if k is not None:
                    neg_max(k)
                if f is not None:
                    scores_out(f, 2)
                    probT_out(f, 1)
                if k is not None:
                    normalise(k)
                if f is not None:
                    scores_out(f, 3)
                    probT_out(f, 2)
                    probT_out(f, 3)
                    for w in range(4):
                        out_sum(f, w)
                    x1(f)

            turns(dve, schedule, NB)

        @block.tensor
        def _(pe):
            def mm(out, lhsT, rhs, start=True, stop=True):
                return pe.matmul(out, lhsT, rhs, start=start, stop=stop)

            pe.wait_ge(mu_sq_done.sem, 1)
            for h in range(KD):
                for k in range(KD):
                    last = mm(psA[:, h * 256:h * 256 + P], mu_sq[:, k, h * P:(h + 1) * P], ones[:], k == 0, k == KD - 1)
            last.then_inc(mu_ss_mm.sem, 1)
            pe.wait_ge(mu_diag_done.sem, 1)
            for h in range(KD):
                last = mm(psB[:, h * P:(h + 1) * P], ones[:], mu_diag[:, h, :])
            last.then_inc(mu_bc_mm.sem, 1)
            pe.wait_ge(mu_done.sem, 1)

            def turn4(dst, src):
                for k in range(2):
                    for t in range(2):
                        last = pe.transpose(dst[:, k * S + t * P:k * S + (t + 1) * P], src[:, t, k * P:(k + 1) * P], ident[:])
                return last

            def kv(b):
                need(pe, ctx_in, b)
                reuse(pe, osum_done, b, 3)
                for k in range(KD):
                    mm(psA[:, 0:P], wk[:, k, :], ctxT[:, k, :], k == 0, k == KD - 1)
                for k in range(KD):
                    last = mm(psA[:, P:2 * P], ctxT[:, k, :], wv[:, k, :], k == 0, k == KD - 1)
                last.then_inc(kv_mm.sem, 1)

            def turn_z(b):
                need(pe, z_done, b)
                need(pe, kb_done, b)
                need(pe, v_step, b, 2)
                turn4(psA, z).then_inc(zt_mm.sem, 1)

            def queries(b):
                need(pe, zt_ev, b)
                reuse(pe, osum_done, b, 4)
                for m in range(KD):
                    for k in range(KD):
                        last = mm(psB[:, m * S:(m + 1) * S], wq[:, k, m * P:(m + 1) * P], zT[:, k, :], k == 0, k == KD - 1)
                last.then_inc(q_mm.sem, 1)

            def scores(b, u):
                tile, chunk = u // 2, u % 2
                if u == 0:
                    need(pe, q_ev, b)
                    reuse(pe, sub_done, b)
                else:
                    need(pe, sub_done, b, u)
                for h in range(2):
                    last = mm(psS[:, h, 0:UG // 2 * L], qT[:, chunk, tile * P:(tile + 1) * P],
                              kblock[:, h * UG // 2:(h + 1) * UG // 2, :].rearrange("p g l -> p (g l)"))
                last.then_inc(sc_mm.sem, 1)

            def turn_p(b, u):
                need(pe, lo_done, b, u + 1)
                pairs = prob2[:, u % 2].rearrange("p g l two -> p g (l two)").bitcast(F32)
                for n in (2 * u, 2 * u + 1):
                    if n == 0:
                        reuse(pe, pt_ev, b)
                    else:
                        need(pe, pt_ev, b, n)
                    for j in range(4):
                        last = pe.transpose(psT[0:L, j, :], pairs[:, (n % 2) * 4 + j, :], ident[:])
                    last.then_inc(pt_mm.sem, 1)

            def values(b, w):
                tile, half = w // 2, w % 2
                bank = (psA, psB)[half]
                if w == 0:
                    need(pe, pt_ev, b)
                    need(pe, v_step, b)
                if w >= 2:
                    need(pe, osum_done, b, w - 1)
                both = probT[:].rearrange("k h t g -> k h (t g)").bitcast(F16)\
                               .rearrange("k h (q two) -> k h q two", two=2)
                W = 3 * (HD + 1)
                rhs = vpart[:].rearrange("k c d -> k (c d)")
                for h in range(8):
                    for part in (1, 0):
                        last = mm(bank[:, h * W:(h + 1) * W], both[:, half * 8 + h, tile * P:(tile + 1) * P, part], rhs,
                                  part == 1, part == 0)
                last.then_inc(pv_mm.sem, 1)

            def turn_xu(b):
                need(pe, xu_done, b)
                reuse(pe, dt_ev, b)
                turn4(psR, xu).then_inc(xut_mm.sem, 1)

            def logits(b):
                need(pe, xut_ev, b)
                reuse(pe, sl_ev, b)
                for t in range(TT):
                    for k in range(KD):
                        last = mm(psL[:, t, :], xuT[:, k, t * P:(t + 1) * P], mu_unit[:, k, :], k == 0, k == KD - 1)
                last.then_inc(lg_mm.sem, 1)
                reuse(pe, de_done, b)
                for h in range(2):
                    for k in range(KD):
                        last = mm(psM[:, h, :], mu_unit[:, k, h * P:(h + 1) * P], xuT[:, k, :], k == 0, k == KD - 1)
                last.then_inc(lt_mm.sem, 1)

            def turn_comb(b):
                need(pe, ce_done, b)
                turn4(psR, comb).then_inc(ct_mm.sem, 1)

            def turn_disp(b):
                need(pe, dn_done, b)
                need(pe, ct_ev, b)
                turn4(psR, dispT).then_inc(dt_mm.sem, 1)

            def slot_inputs(b):
                need(pe, dt_ev, b)
                need(pe, ce_done, b)
                for k in range(KD):
                    for t in range(TT):
                        last = mm(psL[:, k, :], xn[:, t, k * P:(k + 1) * P], disp[:, t, :], t == 0, t == TT - 1)
                last.then_inc(sl_mm.sem, 1)

            def schedule(f, k):
                if f is not None:
                    kv(f)
                    turn_z(f)
                    queries(f)
                    scores(f, 0)
                if k is not None:
                    turn_xu(k)
                if f is not None:
                    scores(f, 1)
                    turn_p(f, 0)
                if k is not None:
                    logits(k)
                if f is not None:
                    scores(f, 2)
                    turn_p(f, 1)
                if k is not None:
                    turn_comb(k)
                if f is not None:
                    scores(f, 3)
                    turn_p(f, 2)
                if k is not None:
                    turn_disp(k)
                if f is not None:
                    turn_p(f, 3)
                if k is not None:
                    slot_inputs(k)
                if f is not None:
                    for w in range(4):
                        values(f, w)

            turns(pe, schedule, NB)

    def phase_b(self, c):
        nc, ins, SL = self.nc, self.ins, self.SL
        sb = lambda n, s, d=F32: self.sb(c, n, s, d)
        sig = lambda n, per=1, step=1: self.sig(c, n, per, step)
        Q = NE0 // 2
        w1 = sb("e_w1", [P, KD, Q, P])
        w2 = sb("e_w2", [P, Q, D])
        b1 = sb("e_b1", [P, Q])
        b2 = sb("e_b2", [P, KD, NE0])
        hT = [sb(f"e_hT{j}", [P, NB * NS0]) for j in range(2)]
        psH = [self.ps(c, f"ps_hidden{j}", [P, 512]) for j in range(2)]
        psO = [self.ps(c, f"ps_slot_out{j}", [P, KD, NB, NS0]) for j in range(2)]
        w_in, zero_done = sig("e_w_in", 1, 16), sig("e_zero_done")
        h_mm, h_ev, o_mm, o_ev = sig("e_h_mm"), sig("e_h_ev"), sig("e_o_mm"), sig("e_o_ev")
        loads = [(w1[:], ins["w1_pairs"].rearrange("(k p) (q h) -> p k q h", p=P, q=Q)),
                 (w2[:], ins["L0_ffn_w2"].rearrange("(q j) h d -> (j h) q d", j=2)),
                 (b1[:], ins["b1_cols"]), (b2[:], ins["b2_cols"])]
        block = c.enter_context(nc.Block())

        @block.sync
        def _(sp):
            for dst, src in loads:
                sp.dma_start(dst, src).then_inc(w_in.sem, 16)

        @block.scalar
        def _(act):
            act.wait_ge(w_in.sem, 16 * len(loads))
            for e in range(NE0):
                j, rows = e % 2, slice(e % 2 * H0, e % 2 * H0 + H0)
                if e < 2:
                    act.wait_ge(zero_done.sem, 1)
                else:
                    act.wait_ge(o_mm.sem, e - 1)
                act.wait_ge(h_mm.sem, e + 1)
                act.activation(hT[j][rows, :], psH[j][rows, 0:NB * NS0], ACT.Gelu, bias=b1[rows, e // 2:e // 2 + 1])\
                   .then_inc(h_ev.sem, 1)

        @block.vector
        def _(dve):
            dve.memset(hT[0][:], 0.0)
            dve.memset(hT[1][:], 0.0).then_inc(zero_done.sem, 1)
            dve.wait_ge(w_in.sem, 16 * len(loads))
            for e in range(NE0):
                dve.wait_ge(o_mm.sem, e + 1)
                for k in range(KD):
                    last = dve.tensor_scalar(SL[:, k, :, e * NS0:(e + 1) * NS0], psO[e % 2][:, k], b2[:, k, e:e + 1],
                                             None, ALU.add)
                last.then_inc(o_ev.sem, 1)

        @block.tensor
        def _(pe):
            pe.wait_ge(w_in.sem, 16 * len(loads))

            def hidden(e):
                if e >= 2:
                    pe.wait_ge(h_ev.sem, e - 1)
                for k in range(KD):
                    last = pe.matmul(psH[e % 2][:, 0:NB * NS0], w1[:, k, e // 2, :], SL[:, k, :, e * NS0:(e + 1) * NS0],
                                     start=(k == 0), stop=(k == KD - 1))
                last.then_inc(h_mm.sem, 1)

            def outputs(e):
                pe.wait_ge(h_ev.sem, e + 1)
                if e >= 2:
                    pe.wait_ge(o_ev.sem, e - 1)
                for k in range(KD):
                    last = pe.matmul(psO[e % 2][:, k].rearrange("p b s -> p (b s)"), w2[:, e // 2, k * P:(k + 1) * P],
                                     hT[e % 2][:], start=True, stop=True)
                last.then_inc(o_mm.sem, 1)

            hidden(0)
            for e in range(1, NE0):
                hidden(e)
                outputs(e - 1)
            outputs(NE0 - 1)

    def phase_c(self, c):
        nc, ins = self.nc, self.ins
        X, CT, SL, ident = self.X, self.CT, self.SL, self.ident
        sb = lambda n, s, d=F32: self.sb(c, n, s, d)
        sig = lambda n, per=1, step=1: self.sig(c, n, per, step)
        ISQ = float(D) ** -0.5
        YW = D + 2

        w1h, w1l = sb("f_w1_hi", [P, KD, FF], F32R), sb("f_w1_lo", [P, KD, FF], F32R)
        w2h, w2l = sb("f_w2_hi", [P, FC, D], F32R), sb("f_w2_lo", [P, FC, D], F32R)
        wst = sb("f_w_stage", [P, 2, FF])
        fb1 = sb("f_b1", [P, FC])
        rows = sb("f_rows", [P, 7, D])
        cmask = sb("causal", [P, P])
        bias16 = sb("minus_top_score", [P, 1])
        combT = sb("combT", [P, TT, S])
        slT = sb("slT", [P, KD, SLOTS])
        so = sb("so", [P, TT, D])
        ctxT = sb("c_ctxT", [P, KD, P])
        ctx = sb("c_ctx", [L, D])
        y = sb("y", [P, TT, YW])
        yT = sb("yT", [P, KD, S])
        E = sb("sa_exp", [P, 3, P])
        r1, y1 = sb("r1", [P, TT, D]), sb("y1", [P, TT, D])
        y1T = sb("y1T", [P, KD, S])
        pc = sb("ca_prob", [P, TT, L])
        pcT = sb("ca_probT", [L, TT * P])
        r2, y2, y2b = sb("r2", [P, TT, D]), sb("y2", [P, TT, D]), sb("y2b", [P, TT, D])
        y2h, y2l = sb("y2T_hi", [P, KD, S], F32R), sb("y2T_lo", [P, KD, S], F32R)
        hf = sb("f_hidden", [P, 2, 2, S])
        hh, hl = sb("f_hidden_hi", [P, 2, 2, S], F32R), sb("f_hidden_lo", [P, 2, 2, S], F32R)
        r3, y3 = sb("r3", [P, TT, D]), sb("y3", [P, TT, D])
        small = {n: sb(f"c_small_{n}", [P, TT]) for n in ("srec", "cmax", "cbias", "csum", "crec")}
        lns = {}
        for n in ("l3", "la", "lb", "lc"):
            lns[n] = dict(bs=sb(f"bs_{n}", [P, TT, 6]), mv=sb(f"mv_{n}", [P, TT, 2]), rs=sb(f"rs_{n}", [P, TT]),
                          xg=sb(f"xg_{n}", [P, TT, D]) if n != "l3" else None,
                          st=sig(f"st_{n}"), mvd=sig(f"mvd_{n}"), rss=sig(f"rss_{n}", 2), xgd=sig(f"xgd_{n}"),
                          done=sig(f"done_{n}"))

        psT = self.ps(c, "c_turned", [P, 512])
        psO = self.ps(c, "c_out", [P, 512])
        psS = self.ps(c, "c_scores", [P, 512])
        psO2 = self.ps(c, "c_out2", [P, 512])
        psY = self.ps(c, "c_turned_back", [P, 512])
        psH = self.ps(c, "c_hidden", [P, 2, 2, S])
        psF = self.ps(c, "c_mlp", [P, TT, D])

        const_in, rows_done = sig("f_const_in", 1, 16), sig("f_mask_done")
        bias_done = sig("top_score_done")
        wst_in, wh_done, wl_done = sig("wst_in", 1, 16), sig("wh_done"), sig("wl_done")
        load_in = sig("c_load_in", 2, 16)
        ctx_in = sig("c_ctx_in", 2, 16)
        so_mm, so_ev, mix_mm, x2_done = sig("so_mm"), sig("so_ev"), sig("mix_mm"), sig("x2_done")
        yt_mm, yt_ev, sa_mm, sa_exp, sa_mask = sig("yt_mm"), sig("yt_ev"), sig("sa_mm"), sig("sa_exp_done"), sig("sa_mask")
        sao_mm, srec_done, r1_done = sig("sao_mm"), sig("srec_done"), sig("r1_done")
        y1t_mm, y1t_ev, ca_mm, cm_done, ca_exp = sig("y1t_mm"), sig("y1t_ev"), sig("ca_mm"), sig("cm_done", 2), sig("ca_exp")
        pct_mm, pct_ev, cao_mm, crec_done, r2_done = sig("pct_mm"), sig("pct_ev"), sig("cao_mm"), sig("crec_done"), sig("r2_done")
        y2b_done, y2t_mm, y2h_ev, y2l_ev = sig("y2b_done"), sig("y2t_mm"), sig("y2h_ev"), sig("y2l_ev")
        h_mm, h_ev, hh_done, hl_done, f2_mm = sig("c_h_mm", 4), sig("c_h_ev", 4), sig("hh_done", 4), sig("hl_done", 4), sig("f2_mm", 4)
        r3_done, x3_done = sig("r3_done"), sig("x3_done")

        row = lambda ap: spread(ap.rearrange("(a d) -> a d", a=1), 0, P)
        names = ["L1_xattn_g1", "L1_xattn_beta1", "L1_xattn_g2", "L1_xattn_beta2", "L1_xattn_g3", "L1_xattn_beta3", "L1_xattn_b2"]
        const_loads = [(rows[:, n, :], row(ins[name])) for n, name in enumerate(names)] + [(fb1[:], ins["fb1_cols"])]
        w1v = ins["L1_xattn_w1"].rearrange("(k p) f -> p k f", p=P)
        w2v = ins["L1_xattn_w2"].rearrange("(c p) d -> p c d", p=P)
        stages = [(w1v[:, 0], w1h[:, 0], w1l[:, 0]), (w1v[:, 1], w1h[:, 1], w1l[:, 1]),
                  (w2v[:, 0:4], w2h[:, 0:4], w2l[:, 0:4]), (w2v[:, 4:8], w2h[:, 4:8], w2l[:, 4:8])]

        def stage(n, src):
            view = wst[:, n % 2]
            return view.rearrange("p (c d) -> p c d", d=D) if len(src.shape) == 3 else view

        block = c.enter_context(nc.Block())

        @block.sync
        def _(sp):
            def load(b):
                reuse(sp, mix_mm, b)
                sp.dma_start(combT[:], at(CT, b)).then_inc(load_in.sem, 16)
                if isinstance(b, int):
                    src = SL[:, :, b, :]
                else:
                    src = SL[:, :, bass.ds(b, 1), :].rearrange("p k a s -> p k (a s)")
                sp.dma_start(slT[:], src).then_inc(load_in.sem, 16)

            def load_ctx(b):
                reuse(sp, cao_mm, b)
                sp.dma_start(ctxT[:, :, 0:L], at(ins["ctxT"].rearrange("b (k p) l -> p b k l", p=P), b)).then_inc(ctx_in.sem, 16)
                sp.dma_start(ctx[:], at2(ins["ctx_1024"].rearrange("b l d -> l b d"), b)).then_inc(ctx_in.sem, 16)

            load(0)
            sp.wait_ge(rows_done.sem, 1)
            load_ctx(0)
            for dst, src in const_loads:
                sp.dma_start(dst, src).then_inc(const_in.sem, 16)
            for n, (src, _, _) in enumerate(stages):
                if n >= 2:
                    sp.wait_ge(wl_done.sem, n - 1)
                if n >= 1:
                    sp.wait_ge(wst_in.sem, 16 * n)
                sp.dma_start(stage(n, src), src).then_inc(wst_in.sem, 16)
            with sp.Fori(1, NB) as b:
                load(b)
                load_ctx(b)

        all_const = 16 * len(const_loads)

        @block.gpsimd
        def _(pool):
            pool.memset(cmask[:], 1.0)
            pool.memset(y[:, :, D:D + 1], 1.0)
            pool.memset(y[:, :, D + 1:YW], 0.0)
            pool.memset(ctxT[:], 0.0).then_inc(rows_done.sem, 1)
            pool.wait_ge(rows_done.sem, 1)
            pool.affine_select(out=cmask[:], in_=cmask[:], compare_op=ALU.is_ge, fill=0.0, base=0,
                               pattern=[[1, P]], channel_multiplier=-1).then_inc(rows_done.sem, 1)
            for n, (src, hi, lo) in enumerate(stages):
                pool.wait_ge(wst_in.sem, 16 * (n + 1))
                alone(pool)
                pool.tensor_copy(hi, stage(n, src)).then_inc(wh_done.sem, 1)
                pool.wait_ge(wh_done.sem, n + 1)
                pool.tensor_tensor(lo, stage(n, src), hi.bitcast(F32), ALU.subtract).then_inc(wl_done.sem, 1)
            pool.wait_ge(const_in.sem, all_const)

            def rstd(name, b):
                l = lns[name]
                need(pool, l["mvd"], b)
                alone(pool)
                pool.tensor_scalar(l["rs"][:], l["mv"][:, :, 1], LN_EPS, None, ALU.add).then_inc(l["rss"].sem, 1)
                need(pool, l["rss"], b, 1)
                pool.tensor_tensor(l["rs"][:], l["rs"][:], self.minus_half[:, 0:TT], ALU.pow).then_inc(l["rss"].sem, 1)

            def y2_bias(b):
                need(pool, lns["lb"]["done"], b)
                reuse(pool, r3_done, b)
                pool.tensor_tensor(y2b[:], y2[:], spread(rows[:, 6:7, :], 1, TT), ALU.add).then_inc(y2b_done.sem, 1)

            def hidden_hi(b, q):
                need(pool, h_ev, b, q + 1)
                if q < 2:
                    reuse(pool, f2_mm, b, q + 3)
                else:
                    need(pool, f2_mm, b, q - 1)
                alone(pool)
                pool.tensor_copy(hh[:, q % 2], hf[:, q % 2]).then_inc(hh_done.sem, 1)

            def schedule(f, k):
                if f is not None:
                    rstd("l3", f)
                if k is not None:
                    y2_bias(k)
                    hidden_hi(k, 0)
                    hidden_hi(k, 1)
                if f is not None:
                    rstd("la", f)
                if k is not None:
                    hidden_hi(k, 2)
                    hidden_hi(k, 3)
                    rstd("lc", k)
                if f is not None:
                    rstd("lb", f)

            turns(pool, schedule, NB)

        @block.scalar
        def _(act):
            act.wait_ge(const_in.sem, all_const)
            act.wait_ge(bias_done.sem, 1)

            def copy_out(dst, src, ready, prev, done, b):
                need(act, ready, b)
                reuse(act, prev, b)
                act.copy(dst, src).then_inc(done.sem, 1)

            def sa_exps(b):
                need(act, sa_mm, b)
                reuse(act, sao_mm, b)
                act.activation(E[:].rearrange("p a q -> p (a q)"), psS[:, 0:3 * P], ACT.Exp, bias=bias16[:, 0:1], scale=ISQ)\
                   .then_inc(sa_exp.sem, 1)

            def ca_exps(b):
                need(act, cm_done, b)
                reuse(act, pct_mm, b)
                reuse(act, crec_done, b)
                for t in range(TT):
                    last = act.activation(pc[:, t, :], psS[:, t * P:t * P + L], ACT.Exp, bias=small["cbias"][:, t:t + 1],
                                          scale=ISQ, accum_out=small["csum"][:, t:t + 1])
                last.then_inc(ca_exp.sem, 1)

            def hidden_out(b, q):
                need(act, h_mm, b, q + 1)
                if q < 2:
                    reuse(act, hl_done, b, q + 3)
                else:
                    need(act, hl_done, b, q - 1)
                for j in range(2):
                    c_ = 2 * q + j
                    last = act.activation(hf[:, q % 2, j, :], psH[:, q % 2, j, :], ACT.Relu, bias=fb1[:, c_:c_ + 1])
                last.then_inc(h_ev.sem, 1)

            def schedule(f, k):
                flat = lambda t_: t_[:].rearrange("p k s -> p (k s)")
                if f is not None:
                    copy_out(flat(so), psT[:], so_mm, mix_mm, so_ev, f)
                if k is not None:
                    copy_out(flat(y2h), psY[:], y2t_mm, f2_mm, y2h_ev, k)
                if f is not None:
                    copy_out(flat(yT), psT[:], yt_mm, sa_mm, yt_ev, f)
                if k is not None:
                    hidden_out(k, 0)
                if f is not None:
                    sa_exps(f)
                if k is not None:
                    hidden_out(k, 1)
                if f is not None:
                    copy_out(flat(y1T), psT[:], y1t_mm, ca_mm, y1t_ev, f)
                if k is not None:
                    hidden_out(k, 2)
                if f is not None:
                    ca_exps(f)
                    copy_out(pcT[:], psT[0:L, 0:TT * P], pct_mm, cao_mm, pct_ev, f)
                if k is not None:
                    hidden_out(k, 3)

            turns(act, schedule, NB)

        @block.vector
        def _(dve):
            dve.memset(bias16[:], -float(D) * ISQ).then_inc(bias_done.sem, 1)
            dve.wait_ge(rows_done.sem, 2)
            dve.wait_ge(const_in.sem, all_const)

            def stats(name, b, src):
                l = lns[name]
                reuse(dve, l["done"], b)
                alone(dve)
                for t in range(TT):
                    last = dve.bn_stats(l["bs"][:, t, :], src[:, t, :])
                last.then_inc(l["st"].sem, 1)
                need(dve, l["st"], b)
                alone(dve)
                for t in range(TT):
                    last = dve.bn_aggr(l["mv"][:, t, :], l["bs"][:, t, :])
                last.then_inc(l["mvd"].sem, 1)

            def apply(name, b, src, dst, g):
                l = lns[name]
                need(dve, l["mvd"], b)
                for t in range(TT):
                    last = dve.scalar_tensor_tensor(out=l["xg"][:, t, :], in0=src[:, t, :], scalar=l["mv"][:, t, 0:1],
                                                    in1=rows[:, g, :], op0=ALU.subtract, op1=ALU.mult)
                last.then_inc(l["xgd"].sem, 1)
                need(dve, l["rss"], b)
                need(dve, l["xgd"], b)
                for t in range(TT):
                    last = dve.scalar_tensor_tensor(out=dst[:, t, :], in0=l["xg"][:, t, :], scalar=l["rs"][:, t:t + 1],
                                                    in1=rows[:, g + 1, :], op0=ALU.mult, op1=ALU.add)
                last.then_inc(l["done"].sem, 1)

            def x2(b):
                need(dve, mix_mm, b)
                x, rc = at(X, b), at2(self.rcomb, b)
                for t in range(TT):
                    last = dve.scalar_tensor_tensor(out=x[:, t, :], in0=psO[:, t * D:(t + 1) * D], scalar=rc[:, t:t + 1],
                                                    in1=x[:, t, :], op0=ALU.mult, op1=ALU.add)
                last.then_inc(x2_done.sem, 1)
                need(dve, x2_done, b)
                stats("l3", b, x)

            def y0(b):
                l, x = lns["l3"], at(X, b)
                need(dve, l["rss"], b)
                reuse(dve, sao_mm, b)
                reuse(dve, r1_done, b)
                for t in range(TT):
                    last = dve.tensor_scalar(y[:, t, 0:D], x[:, t, :], l["mv"][:, t, 0:1], l["rs"][:, t:t + 1],
                                             ALU.subtract, ALU.mult)
                last.then_inc(l["done"].sem, 1)

            def mask(b):
                need(dve, sa_exp, b)
                diag = E[:, 0:3:2, :]
                dve.tensor_tensor(diag, diag, spread(cmask[:].rearrange("p (a q) -> p a q", a=1), 1, 2), ALU.mult)\
                   .then_inc(sa_mask.sem, 1)

            def residual1(b):
                need(dve, sao_mm, b)
                for t, bank in enumerate((psO, psO2)):
                    last = dve.reciprocal(small["srec"][:, t:t + 1], bank[:, D:D + 1])
                last.then_inc(srec_done.sem, 1)
                need(dve, srec_done, b)
                for t, bank in enumerate((psO, psO2)):
                    last = dve.scalar_tensor_tensor(out=r1[:, t, :], in0=bank[:, 0:D], scalar=small["srec"][:, t:t + 1],
                                                    in1=y[:, t, 0:D], op0=ALU.mult, op1=ALU.add)
                last.then_inc(r1_done.sem, 1)
                need(dve, r1_done, b)
                stats("la", b, r1)

            def ca_max(b):
                need(dve, ca_mm, b)
                dve.tensor_reduce(small["cmax"][:], psS[:, 0:2 * P].rearrange("p (t l) -> p t l", t=TT)[:, :, 0:L], AX.X,
                                  ALU.max).then_inc(cm_done.sem, 1)
                need(dve, cm_done, b, 1)
                reuse(dve, ca_exp, b)
                dve.tensor_scalar(small["cbias"][:], small["cmax"][:], -ISQ, None, ALU.mult).then_inc(cm_done.sem, 1)

            def residual2(b):
                need(dve, ca_exp, b)
                dve.reciprocal(small["crec"][:], small["csum"][:]).then_inc(crec_done.sem, 1)
                need(dve, crec_done, b)
                need(dve, cao_mm, b)
                for t in range(TT):
                    last = dve.scalar_tensor_tensor(out=r2[:, t, :], in0=psO[:, t * D:(t + 1) * D], scalar=small["crec"][:, t:t + 1],
                                                    in1=y1[:, t, :], op0=ALU.mult, op1=ALU.add)
                last.then_inc(r2_done.sem, 1)
                need(dve, r2_done, b)
                stats("lb", b, r2)

            def y2_lo(b):
                need(dve, y2h_ev, b)
                reuse(dve, f2_mm, b)
                dve.tensor_tensor(y2l[:].rearrange("p k s -> p (k s)"), psY[:], y2h[:].bitcast(F32).rearrange("p k s -> p (k s)"),
                                  ALU.subtract).then_inc(y2l_ev.sem, 1)

            def hidden_lo(b, q):
                need(dve, hh_done, b, q + 1)
                dve.tensor_tensor(hl[:, q % 2], hf[:, q % 2], hh[:, q % 2].bitcast(F32), ALU.subtract).then_inc(hl_done.sem, 1)

            def residual3(b):
                need(dve, f2_mm, b)
                need(dve, y2b_done, b)
                dve.tensor_tensor(r3[:], psF[:], y2b[:], ALU.add).then_inc(r3_done.sem, 1)
                need(dve, r3_done, b)
                stats("lc", b, r3)

            def x3(b):
                x = at(X, b)
                need(dve, lns["lc"]["done"], b)
                for t in range(TT):
                    last = dve.scalar_tensor_tensor(out=x[:, t, :], in0=y3[:, t, :], scalar=self.gates[:, 1:2],
                                                    in1=x[:, t, :], op0=ALU.mult, op1=ALU.add)
                last.then_inc(x3_done.sem, 1)

            def schedule(f, k):
                if f is not None:
                    x2(f)
                if k is not None:
                    y2_lo(k)
                if f is not None:
                    y0(f)
                if k is not None:
                    hidden_lo(k, 0)
                if f is not None:
                    mask(f)
                if k is not None:
                    hidden_lo(k, 1)
                if f is not None:
                    residual1(f)
                if f is not None:
                    apply("la", f, r1, y1, 0)
                if k is not None:
                    hidden_lo(k, 2)
                if f is not None:
                    ca_max(f)
                if k is not None:
                    hidden_lo(k, 3)
                if f is not None:
                    residual2(f)
                if k is not None:
                    residual3(k)
                if k is not None:
                    apply("lc", k, r3, y3, 4)
                    x3(k)
                if f is not None:
                    if not isinstance(f, int) or f:
                        reuse(dve, y2b_done, f)
                        reuse(dve, y2t_mm, f)
                    apply("lb", f, r2, y2, 2)

            turns(dve, schedule, NB)

        @block.tensor
        def _(pe):
            def mm(out, lhsT, rhs, start=True, stop=True):
                return pe.matmul(out, lhsT, rhs, start=start, stop=stop)

            def mm3(out, lh, ll, rh, rl, start, stop, shared=False):
                pe.matmul(out, lh, rh, start=start, stop=False, skip_group_check=shared)
                pe.matmul(out, lh, rl, start=False, stop=False, skip_group_check=shared)
                return pe.matmul(out, ll, rh, start=False, stop=stop, skip_group_check=shared)

            def turn4(dst, src):
                for k in range(2):
                    for t in range(2):
                        last = pe.transpose(dst[:, k * S + t * P:k * S + (t + 1) * P], src[:, t, k * P:(k + 1) * P], ident[:])
                return last

            def slot_outputs(b):
                need(pe, load_in, b)
                reuse(pe, pct_ev, b)
                turn4(psT, slT).then_inc(so_mm.sem, 1)

            def mix(b):
                need(pe, so_ev, b)
                reuse(pe, r2_done, b)
                for t in range(TT):
                    for k in range(TT):
                        last = mm(psO[:, t * D:(t + 1) * D], combT[:, k, t * P:(t + 1) * P], so[:, k, :], k == 0, k == TT - 1)
                last.then_inc(mix_mm.sem, 1)

            def turn_y(b):
                need(pe, lns["l3"]["done"], b)
                turn4(psT, y).then_inc(yt_mm.sem, 1)

            def sa_scores(b):
                need(pe, yt_ev, b)
                reuse(pe, ca_exp, b)
                for k in range(KD):
                    mm(psS[:, 0:S], yT[:, k, 0:P], yT[:, k, :], k == 0, k == KD - 1)
                for k in range(KD):
                    last = mm(psS[:, S:S + P], yT[:, k, P:S], yT[:, k, P:S], k == 0, k == KD - 1)
                last.then_inc(sa_mm.sem, 1)

            def sa_out(b):
                need(pe, sa_mask, b)
                need(pe, x2_done, b)
                reuse(pe, r1_done, b)
                mm(psO[:, 0:YW], E[:, 0, :], y[:, 0, :])
                mm(psO2[:, 0:YW], E[:, 1, :], y[:, 0, :], True, False)
                mm(psO2[:, 0:YW], E[:, 2, :], y[:, 1, :], False, True).then_inc(sao_mm.sem, 1)

            def turn_y1(b):
                need(pe, lns["la"]["done"], b)
                turn4(psT, y1).then_inc(y1t_mm.sem, 1)

            def ca_scores(b):
                need(pe, y1t_ev, b)
                need(pe, ctx_in, b)
                for t in range(TT):
                    for k in range(KD):
                        last = mm(psS[:, t * P:(t + 1) * P], y1T[:, k, t * P:(t + 1) * P], ctxT[:, k, :], k == 0, k == KD - 1)
                last.then_inc(ca_mm.sem, 1)

            def turn_pc(b):
                need(pe, ca_exp, b)
                for t in range(TT):
                    last = pe.transpose(psT[0:L, t * P:(t + 1) * P], pc[:, t, :], ident[:])
                last.then_inc(pct_mm.sem, 1)

            def ca_out(b):
                need(pe, pct_ev, b)
                for t in range(TT):
                    last = mm(psO[:, t * D:(t + 1) * D], pcT[:, t * P:(t + 1) * P], ctx[:])
                last.then_inc(cao_mm.sem, 1)

            def turn_y2(b):
                need(pe, lns["lb"]["done"], b)
                reuse(pe, y2l_ev, b)
                turn4(psY, y2).then_inc(y2t_mm.sem, 1)

            def mlp_in(b, q):
                if q == 0:
                    need(pe, y2l_ev, b)
                if q < 2:
                    reuse(pe, h_ev, b, q + 3)
                else:
                    need(pe, h_ev, b, q - 1)
                for j in range(2):
                    cols = slice((2 * q + j) * P, (2 * q + j + 1) * P)
                    for k in range(KD):
                        last = mm3(psH[:, q % 2, j, :], w1h[:, k, cols], w1l[:, k, cols], y2h[:, k, :], y2l[:, k, :],
                                   k == 0, k == KD - 1)
                last.then_inc(h_mm.sem, 1)

            def mlp_out(b, q):
                need(pe, hl_done, b, q + 1)
                if q == 0:
                    reuse(pe, r3_done, b)
                for j in range(2):
                    c_ = 2 * q + j
                    for t in range(TT):
                        cols = slice(t * P, (t + 1) * P)
                        last = mm3(psF[:, t, :], hh[:, q % 2, j, cols], hl[:, q % 2, j, cols], w2h[:, c_, :], w2l[:, c_, :],
                                   c_ == 0 and t == 0, c_ == FC - 1, shared=True)
                last.then_inc(f2_mm.sem, 1)

            pe.wait_ge(wl_done.sem, len(stages))

            def schedule(f, k):
                if f is not None:
                    slot_outputs(f)
                    mix(f)
                if k is not None:
                    turn_y2(k)
                    mlp_in(k, 0)
                if f is not None:
                    turn_y(f)
                if k is not None:
                    mlp_in(k, 1)
                if f is not None:
                    sa_scores(f)
                if k is not None:
                    mlp_out(k, 0)
                if f is not None:
                    sa_out(f)
                if k is not None:
                    mlp_in(k, 2)
                    mlp_out(k, 1)
                if f is not None:
                    turn_y1(f)
                if k is not None:
                    mlp_in(k, 3)
                if f is not None:
                    ca_scores(f)
                if k is not None:
                    mlp_out(k, 2)
                if f is not None:
                    turn_pc(f)
                    ca_out(f)
                if k is not None:
                    mlp_out(k, 3)

            turns(pe, schedule, NB)

    def phase_d(self, c):
        nc, ins, ident = self.nc, self.ins, self.ident
        sb = lambda n, s, d=F32: self.sb(c, n, s, d)
        sig = lambda n, per=1, step=1: self.sig(c, n, per, step)
        X = self.X[:].rearrange("p (j a) t d -> p j (a t) d", j=NBLK)
        HW = HC * P
        CP = HC // 2 + 1
        Y = self.out.rearrange("(j a) (t p) d -> p j (a t) d", p=P, j=NBLK)

        uph, upl = sb("up_hi", [P, KD, HW], F32R), sb("up_lo", [P, KD, HW], F32R)
        gth, gtl = sb("gate_hi", [P, KD, HW], F32R), sb("gate_lo", [P, KD, HW], F32R)
        dnh, dnl = sb("down_hi", [P, HC, D], F32R), sb("down_lo", [P, HC, D], F32R)
        stage = sb("m_stage", [P, 2, CP * D])
        router = sb("router", [P, KD, P])
        experts = sb("experts", [P, NE1])
        experts_i = sb("experts_i", [P, NE1], mybir.dt.int32)
        zn = sb("m_z", [P, BT, D])
        zf = sb("m_zT", [P, KD, TB])
        zh, zl = sb("m_zT_hi", [P, KD, TB], F32R), sb("m_zT_lo", [P, KD, TB], F32R)
        bs, mv, rs = sb("m_bs", [P, BT, 6]), sb("m_mv", [P, BT, 2]), sb("m_rs", [P, BT])
        top, topd = sb("top", [P, BT, 8]), sb("top_exp", [P, BT, 8])
        idx, idxf = sb("top_idx", [P, BT, 8], U32), sb("top_idx_f", [P, BT, 2])
        tsum, trec = sb("top_sum", [P, BT]), sb("top_rec", [P, BT])
        wtop = sb("top_weight", [P, BT, 2])
        pick = sb("pick", [P, 2, BT, NE1])
        wd = sb("route", [P, P])
        wdT = sb("routeT", [BT * NE1, P])
        wb = sb("route_spread", [P, EC, TB])
        sg, sw = sb("silu", [P, 2, TB]), sb("silu_weighted", [P, 2, TB])
        hf = sb("m_hidden", [P, 2, TB])
        hh, hl = sb("m_hidden_hi", [P, 2, TB], F32R), sb("m_hidden_lo", [P, 2, TB], F32R)
        o = sb("m_out", [P, BT, D])

        psY = self.ps(c, "m_up", [P, 2, TB])
        psG = self.ps(c, "m_gate", [P, 2, TB])
        psA = self.ps(c, "m_acc", [P, BT, D])
        psT = self.ps(c, "m_turned", [P, TB])
        psR = self.ps(c, "m_router", [P, BT, P])

        fill_done, iota_done, exp_ready = sig("m_fill"), sig("m_iota"), sig("m_experts")
        st_in, hi_done, lo_done = sig("m_stage_in", 1, 16), sig("m_whi"), sig("m_wlo")
        gate_in = sig("m_router_in", 1, 16)
        st, mvd, rss, zn_done = sig("m_st"), sig("m_mvd"), sig("m_rss", 2), sig("m_zn")
        zt_mm, zt_ev, r_mm = sig("m_zt_mm", 2), sig("m_zt_ev", 2), sig("m_r_mm")
        top_done, topd_done, texp, r_step = sig("m_top", 3), sig("m_topd"), sig("m_texp"), sig("m_r_step", 7)
        wdt_mm, wdt_ev, wd_out, wb_in = sig("m_wdt_mm"), sig("m_wdt_ev"), sig("m_wd_out", 1, 16), sig("m_wb_in", 4, 16)
        zh_done, zl_done = sig("m_zh"), sig("m_zl")
        yg_mm, silu_ev, sw_done = sig("m_yg_mm", HC), sig("m_silu", HC), sig("m_sw", EC)
        hf_done, hh_done, hl_done, dn_mm = sig("m_hf", HC), sig("m_hh", HC), sig("m_hl", HC), sig("m_dn_mm", HC)
        o_done, o_out = sig("m_o"), sig("m_o_out", 1, 16)

        upv, gtv = ins["up"].rearrange("(k p) h -> p k h", p=P), ins["gate"].rearrange("(k p) h -> p k h", p=P)
        dnv = ins["down"].rearrange("(c p) d -> p c d", p=P)
        stages = [(upv[:, k], uph[:, k], upl[:, k]) for k in range(KD)] + [(gtv[:, k], gth[:, k], gtl[:, k]) for k in range(KD)] \
            + [(dnv[:, 0:CP], dnh[:, 0:CP], dnl[:, 0:CP]), (dnv[:, CP:HC], dnh[:, CP:HC], dnl[:, CP:HC])]

        def staged(n, src):
            if len(src.shape) == 3:
                return stage[:, n % 2, 0:src.shape[1] * D].rearrange("p (c d) -> p c d", d=D)
            return stage[:, n % 2, 0:HW]

        block = c.enter_context(nc.Block())

        @block.sync
        def _(sp):
            for n, (src, _, _) in enumerate(stages):
                if n >= 2:
                    sp.wait_ge(lo_done.sem, n - 1)
                if n >= 1:
                    sp.wait_ge(st_in.sem, 16 * n)
                sp.dma_start(staged(n, src), src).then_inc(st_in.sem, 16)
                if n == 0:
                    sp.wait_ge(fill_done.sem, 1)
                    sp.dma_start(router[:, :, 0:NE1], ins["gate_wT"].rearrange("(k p) e -> p k e", p=P)).then_inc(gate_in.sem, 16)

            chunks = wb[:].rearrange("p (m r) q -> p m r q", r=3)
            pairs = self.routes.rearrange("(a m two t) q -> a m two (t q)", a=1, two=2, t=BT)

            def schedule(f, k):
                if f is not None:
                    need(sp, wdt_ev, f)
                    sp.dma_start(self.routes, wdT[:]).then_inc(wd_out.sem, 16)
                    need(sp, wd_out, f)
                    reuse(sp, sw_done, f)
                    for r, rows, odd in ((0, slice(0, P), 0), (1, slice(0, P // 2), 0), (1, slice(P // 2, P), 1), (2, slice(0, P), 1)):
                        sp.dma_start(chunks[rows, :, r, :], spread(pairs[:, :, odd, :], 0, P)[rows]).then_inc(wb_in.sem, 16)
                if k is not None:
                    need(sp, o_done, k)
                    sp.dma_start(at(Y, k), o[:]).then_inc(o_out.sem, 16)

            turns(sp, schedule, NBLK)
            need(sp, o_out, NBLK - 1)

        @block.gpsimd
        def _(pool):
            pool.memset(router[:], 0.0)
            pool.memset(wd[:], 0.0)
            pool.iota(experts_i[:], pattern=[[1, NE1]], base=0, channel_multiplier=0).then_inc(fill_done.sem, 1)

            def rstd(b):
                need(pool, mvd, b)
                alone(pool)
                pool.tensor_scalar(rs[:], mv[:, :, 1], LN_EPS, None, ALU.add).then_inc(rss.sem, 1)
                need(pool, rss, b, 1)
                pool.tensor_tensor(rs[:], rs[:], self.minus_half[:, 0:BT], ALU.pow).then_inc(rss.sem, 1)

            def weigh(b, n):
                need(pool, silu_ev, b, n + 1)
                if n == 0:
                    need(pool, wb_in, b)
                if n < 2:
                    reuse(pool, hf_done, b, EC - 1 + n)
                else:
                    need(pool, hf_done, b, n - 1)
                pool.tensor_tensor(sw[:, n % 2, :], sg[:, n % 2, :], wb[:, n, :], ALU.mult).then_inc(sw_done.sem, 1)

            def schedule(f, k):
                if f is not None:
                    rstd(f)
                if k is not None:
                    for n in range(EC):
                        weigh(k, n)

            turns(pool, schedule, NBLK)

        @block.scalar
        def _(act):
            for n, (src, hi, _) in enumerate(stages):
                act.wait_ge(st_in.sem, 16 * (n + 1))
                act.copy(hi, staged(n, src)).then_inc(hi_done.sem, 1)

            def zT_out(b, k):
                need(act, zt_mm, b, k + 1)
                if k == 0:
                    reuse(act, zl_done, b)
                    reuse(act, r_mm, b)
                act.copy(zf[:, k, :], psT[:]).then_inc(zt_ev.sem, 1)

            def top_exp(b):
                need(act, topd_done, b)
                act.activation(topd[:], topd[:], ACT.Exp).then_inc(texp.sem, 1)

            def wdT_out(b):
                need(act, wdt_mm, b)
                reuse(act, wd_out, b)
                act.copy(wdT[:], psR[0:BT * NE1, 0, :]).then_inc(wdt_ev.sem, 1)

            def z_hi(b):
                need(act, zt_ev, b)
                reuse(act, yg_mm, b)
                act.copy(zh[:], zf[:]).then_inc(zh_done.sem, 1)

            def silu(b, n):
                need(act, yg_mm, b, n + 1)
                if n < 2:
                    reuse(act, hf_done, b, HC - 1 + n)
                else:
                    need(act, hf_done, b, n - 1)
                act.activation(sg[:, n % 2, :], psG[:, n % 2, :], ACT.Silu).then_inc(silu_ev.sem, 1)

            def hidden_hi(b, n):
                need(act, hf_done, b, n + 1)
                if n < 2:
                    reuse(act, dn_mm, b, HC - 1 + n)
                else:
                    need(act, dn_mm, b, n - 1)
                act.copy(hh[:, n % 2, :], hf[:, n % 2, :]).then_inc(hh_done.sem, 1)

            prep = {3: lambda b: zT_out(b, 0), 4: lambda b: zT_out(b, 1), 9: top_exp, 12: wdT_out}

            def schedule(f, k):
                for n in range(HC + 1):
                    if f is not None and n in prep:
                        prep[n](f)
                    if k is not None:
                        if n < HC:
                            silu(k, n)
                        if n >= 1:
                            hidden_hi(k, n - 1)
                if f is not None:
                    z_hi(f)

            turns(act, schedule, NBLK)

        @block.vector
        def _(dve):
            for n, (src, hi, lo) in enumerate(stages):
                dve.wait_ge(hi_done.sem, n + 1)
                dve.tensor_tensor(lo, staged(n, src), hi.bitcast(F32), ALU.subtract).then_inc(lo_done.sem, 1)
            dve.wait_ge(fill_done.sem, 1)
            dve.tensor_copy(experts[:], experts_i[:]).then_inc(exp_ready.sem, 1)
            dve.wait_ge(exp_ready.sem, 1)

            def stats(b):
                x = at(X, b)
                reuse(dve, zn_done, b)
                alone(dve)
                for t in range(BT):
                    last = dve.bn_stats(bs[:, t, :], x[:, t, :])
                last.then_inc(st.sem, 1)
                need(dve, st, b)
                alone(dve)
                for t in range(BT):
                    last = dve.bn_aggr(mv[:, t, :], bs[:, t, :])
                last.then_inc(mvd.sem, 1)

            def apply(b):
                x = at(X, b)
                need(dve, rss, b)
                reuse(dve, zt_mm, b)
                for t in range(BT):
                    last = dve.tensor_scalar(zn[:, t, :], x[:, t, :], mv[:, t, 0:1], rs[:, t:t + 1], ALU.subtract, ALU.mult)
                last.then_inc(zn_done.sem, 1)

            def top_two(b):
                need(dve, r_mm, b)
                alone(dve)
                for t in range(BT):
                    last = dve.max(top[:, t, :], psR[:, t, 0:NE1])
                last.then_inc(top_done.sem, 1)
                need(dve, top_done, b, 1)
                alone(dve)
                for t in range(BT):
                    last = dve.max_index(idx[:, t, :], top[:, t, :], psR[:, t, 0:NE1])
                last.then_inc(top_done.sem, 1)
                need(dve, top_done, b, 2)
                dve.tensor_copy(idxf[:], idx[:, :, 0:2]).then_inc(top_done.sem, 1)
                dve.tensor_tensor(topd[:], top[:], spread(top[:, :, 0:1], 2, 8), ALU.subtract).then_inc(topd_done.sem, 1)

            def route(b):
                need(dve, texp, b)
                dve.tensor_reduce(tsum[:], topd[:], AX.X, ALU.add).then_inc(r_step.sem, 1)
                need(dve, r_step, b, 1)
                dve.reciprocal(trec[:], tsum[:]).then_inc(r_step.sem, 1)
                need(dve, r_step, b, 2)
                dve.tensor_tensor(wtop[:], topd[:, :, 0:2], spread(trec[:].rearrange("p (t a) -> p t a", a=1), 2, 2), ALU.mult)\
                   .then_inc(r_step.sem, 1)
                need(dve, top_done, b)
                need(dve, r_step, b, 3)
                for i in range(2):
                    last = dve.tensor_tensor(pick[:, i], spread(experts[:].rearrange("p (a e) -> p a e", a=1), 1, BT),
                                             spread(idxf[:, :, i:i + 1], 2, NE1), ALU.is_equal)
                last.then_inc(r_step.sem, 1)
                need(dve, r_step, b, 4)
                for i in range(2):
                    last = dve.tensor_tensor(pick[:, i], pick[:, i], spread(wtop[:, :, i:i + 1], 2, NE1), ALU.mult)
                last.then_inc(r_step.sem, 1)
                need(dve, r_step, b, 5)
                reuse(dve, wdt_mm, b)
                dve.tensor_tensor(wd[:, 0:NE1 * BT].rearrange("p (e t) -> p t e", t=BT), pick[:, 0], pick[:, 1], ALU.add)\
                   .then_inc(r_step.sem, 1)
                need(dve, r_step, b, 6)
                dve.tensor_copy(tsum[:], trec[:]).then_inc(r_step.sem, 1)

            def z_lo(b):
                need(dve, zh_done, b)
                dve.tensor_tensor(zl[:], zf[:], zh[:].bitcast(F32), ALU.subtract).then_inc(zl_done.sem, 1)

            def hidden(b, n):
                if n < EC:
                    need(dve, sw_done, b, n + 1)
                else:
                    need(dve, silu_ev, b, n + 1)
                if n < 2:
                    reuse(dve, hl_done, b, HC - 1 + n)
                else:
                    need(dve, hl_done, b, n - 1)
                s_ = (sw if n < EC else sg)[:, n % 2, :]
                dve.tensor_tensor(hf[:, n % 2, :], psY[:, n % 2, :], s_, ALU.mult).then_inc(hf_done.sem, 1)

            def hidden_lo(b, n):
                need(dve, hh_done, b, n + 1)
                dve.tensor_tensor(hl[:, n % 2, :], hf[:, n % 2, :], hh[:, n % 2, :].bitcast(F32), ALU.subtract)\
                   .then_inc(hl_done.sem, 1)

            def result(b):
                x = at(X, b)
                need(dve, dn_mm, b)
                reuse(dve, o_out, b)
                for h in range(2):
                    tiles = slice(2 * h, 2 * h + 2)
                    last = dve.scalar_tensor_tensor(out=o[:, tiles, :], in0=psA[:, tiles, :], scalar=self.gates[:, 3:4],
                                                    in1=x[:, tiles, :], op0=ALU.mult, op1=ALU.add)
                last.then_inc(o_done.sem, 1)

            prep = {0: stats, 1: apply, 7: top_two, 10: route}

            def schedule(f, k):
                for n in range(HC + 1):
                    if f is not None and n in prep:
                        prep[n](f)
                    if k is not None:
                        if n < HC:
                            hidden(k, n)
                        if n >= 1:
                            hidden_lo(k, n - 1)
                if f is not None:
                    z_lo(f)
                if k is not None:
                    result(k)

            turns(dve, schedule, NBLK)

        @block.tensor
        def _(pe):
            pe.wait_ge(lo_done.sem, len(stages))
            pe.wait_ge(gate_in.sem, 16)

            def mm3(out, lh, ll, rh, rl, start, stop, shared=False):
                pe.matmul(out, lh, rh, start=start, stop=False, skip_group_check=shared)
                pe.matmul(out, lh, rl, start=False, stop=False, skip_group_check=shared)
                return pe.matmul(out, ll, rh, start=False, stop=stop, skip_group_check=shared)

            def turn_z(b, k):
                if k == 0:
                    need(pe, zn_done, b)
                    reuse(pe, zt_ev, b)
                else:
                    need(pe, zt_ev, b, 1)
                for t in range(BT):
                    last = pe.transpose(psT[:, t * P:(t + 1) * P], zn[:, t, k * P:(k + 1) * P], ident[:])
                last.then_inc(zt_mm.sem, 1)

            def route(b):
                need(pe, zt_ev, b)
                reuse(pe, wdt_ev, b)
                for t in range(BT):
                    for k in range(KD):
                        last = pe.matmul(psR[:, t, :], zf[:, k, t * P:(t + 1) * P], router[:, k, :], start=(k == 0), stop=(k == KD - 1))
                last.then_inc(r_mm.sem, 1)

            def turn_w(b):
                need(pe, r_step, b, 6)
                need(pe, top_done, b)
                pe.transpose(psR[:, 0, :], wd[:], ident[:]).then_inc(wdt_mm.sem, 1)

            def up(b, n):
                if n == 0:
                    need(pe, zl_done, b)
                if n < 2:
                    reuse(pe, hf_done, b, HC - 1 + n)
                else:
                    need(pe, hf_done, b, n - 1)
                cols = slice(n * P, (n + 1) * P)
                for ps_, wh, wl in ((psG, gth, gtl), (psY, uph, upl)):
                    for k in range(KD):
                        last = mm3(ps_[:, n % 2, :], wh[:, k, cols], wl[:, k, cols], zh[:, k, :], zl[:, k, :], k == 0, k == KD - 1)
                last.then_inc(yg_mm.sem, 1)

            def down(b, n):
                need(pe, hl_done, b, n + 1)
                if n == 0:
                    reuse(pe, o_done, b)
                for t in range(BT):
                    cols = slice(t * P, (t + 1) * P)
                    last = mm3(psA[:, t, :], hh[:, n % 2, cols], hl[:, n % 2, cols], dnh[:, n, :], dnl[:, n, :],
                               n == 0 and t % 2 == 0, n == HC - 1, shared=True)
                last.then_inc(dn_mm.sem, 1)

            prep = {2: lambda b: turn_z(b, 0), 3: lambda b: turn_z(b, 1), 6: route, 11: turn_w}

            def schedule(f, k):
                for n in range(HC + 1):
                    if f is not None and n in prep:
                        prep[n](f)
                    if k is not None:
                        if n < HC:
                            up(k, n)
                        if n >= 1:
                            down(k, n - 1)

            turns(pe, schedule, NBLK)


def spread(ap, dim, n):
    shape = list(ap.shape)
    shape[dim] = n
    return ap.broadcast_to(shape)


def at2(tensor, b):
    if isinstance(b, int):
        return tensor[:, b, :]
    return tensor[:, bass.ds(b, 1), :].rearrange("p a n -> p (a n)")


def layout(inputs):
    import numpy as np

    d = {k: np.asarray(v) for k, v in inputs.items()}

    def columns(v):
        return v.reshape(-1, P).T

    d["wk8"] = np.tile(d.pop("L0_xattn_Wk"), (1, UG))
    d["bk8"] = np.tile(d.pop("L0_xattn_bk"), UG)
    d["bq_cols"] = columns(d.pop("L0_xattn_bq"))
    d["ctxT"] = d["ctx_1024"].transpose(0, 2, 1)
    d["w1_pairs"] = d.pop("L0_ffn_w1").transpose(1, 0, 2).reshape(D, NE0 * H0)
    d["b1_cols"] = columns(d.pop("L0_ffn_b1").reshape(-1))
    d["b2_cols"] = d.pop("L0_ffn_b2").T.reshape(KD, P, NE0).transpose(1, 0, 2)
    d["fb1_cols"] = columns(d.pop("L1_xattn_b1"))
    w1, ws1, hs = d.pop("L1_ffn_W1"), d.pop("L1_ffn_Ws1"), SH
    d["up"] = np.concatenate([w1[:, :H1].reshape(-1, D), ws1[:hs]]).T
    d["gate"] = np.concatenate([w1[:, H1:].reshape(-1, D), ws1[hs:]]).T
    d["down"] = np.concatenate([d.pop("L1_ffn_W2").transpose(0, 2, 1).reshape(-1, D), d.pop("L1_ffn_Ws2").T])
    d["gate_wT"] = d.pop("L1_ffn_gate_w").T
    return {k: np.ascontiguousarray(v) for k, v in d.items()}


def kernel(**inputs):
    from concourse import bacc
    from concourse.bass_utils import run_bass_kernel_spmd

    nc = bacc.Bacc("TRN2", target_bir_lowering=False, num_devices=1)
    arrays = layout(inputs)
    ins = {name: nc.dram_tensor(name, a.shape, mybir.dt.from_np(a.dtype), kind="ExternalInput").ap()
           for name, a in arrays.items()}
    out = nc.dram_tensor("out", (NB, S, D), F32, kind="ExternalOutput").ap()
    Kernel(nc, ins, out).build()
    return run_bass_kernel_spmd(nc, [arrays], core_ids=[0]).results[0]["out"]
```

```python
from contextlib import ExitStack

import concourse.bass as bass
from concourse import mybir

F32 = mybir.dt.float32
F32R = mybir.dt.float32r
F16 = mybir.dt.float16
BF16 = mybir.dt.bfloat16
U32 = mybir.dt.uint32
ALU = mybir.AluOpType
ACT = mybir.ActivationFunctionType
AX = mybir.AxisListType

P = 128
NB, S, D = 16, 256, 256
TT = S // P
KD = D // P
L = 77
G, HD = 16, 16
UG = 8
NE0, NS0, H0 = 16, 16, 64
SLOTS = NE0 * NS0
FF = 1024
FC = FF // P
NE1, H1 = 8, 192
SH = 384
HC = (NE1 * H1 + SH) // P
EC = NE1 * H1 // P
TB = 512
NBLK = NB * S // TB
BT = TB // P
LN_EPS = 1e-5
L2_EPS = 1e-12


class Signal:

    def __init__(self, sem, per=1, step=1):
        self.sem, self.per, self.step = sem, per, step


def need(eng, sig, b, count=None):
    count = sig.per if count is None else count
    eng.wait_ge(sig.sem, (b * sig.per + count) * sig.step)


def alone(eng):
    eng.nop(nofuse=True)


def reuse(eng, sig, b, count=None):
    if isinstance(b, int) and b == 0:
        return
    count = sig.per if count is None else count
    eng.wait_ge(sig.sem, (b * sig.per + (count - sig.per)) * sig.step)


def at(tensor, b):
    if isinstance(b, int):
        return tensor[:, b]
    part = tensor[:, bass.ds(b, 1)]
    names = " ".join("wxyz"[: len(part.shape) - 2])
    first = names.split()[0]
    return part.rearrange(f"p a {names} -> p (a {first}) {names[2:]}")


def reuse2(eng, sig, b, count=None):
    if isinstance(b, int) and b < 2:
        return
    count = sig.per if count is None else count
    eng.wait_ge(sig.sem, (b * sig.per + (count - 2 * sig.per)) * sig.step)


def run(eng, order, steps, n):
    behind = max(step[0] for step in order)

    def turn(first):
        for stage, name, *part in order:
            b = first - stage
            if name in steps and not (isinstance(b, int) and (b < 0 or b >= n)):
                steps[name](b, *part)

    for t in range(behind + 1):
        turn(t)
    with eng.Fori(behind, n - 1) as i:
        turn(i + 1)
    for t in range(n, n + behind):
        turn(t)


def turns(eng, schedule, n):
    schedule(0, None)
    schedule(1, 0)
    with eng.Fori(1, n - 1) as i:
        schedule(i + 1, i)
    schedule(None, n - 1)


class Kernel:
    def __init__(self, nc, ins, out, stop=None):
        self.nc, self.ins, self.out, self.stop = nc, ins, out, stop
        self.used = []

    def sb(self, ctx, name, shape, dt=F32):
        return ctx.enter_context(self.nc.sbuf_tensor(name, shape, dt))

    def ps(self, ctx, name, shape, dt=F32):
        return ctx.enter_context(self.nc.psum_tensor(name, shape, dt))

    def sig(self, ctx, name, per=1, step=1):
        sem = ctx.enter_context(self.nc.semaphore(name))
        self.used.append(sem.num)
        return Signal(sem, per, step)

    def clear_signals(self):
        used, self.used = sorted(set(self.used)), []
        starts = [n for n in used if n - 1 not in used]
        ends = [n + 1 for n in used if n + 1 not in used]
        with self.nc.Block() as block:
            @block.gpsimd
            def _(pool):
                for a, b in zip(starts, ends):
                    pool.sem_clear(range(a, b))

    def build(self):
        nc = self.nc
        self.routes = nc.dram_tensor("routes", [NE1 * BT, P], F32, kind="Internal").ap()
        with ExitStack() as whole:
            self.X = self.sb(whole, "x_all", [P, NB, TT, D])
            self.ident = self.sb(whole, "ident", [P, P])
            self.gates = self.sb(whole, "gates", [P, 4])
            self.minus_half = self.sb(whole, "minus_half", [P, 4])
            with ExitStack() as moe:
                self.CT = self.sb(moe, "combineT_all", [P, NB, TT, S])
                self.SL = self.sb(moe, "slots_all", [P, KD, NB, SLOTS])
                self.rcomb = self.sb(moe, "combine_scale_all", [P, NB, TT])
                with ExitStack() as c:
                    self.phase_a(c)
                if self.stop == "a":
                    return self.dump(self.X)
                self.clear_signals()
                with ExitStack() as c:
                    self.phase_b(c)
                if self.stop == "b":
                    return self.dump(self.X)
                with ExitStack() as c:
                    self.phase_c(c)
                if self.stop == "c":
                    return self.dump(self.X)
            self.clear_signals()
            with ExitStack() as c:
                self.phase_d(c)

    def dump(self, X):
        with ExitStack() as c:
            done = self.sig(c, "dumped", 1, 16)
            block = c.enter_context(self.nc.Block())

            @block.sync
            def _(sp):
                sp.dma_start(self.out.rearrange("b (t p) d -> p b t d", p=P), X[:]).then_inc(done.sem, 16)
                sp.wait_ge(done.sem, 16)

    def phase_a(self, c):
        nc, ins = self.nc, self.ins
        X, CT, SL, ident = self.X, self.CT, self.SL, self.ident
        sb = lambda n, s, d=F32: self.sb(c, n, s, d)
        sig = lambda n, per=1, step=1: self.sig(c, n, per, step)

        wq = sb("wq", [P, KD, D])
        wk = sb("wk", [P, KD, P])
        wv = sb("wv", [P, KD, P])
        bq = sb("bq", [P, KD])
        bk = sb("bk", [P, 1])
        bvt = sb("bv_gated", [P, G, HD])
        scale0 = sb("scale0", [P, 1])
        gam0 = sb("gamma0", [P, D])
        bet0 = sb("beta0", [P, D])
        ones = sb("ones", [P, P])
        gmask = sb("group_mask", [P, UG])
        mu = sb("mu", [P, KD, SLOTS])
        mu_sq = sb("mu_sq", [P, KD, SLOTS])
        mu_ss = sb("mu_ss", [P, KD])
        mu_rn = sb("mu_rn", [P, KD])
        mu_diag = sb("mu_diag", [P, KD, P])
        mu_unit = sb("mu_unit", [P, KD, SLOTS])
        ctxT = sb("ctx_turned", [P, KD, P])
        kblock = sb("kblock", [P, UG, L])
        vpart = sb("vpart_all", [L, NB, 3, HD + 1], BF16)
        vres = sb("vres", [L, 3, HD])
        z = sb("z", [P, TT, D])
        zT = sb("zT", [P, KD, S])
        qT = sb("qT", [P, KD, S])
        mx = sb("mx", [P, UG])
        prob = sb("prob", [P, 2, UG, L])
        prob2 = sb("prob_lo_hi", [P, 2, UG, L, 2], F16)
        probT = sb("probT", [L, G, G, G], U32)
        osum = sb("osum", [P, TT, G, HD + 1])
        orec = sb("orec", [P, TT, G])
        oprod = sb("oprod", [P, TT, G, HD])
        mv1 = sb("mv1", [P, TT, 2])
        bs1 = sb("bs1", [P, TT, 6])
        rs1 = sb("rs1", [P, TT])
        bs2 = sb("bs2", [P, TT, 6])
        mv2 = sb("mv2", [P, TT, 2])
        rs2 = sb("rs2", [P, TT])
        xg = sb("xg", [P, TT, D])
        xn = sb("xn", [P, TT, D])
        sq = sb("sq", [P, TT, D])
        ss = sb("ss", [P, TT])
        ru = sb("ru", [P, TT])
        xu = sb("xu", [P, TT, D])
        xuT = sb("xuT", [P, KD, S])
        negmax = sb("negmax", [P, 2, TT])
        esum = sb("esum", [P, 2, TT])
        erec = sb("erec", [P, 2, TT])
        comb = sb("comb", [P, TT, SLOTS])
        dispT = sb("dispT", [P, TT, S])
        disp = sb("disp", [P, TT, SLOTS])

        psA = self.ps(c, "ps_small_a", [P, 512])
        psS = self.ps(c, "ps_scores", [P, 2, 512])
        psT = self.ps(c, "ps_probT", [P, UG, P])
        psB = psT[:, UG // 2:UG, :].rearrange("p g q -> p (g q)")
        psR = self.ps(c, "ps_turned", [P, 512])
        psL = self.ps(c, "ps_logits", [P, 2, 256])
        psM = self.ps(c, "ps_logitsT", [P, 2, 256])

        const_in = sig("const_in", 1, 16)
        x_in, ctx_in = sig("x_in", 1, 16), sig("ctx_in", 1, 16)
        filled, id_done, gate_done, bv_done = sig("filled"), sig("id_done"), sig("gate_done"), sig("bv_done")
        mu_sq_done, mu_ss_mm, mu_ss_ev, mu_rn_done = sig("mu_sq_done"), sig("mu_ss_mm"), sig("mu_ss_ev"), sig("mu_rn_done")
        mu_diag_done, mu_bc_mm, mu_done = sig("mu_diag_done"), sig("mu_bc_mm"), sig("mu_done")
        v_out, kv_mm, kb_done, v_step = sig("v_out"), sig("kv_mm"), sig("kb_done"), sig("v_step", 5)
        st1, mv1_done, rs1_step, z_done = sig("st1"), sig("mv1_done"), sig("rs1_step", 2), sig("z_done")
        zt_mm, zt_ev, q_mm, q_ev = sig("zt_mm"), sig("zt_ev"), sig("q_mm"), sig("q_ev")
        sc_mm, mx_done, sub_done, exp_done = sig("sc_mm", 4), sig("mx_done", 4), sig("sub_done", 4), sig("exp_done", 4)
        hi_done, lo_done, pt_mm, pt_ev = sig("hi_done", 4), sig("lo_done", 4), sig("pt_mm", 4), sig("pt_ev", 4)
        pv_mm, osum_done = sig("pv_mm", 4), sig("osum_done", 4)
        xb_done, o_step, x1_done = sig("xb_done"), sig("o_step", 2), sig("x1_done")
        st2, mv2_done, rs2_step, xg_done, xn_done = sig("st2"), sig("mv2_done"), sig("rs2_step", 2), sig("xg_done"), sig("xn_done")
        ss_done, ru_step, xu_done = sig("ss_done"), sig("ru_step", 2), sig("xu_done")
        xut_mm, xut_ev, lg_mm, lt_mm = sig("xut_mm"), sig("xut_ev"), sig("lg_mm"), sig("lt_mm")
        nm_done, ce_done, de_done = sig("nm_done", 2), sig("ce_done"), sig("de_done")
        rec_done, dn_done = sig("rec_done", 2), sig("dn_done")
        ct_mm, ct_ev, dt_mm, dt_ev, sl_mm, sl_ev = sig("ct_mm"), sig("ct_ev"), sig("dt_mm"), sig("dt_ev"), sig("sl_mm"), sig("sl_ev")

        row = lambda ap, n: spread(ap.rearrange("(a d) -> a d", a=1), 0, n)
        const_loads = [
            (wq[:], ins["L0_xattn_Wq"].rearrange("(k p) f -> p k f", p=P)),
            (wk[:], ins["wk8"].rearrange("(k p) f -> p k f", p=P)),
            (wv[:, :, 0:HD], ins["L0_xattn_Wv"].rearrange("(k p) f -> p k f", p=P)),
            (bq[:], ins["bq_cols"]),
            (bk[:], ins["bk8"].rearrange("(p a) -> p a", a=1)),
            (bvt[:], spread(spread(ins["L0_xattn_bv"].rearrange("(a b d) -> a b d", a=1, b=1), 0, P), 1, G)),
            (scale0[:], row(ins["L0_ffn_scale"], P)),
            (gam0[:], row(ins["L0_ffn_ln_gamma"], P)),
            (bet0[:], row(ins["L0_ffn_ln_beta"], P)),
            (self.gates[:, 0:2], row(ins["g_xattn"], P)),
            (self.gates[:, 2:4], row(ins["g_ffn"], P)),
            (mu[:], ins["L0_ffn_mu"].rearrange("(k p) e s -> p k (e s)", p=P)),
        ]
        block = c.enter_context(nc.Block())
        PRE, MID, OUT, MIX = range(4)

        def unit_steps(u):
            return [(MID, "scores_out", u), (MID, "exps", u), (MID, "high_part", u), (MID, "low_part", u)]

        order = [(PRE, "ln1_stats"), (MID, "scores", 0), (OUT, "values", 0), (OUT, "values", 1),
                 (MID, "scores_out", 0), (OUT, "out_sum", 0), (PRE, "rstd1"), (MIX, "turn_xu"), (PRE, "ln1_apply"),
                 (MID, "scores", 1), (OUT, "values", 2), (OUT, "out_sum", 1), (OUT, "values", 3), (MID, "exps", 0),
                 (MID, "scores_out", 1), (MID, "high_part", 0), (OUT, "out_sum", 2), (MIX, "xuT_out"),
                 (MID, "exps", 1), (OUT, "out_sum", 3), (MID, "low_part", 0), (MID, "scores", 2), (OUT, "x1"),
                 (MID, "turn_p", 0), (MID, "scores_out", 2), (MID, "high_part", 1), (MID, "probT_out", 0),
                 (MID, "exps", 2), (MIX, "logits"), (MID, "high_part", 2), (MID, "scores", 3), (MIX, "neg_max"),
                 (MID, "low_part", 1), (MIX, "combine"), (MID, "turn_p", 1), (MID, "scores_out", 3),
                 (MID, "probT_out", 1), (PRE, "kv"), (MID, "low_part", 2), (MIX, "turn_comb"), (MIX, "dispatch"),
                 (MIX, "combineT_out"), (MIX, "normalise"), (MID, "exps", 3), (PRE, "v_move"), (MID, "high_part", 3),
                 (MID, "low_part", 3), (PRE, "add_bv"), (MID, "turn_p", 2), (MIX, "turn_disp"), (PRE, "kv_out"),
                 (PRE, "turn_z"), (MID, "probT_out", 2), (OUT, "ln2_stats"), (OUT, "rstd2"), (MID, "turn_p", 3),
                 (MIX, "disp_out"), (MIX, "slot_inputs"), (MID, "probT_out", 3), (OUT, "ln2_apply"), (PRE, "zT_out"),
                 (MIX, "slots_out"), (OUT, "squares"), (PRE, "queries"), (OUT, "runit"), (PRE, "q_out"),
                 (OUT, "unit"), (PRE, "v_parts")]

        @block.sync
        def _(sp):
            def load_x(b):
                sp.dma_start(at(X, b), ins["x"].rearrange("b (t p) d -> p b t d", p=P)[:, b] if isinstance(b, int)
                             else at(ins["x"].rearrange("b (t p) d -> p b t d", p=P), b)).then_inc(x_in.sem, 16)

            def load_ctx(b):
                reuse(sp, kv_mm, b)
                src = ins["ctxT"].rearrange("b (k p) l -> p b k l", p=P)
                sp.dma_start(ctxT[:, :, 0:L], at(src, b)).then_inc(ctx_in.sem, 16)

            load_x(0)
            sp.wait_ge(filled.sem, 1)
            load_ctx(0)
            for dst, src in const_loads:
                sp.dma_start(dst, src).then_inc(const_in.sem, 16)
            with sp.Fori(1, NB) as b:
                sp.wait_ge(x_in.sem, b * 16)
                load_x(b)
                load_ctx(b)

        all_const = 16 * len(const_loads)

        @block.gpsimd
        def _(pool):
            pool.memset(ident[:], 0.0)
            pool.memset(gmask[:], 1.0)
            pool.memset(ones[:], 1.0)
            pool.memset(self.minus_half[:], -0.5)
            pool.memset(wv[:, :, HD:P], 0.0)
            pool.memset(vpart[:, :, 0, HD:HD + 1], 1.0)
            pool.memset(vpart[:, :, 1:3, HD:HD + 1], 0.0)
            pool.memset(ctxT[:], 0.0).then_inc(filled.sem, 1)
            pool.wait_ge(filled.sem, 1)
            pool.affine_select(out=ident[:], in_=ident[:], compare_op=ALU.not_equal, fill=1.0, base=0,
                               pattern=[[-1, P]], channel_multiplier=1).then_inc(id_done.sem, 1)
            pool.affine_select(out=gmask[:], in_=gmask[:], compare_op=ALU.is_ge, fill=0.0, base=0,
                               pattern=[[-HD, UG]], channel_multiplier=1).then_inc(id_done.sem, 1)
            pool.wait_ge(id_done.sem, 2)
            pool.affine_select(out=gmask[:], in_=gmask[:], compare_op=ALU.is_ge, fill=0.0, base=HD - 1,
                               pattern=[[HD, UG]], channel_multiplier=-1).then_inc(id_done.sem, 1)
            pool.wait_ge(mu_ss_ev.sem, 1)
            pool.tensor_tensor(mu_rn[:], mu_ss[:], self.minus_half[:, 0:KD], ALU.pow).then_inc(mu_rn_done.sem, 1)
            pool.wait_ge(gate_done.sem, 1)
            alone(pool)
            pool.tensor_scalar(bvt[:], bvt[:], self.gates[:, 0:1], None, ALU.mult).then_inc(bv_done.sem, 1)
            pool.wait_ge(bv_done.sem, 1)

            def rstd1(b):
                need(pool, mv1_done, b)
                alone(pool)
                pool.tensor_scalar(rs1[:], mv1[:, :, 1], LN_EPS, None, ALU.add).then_inc(rs1_step.sem, 1)
                need(pool, rs1_step, b, 1)
                pool.tensor_tensor(rs1[:], rs1[:], self.minus_half[:, 0:TT], ALU.pow).then_inc(rs1_step.sem, 1)

            def add_bv(b):
                need(pool, z_done, b)
                alone(pool)
                pool.tensor_tensor(at(X, b), at(X, b), spread(bvt[:].rearrange("p (a g) d -> p a (g d)", a=1), 1, TT),
                                   ALU.add).then_inc(xb_done.sem, 1)

            def low_part(b, u):
                need(pool, hi_done, b, u + 1)
                pool.tensor_tensor(prob2[:, u % 2, :, :, 0], prob[:, u % 2], prob2[:, u % 2, :, :, 1],
                                   ALU.subtract).then_inc(lo_done.sem, 1)

            def v_parts(b):
                v = at(vpart, b)
                need(pool, v_out, b)
                alone(pool)
                pool.tensor_copy(v[:, 0, 0:HD], vres[:, 0, :]).then_inc(v_step.sem, 1)
                need(pool, v_step, b, 1)
                alone(pool)
                pool.tensor_tensor(vres[:, 1, :], vres[:, 0, :], v[:, 0, 0:HD], ALU.subtract).then_inc(v_step.sem, 1)
                need(pool, v_step, b, 2)
                alone(pool)
                pool.tensor_copy(v[:, 1, 0:HD], vres[:, 1, :]).then_inc(v_step.sem, 1)
                need(pool, v_step, b, 3)
                alone(pool)
                pool.tensor_tensor(vres[:, 2, :], vres[:, 1, :], v[:, 1, 0:HD], ALU.subtract).then_inc(v_step.sem, 1)
                need(pool, v_step, b, 4)
                alone(pool)
                pool.tensor_copy(v[:, 2, 0:HD], vres[:, 2, :]).then_inc(v_step.sem, 1)

            def rstd2(b):
                need(pool, mv2_done, b)
                alone(pool)
                pool.tensor_scalar(rs2[:], mv2[:, :, 1], 1.0 + LN_EPS, LN_EPS * LN_EPS, ALU.mult, ALU.add)\
                    .then_inc(rs2_step.sem, 1)
                need(pool, rs2_step, b, 1)
                pool.tensor_tensor(rs2[:], rs2[:], self.minus_half[:, 0:TT], ALU.pow).then_inc(rs2_step.sem, 1)

            def runit(b):
                need(pool, ss_done, b)
                reuse(pool, xu_done, b)
                alone(pool)
                pool.tensor_scalar(ru[:], ss[:], L2_EPS * L2_EPS, None, ALU.max).then_inc(ru_step.sem, 1)
                need(pool, ru_step, b, 1)
                pool.tensor_tensor(ru[:], ru[:], self.minus_half[:, 0:TT], ALU.pow).then_inc(ru_step.sem, 1)

            run(pool, order, dict(rstd1=rstd1, add_bv=add_bv, low_part=low_part, v_parts=v_parts, rstd2=rstd2, runit=runit), NB)

        @block.scalar
        def _(act):
            act.wait_ge(const_in.sem, all_const)
            act.activation(self.gates[:], self.gates[:], ACT.Tanh).then_inc(gate_done.sem, 1)

            def zT_out(b):
                need(act, zt_mm, b)
                reuse(act, q_mm, b)
                act.copy(zT[:].rearrange("p k s -> p (k s)"), psA[:]).then_inc(zt_ev.sem, 1)

            def q_out(b):
                need(act, q_mm, b)
                reuse(act, sc_mm, b)
                for k in range(KD):
                    ins_ = act.activation(qT[:, k, :], psB[:, k * S:(k + 1) * S], ACT.Identity, bias=bq[:, k:k + 1])
                ins_.then_inc(q_ev.sem, 1)

            def v_move(b):
                need(act, kv_mm, b)
                reuse(act, v_step, b)
                act.copy(vres[:, 0, :], psA[0:L, P:P + HD]).then_inc(v_out.sem, 1)

            def high_part(b, u):
                need(act, exp_done, b, u + 1)
                if u < 2:
                    reuse(act, pt_mm, b, 3 + u)
                else:
                    need(act, pt_mm, b, u - 1)
                act.copy(prob2[:, u % 2, :, :, 1], prob[:, u % 2]).then_inc(hi_done.sem, 1)

            def exps(b, u):
                need(act, sub_done, b, u + 1)
                act.activation(prob[:, u % 2], prob[:, u % 2], ACT.Exp, scale=float(D) ** -0.5).then_inc(exp_done.sem, 1)

            def squares(b):
                need(act, xn_done, b)
                reuse(act, ss_done, b)
                reuse(act, ru_step, b, 1)
                for t in range(TT):
                    ins_ = act.activation(sq[:, t, :], xn[:, t, :], ACT.Square, accum_out=ss[:, t:t + 1])
                ins_.then_inc(ss_done.sem, 1)

            def xuT_out(b):
                need(act, xut_mm, b)
                reuse(act, lt_mm, b)
                act.copy(xuT[:].rearrange("p k s -> p (k s)"), psR[:]).then_inc(xut_ev.sem, 1)

            def combine(b):
                need(act, nm_done, b, 1)
                reuse(act, ct_mm, b)
                reuse(act, rec_done, b, 1)
                for t in range(TT):
                    ins_ = act.activation(comb[:, t, :], psL[:, t, :], ACT.Exp, bias=negmax[:, 0, t:t + 1],
                                          accum_out=esum[:, 0, t:t + 1])
                ins_.then_inc(ce_done.sem, 1)

            def dispatch(b):
                need(act, nm_done, b, 2)
                reuse(act, dt_mm, b)
                reuse(act, rec_done, b, 2)
                for t in range(TT):
                    ins_ = act.activation(dispT[:, t, :], psM[:, t, :], ACT.Exp, bias=negmax[:, 1, t:t + 1],
                                          accum_out=esum[:, 1, t:t + 1])
                ins_.then_inc(de_done.sem, 1)

            def combineT_out(b):
                need(act, ct_mm, b)
                act.copy(at(CT, b), psR[:].rearrange("p (k s) -> p k s", k=TT)).then_inc(ct_ev.sem, 1)

            def disp_out(b):
                need(act, dt_mm, b)
                reuse(act, sl_mm, b)
                act.copy(disp[:].rearrange("p k s -> p (k s)"), psR[:]).then_inc(dt_ev.sem, 1)

            def slots_out(b):
                need(act, sl_mm, b)
                for k in range(KD):
                    dst = SL[:, k, b, :] if isinstance(b, int) else SL[:, k, bass.ds(b, 1), :].rearrange("p a s -> p (a s)")
                    ins_ = act.copy(dst, psL[:, k, :])
                ins_.then_inc(sl_ev.sem, 1)

            run(act, order, dict(v_move=v_move, zT_out=zT_out, q_out=q_out, exps=exps, high_part=high_part, squares=squares,
                                 xuT_out=xuT_out, combine=combine, dispatch=dispatch, combineT_out=combineT_out,
                                 disp_out=disp_out, slots_out=slots_out), NB)

        @block.vector
        def _(dve):
            dve.wait_ge(const_in.sem, all_const)
            dve.tensor_tensor(mu_sq[:], mu[:], mu[:], ALU.mult).then_inc(mu_sq_done.sem, 1)
            dve.wait_ge(mu_ss_mm.sem, 1)
            dve.tensor_scalar(mu_ss[:], psA[:].rearrange("p (k s) -> p k s", k=KD)[:, :, 0], L2_EPS * L2_EPS, None, ALU.max)\
               .then_inc(mu_ss_ev.sem, 1)
            dve.wait_ge(mu_rn_done.sem, 1)
            dve.wait_ge(id_done.sem, 3)
            for k in range(KD):
                last = dve.tensor_scalar(mu_diag[:, k, :], ident[:], mu_rn[:, k:k + 1], None, ALU.mult)
            last.then_inc(mu_diag_done.sem, 1)
            dve.wait_ge(mu_bc_mm.sem, 1)
            dve.tensor_tensor(mu_unit[:], mu[:], spread(psB[:, 0:SLOTS].rearrange("p (a s) -> p a s", a=1), 1, KD), ALU.mult)\
               .then_inc(mu_done.sem, 1)

            def kv_out(b):
                need(dve, kv_mm, b)
                need(dve, v_out, b)
                reuse(dve, sc_mm, b)
                dve.scalar_tensor_tensor(out=kblock[:], in0=spread(psA[:, 0:L].rearrange("p (a l) -> p a l", a=1), 1, UG),
                                         scalar=bk[:, 0:1], in1=spread(gmask[:].rearrange("p (g a) -> p g a", a=1), 2, L),
                                         op0=ALU.add, op1=ALU.mult).then_inc(kb_done.sem, 1)

            def stats(b, src, bs, mv, st, done, readers):
                reuse(dve, readers, b)
                alone(dve)
                for t in range(TT):
                    last = dve.bn_stats(bs[:, t, :], src[:, t, :])
                last.then_inc(st.sem, 1)
                need(dve, st, b)
                alone(dve)
                for t in range(TT):
                    last = dve.bn_aggr(mv[:, t, :], bs[:, t, :])
                last.then_inc(done.sem, 1)

            def ln1_stats(b):
                need(dve, x_in, b)
                stats(b, at(X, b), bs1, mv1, st1, mv1_done, z_done)

            def ln1_apply(b):
                need(dve, rs1_step, b)
                reuse(dve, zt_mm, b)
                x = at(X, b)
                for t in range(TT):
                    last = dve.tensor_scalar(z[:, t, :], x[:, t, :], mv1[:, t, 0:1], rs1[:, t:t + 1], ALU.subtract, ALU.mult)
                last.then_inc(z_done.sem, 1)

            def scores_out(b, u):
                need(dve, sc_mm, b, u + 1)
                s = psS[:, :, 0:UG // 2 * L].rearrange("p c (g l) -> p c g l", l=L)
                m = mx[:].rearrange("p (c g) -> p c g", c=2)
                dve.tensor_reduce(m, s, AX.X, ALU.max).then_inc(mx_done.sem, 1)
                need(dve, mx_done, b, u + 1)
                if u < 2:
                    reuse(dve, lo_done, b, 3 + u)
                else:
                    need(dve, lo_done, b, u - 1)
                dve.tensor_tensor(prob[:, u % 2].rearrange("p (c g) l -> p c g l", c=2), s,
                                  spread(mx[:].rearrange("p (c g a) -> p c g a", c=2, a=1), 3, L),
                                  ALU.subtract).then_inc(sub_done.sem, 1)

            def probT_out(b, u):
                need(dve, pt_mm, b, u + 1)
                if u == 0:
                    reuse(dve, pv_mm, b)
                tile, g0 = u // 2, (u % 2) * UG
                dst = probT[:, tile * UG:(tile + 1) * UG, :, g0:g0 + UG].rearrange("k h t g -> k (h t) g")
                dve.tensor_copy(dst, psT[0:L].bitcast(U32).rearrange("k g q -> k q g")).then_inc(pt_ev.sem, 1)

            def out_sum(b, w):
                need(dve, pv_mm, b, w + 1)
                bank = (psA, psB)[w % 2]
                dve.tensor_reduce(osum[:, w // 2, (w % 2) * 8:(w % 2) * 8 + 8, :],
                                  bank[:, 0:8 * 3 * (HD + 1)].rearrange("p (h c d) -> p h d c", h=8, c=3),
                                  AX.X, ALU.add).then_inc(osum_done.sem, 1)

            def x1(b):
                need(dve, osum_done, b)
                dve.reciprocal(orec[:], osum[:, :, :, HD]).then_inc(o_step.sem, 1)
                need(dve, o_step, b, 1)
                dve.scalar_tensor_tensor(out=oprod[:].rearrange("p t g d -> p (t g) d"),
                                         in0=osum[:, :, :, 0:HD].rearrange("p t g d -> p (t g) d"), scalar=self.gates[:, 0:1],
                                         in1=spread(orec[:].rearrange("p t (g a) -> p (t g) a", a=1), 2, HD),
                                         op0=ALU.mult, op1=ALU.mult).then_inc(o_step.sem, 1)
                need(dve, o_step, b, 2)
                need(dve, xb_done, b)
                dve.tensor_tensor(at(X, b), at(X, b), oprod[:].rearrange("p t g d -> p t (g d)"), ALU.add).then_inc(x1_done.sem, 1)

            def ln2_stats(b):
                need(dve, x1_done, b)
                stats(b, at(X, b), bs2, mv2, st2, mv2_done, xn_done)

            def ln2_apply(b):
                x = at(X, b)
                need(dve, mv2_done, b)
                for t in range(TT):
                    last = dve.scalar_tensor_tensor(out=xg[:, t, :], in0=x[:, t, :], scalar=mv2[:, t, 0:1], in1=gam0[:],
                                                    op0=ALU.subtract, op1=ALU.mult)
                last.then_inc(xg_done.sem, 1)
                need(dve, rs2_step, b)
                need(dve, xg_done, b)
                reuse(dve, sl_mm, b)
                reuse(dve, ss_done, b)
                for t in range(TT):
                    last = dve.scalar_tensor_tensor(out=xn[:, t, :], in0=xg[:, t, :], scalar=rs2[:, t:t + 1], in1=bet0[:],
                                                    op0=ALU.mult, op1=ALU.add)
                last.then_inc(xn_done.sem, 1)

            def unit(b):
                need(dve, ru_step, b)
                reuse(dve, xut_mm, b)
                for t in range(TT):
                    last = dve.tensor_scalar(xu[:, t, :], xn[:, t, :], ru[:, t:t + 1], scale0[:, 0:1], ALU.mult, ALU.mult)
                last.then_inc(xu_done.sem, 1)

            def neg_max(b):
                need(dve, lg_mm, b)
                reuse(dve, ce_done, b)
                dve.tensor_reduce(negmax[:, 0, :], psL[:], AX.X, ALU.max, negate=True).then_inc(nm_done.sem, 1)
                need(dve, lt_mm, b)
                reuse(dve, de_done, b)
                dve.tensor_reduce(negmax[:, 1, :], psM[:], AX.X, ALU.max, negate=True).then_inc(nm_done.sem, 1)

            def normalise(b):
                need(dve, ce_done, b)
                dve.reciprocal(erec[:, 0, :], esum[:, 0, :]).then_inc(rec_done.sem, 1)
                need(dve, de_done, b)
                dve.reciprocal(erec[:, 1, :], esum[:, 1, :]).then_inc(rec_done.sem, 1)
                need(dve, rec_done, b)
                dve.tensor_scalar(at2(self.rcomb, b), erec[:, 0, :], self.gates[:, 2:3], None, ALU.mult)
                for t in range(TT):
                    last = dve.tensor_scalar(dispT[:, t, :], dispT[:, t, :], erec[:, 1, t:t + 1], None, ALU.mult)
                last.then_inc(dn_done.sem, 1)

            run(dve, order, dict(kv_out=kv_out, ln1_stats=ln1_stats, ln1_apply=ln1_apply, scores_out=scores_out,
                                 probT_out=probT_out, out_sum=out_sum, x1=x1, ln2_stats=ln2_stats, ln2_apply=ln2_apply,
                                 unit=unit, neg_max=neg_max, normalise=normalise), NB)

        @block.tensor
        def _(pe):
            def mm(out, lhsT, rhs, start=True, stop=True):
                return pe.matmul(out, lhsT, rhs, start=start, stop=stop)

            pe.wait_ge(mu_sq_done.sem, 1)
            for h in range(KD):
                for k in range(KD):
                    last = mm(psA[:, h * 256:h * 256 + P], mu_sq[:, k, h * P:(h + 1) * P], ones[:], k == 0, k == KD - 1)
            last.then_inc(mu_ss_mm.sem, 1)
            pe.wait_ge(mu_diag_done.sem, 1)
            for h in range(KD):
                last = mm(psB[:, h * P:(h + 1) * P], ones[:], mu_diag[:, h, :])
            last.then_inc(mu_bc_mm.sem, 1)
            pe.wait_ge(mu_done.sem, 1)

            def turn4(dst, src):
                for k in range(2):
                    for t in range(2):
                        last = pe.transpose(dst[:, k * S + t * P:k * S + (t + 1) * P], src[:, t, k * P:(k + 1) * P], ident[:])
                return last

            def kv(b):
                need(pe, ctx_in, b)
                reuse2(pe, osum_done, b)
                for k in range(KD):
                    mm(psA[:, 0:P], wk[:, k, :], ctxT[:, k, :], k == 0, k == KD - 1)
                for k in range(KD):
                    last = mm(psA[:, P:2 * P], ctxT[:, k, :], wv[:, k, :], k == 0, k == KD - 1)
                last.then_inc(kv_mm.sem, 1)

            def turn_z(b):
                need(pe, z_done, b)
                need(pe, kb_done, b)
                need(pe, v_out, b)
                turn4(psA, z).then_inc(zt_mm.sem, 1)

            def queries(b):
                need(pe, zt_ev, b)
                reuse(pe, pt_ev, b)
                for m in range(KD):
                    for k in range(KD):
                        last = mm(psB[:, m * S:(m + 1) * S], wq[:, k, m * P:(m + 1) * P], zT[:, k, :], k == 0, k == KD - 1)
                last.then_inc(q_mm.sem, 1)

            def scores(b, u):
                tile, chunk = u // 2, u % 2
                if u == 0:
                    need(pe, q_ev, b)
                    reuse(pe, sub_done, b)
                else:
                    need(pe, sub_done, b, u)
                for h in range(2):
                    last = mm(psS[:, h, 0:UG // 2 * L], qT[:, chunk, tile * P:(tile + 1) * P],
                              kblock[:, h * UG // 2:(h + 1) * UG // 2, :].rearrange("p g l -> p (g l)"))
                last.then_inc(sc_mm.sem, 1)

            def turn_p(b, u):
                need(pe, lo_done, b, u + 1)
                if u == 0:
                    reuse(pe, pt_ev, b)
                    reuse(pe, osum_done, b)
                else:
                    need(pe, pt_ev, b, u)
                pairs = prob2[:, u % 2].rearrange("p g l two -> p g (l two)").bitcast(F32)
                for g in range(UG):
                    last = pe.transpose(psT[0:L, g, :], pairs[:, g, :], ident[:])
                last.then_inc(pt_mm.sem, 1)

            def values(b, w):
                tile, half = w // 2, w % 2
                bank = (psA, psB)[half]
                if w == 0:
                    need(pe, pt_ev, b)
                    need(pe, v_step, b)
                if w >= 2:
                    need(pe, osum_done, b, w - 1)
                both = probT[:].rearrange("k h t g -> k h (t g)").bitcast(F16)\
                               .rearrange("k h (q two) -> k h q two", two=2)
                W = 3 * (HD + 1)
                rhs = at(vpart, b).rearrange("k c d -> k (c d)")
                for h in range(8):
                    for part in (1, 0):
                        last = mm(bank[:, h * W:(h + 1) * W], both[:, half * 8 + h, tile * P:(tile + 1) * P, part], rhs,
                                  part == 1, part == 0)
                last.then_inc(pv_mm.sem, 1)

            def turn_xu(b):
                need(pe, xu_done, b)
                reuse(pe, dt_ev, b)
                turn4(psR, xu).then_inc(xut_mm.sem, 1)

            def logits(b):
                need(pe, xut_ev, b)
                reuse(pe, sl_ev, b)
                for t in range(TT):
                    for k in range(KD):
                        last = mm(psL[:, t, :], xuT[:, k, t * P:(t + 1) * P], mu_unit[:, k, :], k == 0, k == KD - 1)
                last.then_inc(lg_mm.sem, 1)
                reuse(pe, de_done, b)
                for h in range(2):
                    for k in range(KD):
                        last = mm(psM[:, h, :], mu_unit[:, k, h * P:(h + 1) * P], xuT[:, k, :], k == 0, k == KD - 1)
                last.then_inc(lt_mm.sem, 1)

            def turn_comb(b):
                need(pe, ce_done, b)
                turn4(psR, comb).then_inc(ct_mm.sem, 1)

            def turn_disp(b):
                need(pe, dn_done, b)
                need(pe, ct_ev, b)
                turn4(psR, dispT).then_inc(dt_mm.sem, 1)

            def slot_inputs(b):
                need(pe, dt_ev, b)
                need(pe, ce_done, b)
                for k in range(KD):
                    for t in range(TT):
                        last = mm(psL[:, k, :], xn[:, t, k * P:(k + 1) * P], disp[:, t, :], t == 0, t == TT - 1)
                last.then_inc(sl_mm.sem, 1)

            run(pe, order, dict(kv=kv, turn_z=turn_z, queries=queries, scores=scores, turn_p=turn_p, values=values,
                                turn_xu=turn_xu, logits=logits, turn_comb=turn_comb, turn_disp=turn_disp,
                                slot_inputs=slot_inputs), NB)

    def phase_b(self, c):
        nc, ins, SL = self.nc, self.ins, self.SL
        sb = lambda n, s, d=F32: self.sb(c, n, s, d)
        sig = lambda n, per=1, step=1: self.sig(c, n, per, step)
        Q = NE0 // 2
        w1 = sb("e_w1", [P, KD, Q, P])
        w2 = sb("e_w2", [P, Q, D])
        b1 = sb("e_b1", [P, Q])
        b2 = sb("e_b2", [P, KD, NE0])
        hT = [sb(f"e_hT{j}", [P, NB * NS0]) for j in range(2)]
        psH = [self.ps(c, f"ps_hidden{j}", [P, 512]) for j in range(2)]
        psO = [self.ps(c, f"ps_slot_out{j}", [P, KD, NB, NS0]) for j in range(2)]
        w_in, zero_done = sig("e_w_in", 1, 16), sig("e_zero_done")
        h_mm, h_ev, o_mm, o_ev = sig("e_h_mm"), sig("e_h_ev"), sig("e_o_mm"), sig("e_o_ev")
        loads = [(w1[:], ins["w1_pairs"].rearrange("(k p) (q h) -> p k q h", p=P, q=Q)),
                 (w2[:], ins["L0_ffn_w2"].rearrange("(q j) h d -> (j h) q d", j=2)),
                 (b1[:], ins["b1_cols"]), (b2[:], ins["b2_cols"])]
        block = c.enter_context(nc.Block())

        @block.sync
        def _(sp):
            for dst, src in loads:
                sp.dma_start(dst, src).then_inc(w_in.sem, 16)

        @block.scalar
        def _(act):
            act.wait_ge(w_in.sem, 16 * len(loads))
            for e in range(NE0):
                j, rows = e % 2, slice(e % 2 * H0, e % 2 * H0 + H0)
                if e < 2:
                    act.wait_ge(zero_done.sem, 1)
                else:
                    act.wait_ge(o_mm.sem, e - 1)
                act.wait_ge(h_mm.sem, e + 1)
                act.activation(hT[j][rows, :], psH[j][rows, 0:NB * NS0], ACT.Gelu, bias=b1[rows, e // 2:e // 2 + 1])\
                   .then_inc(h_ev.sem, 1)

        @block.vector
        def _(dve):
            dve.memset(hT[0][:], 0.0)
            dve.memset(hT[1][:], 0.0).then_inc(zero_done.sem, 1)
            dve.wait_ge(w_in.sem, 16 * len(loads))
            for e in range(NE0):
                dve.wait_ge(o_mm.sem, e + 1)
                for k in range(KD):
                    last = dve.tensor_scalar(SL[:, k, :, e * NS0:(e + 1) * NS0], psO[e % 2][:, k], b2[:, k, e:e + 1],
                                             None, ALU.add)
                last.then_inc(o_ev.sem, 1)

        @block.tensor
        def _(pe):
            pe.wait_ge(w_in.sem, 16 * len(loads))

            def hidden(e):
                if e >= 2:
                    pe.wait_ge(h_ev.sem, e - 1)
                for k in range(KD):
                    last = pe.matmul(psH[e % 2][:, 0:NB * NS0], w1[:, k, e // 2, :], SL[:, k, :, e * NS0:(e + 1) * NS0],
                                     start=(k == 0), stop=(k == KD - 1))
                last.then_inc(h_mm.sem, 1)

            def outputs(e):
                pe.wait_ge(h_ev.sem, e + 1)
                if e >= 2:
                    pe.wait_ge(o_ev.sem, e - 1)
                for k in range(KD):
                    last = pe.matmul(psO[e % 2][:, k].rearrange("p b s -> p (b s)"), w2[:, e // 2, k * P:(k + 1) * P],
                                     hT[e % 2][:], start=True, stop=True)
                last.then_inc(o_mm.sem, 1)

            hidden(0)
            for e in range(1, NE0):
                hidden(e)
                outputs(e - 1)
            outputs(NE0 - 1)

    def phase_c(self, c):
        nc, ins = self.nc, self.ins
        X, CT, SL, ident = self.X, self.CT, self.SL, self.ident
        sb = lambda n, s, d=F32: self.sb(c, n, s, d)
        sig = lambda n, per=1, step=1: self.sig(c, n, per, step)
        ISQ = float(D) ** -0.5
        YW = D + 2

        w1h, w1l = sb("f_w1_hi", [P, KD, FF], F32R), sb("f_w1_lo", [P, KD, FF], F32R)
        w2h, w2l = sb("f_w2_hi", [P, FC, D], F32R), sb("f_w2_lo", [P, FC, D], F32R)
        wst = sb("f_w_stage", [P, 2, FF])
        fb1 = sb("f_b1", [P, FC])
        rows = sb("f_rows", [P, 7, D])
        cmask = sb("causal", [P, P])
        bias16 = sb("minus_top_score", [P, 1])
        combT = sb("combT", [P, TT, S])
        slT = sb("slT", [P, KD, SLOTS])
        so = sb("so", [P, TT, D])
        ctxT = sb("c_ctxT", [P, KD, P])
        ctx = sb("c_ctx", [L, D])
        y = sb("y", [P, TT, YW])
        yT = sb("yT", [P, KD, S])
        E = sb("sa_exp", [P, 3, P])
        r1, y1 = sb("r1", [P, TT, D]), sb("y1", [P, TT, D])
        y1T = sb("y1T", [P, KD, S])
        pc = sb("ca_prob", [P, TT, L])
        pcT = sb("ca_probT", [L, TT * P])
        r2, y2, y2b = sb("r2", [P, TT, D]), sb("y2", [P, TT, D]), sb("y2b", [P, TT, D])
        y2h, y2l = sb("y2T_hi", [P, KD, S], F32R), sb("y2T_lo", [P, KD, S], F32R)
        hf = sb("f_hidden", [P, 2, 2, S])
        hh, hl = sb("f_hidden_hi", [P, 2, 2, S], F32R), sb("f_hidden_lo", [P, 2, 2, S], F32R)
        r3, y3 = sb("r3", [P, TT, D]), sb("y3", [P, TT, D])
        small = {n: sb(f"c_small_{n}", [P, TT]) for n in ("srec", "cmax", "cbias", "csum", "crec")}
        lns = {}
        for n in ("l3", "la", "lb", "lc"):
            lns[n] = dict(bs=sb(f"bs_{n}", [P, TT, 6]), mv=sb(f"mv_{n}", [P, TT, 2]), rs=sb(f"rs_{n}", [P, TT]),
                          xg=sb(f"xg_{n}", [P, TT, D]) if n != "l3" else None,
                          st=sig(f"st_{n}"), mvd=sig(f"mvd_{n}"), rss=sig(f"rss_{n}", 2), xgd=sig(f"xgd_{n}"),
                          done=sig(f"done_{n}"))

        psT = self.ps(c, "c_turned", [P, 512])
        psO = self.ps(c, "c_out", [P, 512])
        psS = self.ps(c, "c_scores", [P, 512])
        psT2 = self.ps(c, "c_turned2", [P, 512])
        psC = self.ps(c, "c_cross", [P, 512])
        psH = self.ps(c, "c_hidden", [P, 2, 2, S])
        psF = self.ps(c, "c_mlp", [P, TT, D])

        const_in, rows_done = sig("f_const_in", 1, 16), sig("f_mask_done")
        bias_done = sig("top_score_done")
        wst_in, wh_done, wl_done = sig("wst_in", 1, 16), sig("wh_done"), sig("wl_done")
        load_in = sig("c_load_in", 2, 16)
        ctx_in = sig("c_ctx_in", 2, 16)
        so_mm, so_ev, mix_mm, x2_done = sig("so_mm"), sig("so_ev"), sig("mix_mm"), sig("x2_done")
        yt_mm, yt_ev, sa_mm, sa_exp, sa_mask = sig("yt_mm"), sig("yt_ev"), sig("sa_mm"), sig("sa_exp_done"), sig("sa_mask")
        sao_mm, srec_done, r1_done = sig("sao_mm"), sig("srec_done"), sig("r1_done")
        y1t_mm, y1t_ev, ca_mm, cm_done, ca_exp = sig("y1t_mm"), sig("y1t_ev"), sig("ca_mm"), sig("cm_done", 2), sig("ca_exp")
        pct_mm, pct_ev, cao_mm, crec_done, r2_done = sig("pct_mm"), sig("pct_ev"), sig("cao_mm"), sig("crec_done"), sig("r2_done")
        y2b_done, y2t_mm, y2h_ev, y2l_ev = sig("y2b_done"), sig("y2t_mm"), sig("y2h_ev"), sig("y2l_ev")
        h_mm, h_ev, hh_done, hl_done, f2_mm = sig("c_h_mm", 4), sig("c_h_ev", 4), sig("hh_done", 4), sig("hl_done", 4), sig("f2_mm", 4)
        r3_done, x3_done = sig("r3_done"), sig("x3_done")

        row = lambda ap: spread(ap.rearrange("(a d) -> a d", a=1), 0, P)
        names = ["L1_xattn_g1", "L1_xattn_beta1", "L1_xattn_g2", "L1_xattn_beta2", "L1_xattn_g3", "L1_xattn_beta3", "L1_xattn_b2"]
        const_loads = [(rows[:, n, :], row(ins[name])) for n, name in enumerate(names)] + [(fb1[:], ins["fb1_cols"])]
        w1v = ins["L1_xattn_w1"].rearrange("(k p) f -> p k f", p=P)
        w2v = ins["L1_xattn_w2"].rearrange("(c p) d -> p c d", p=P)
        stages = [(w1v[:, 0], w1h[:, 0], w1l[:, 0]), (w1v[:, 1], w1h[:, 1], w1l[:, 1]),
                  (w2v[:, 0:4], w2h[:, 0:4], w2l[:, 0:4]), (w2v[:, 4:8], w2h[:, 4:8], w2l[:, 4:8])]

        def stage(n, src):
            view = wst[:, n % 2]
            return view.rearrange("p (c d) -> p c d", d=D) if len(src.shape) == 3 else view

        SELF, CROSS, MLP, LAST = range(4)
        order = [(MLP, "turn_y2"), (SELF, "slot_outputs"), (MLP, "y2_hi"), (SELF, "so_out"), (MLP, "y2_lo"),
                 (MLP, "mlp_in", 0), (SELF, "mix"), (CROSS, "y1_apply"), (MLP, "hidden_out", 0), (LAST, "residual3"),
                 (SELF, "x2"), (CROSS, "turn_y1"), (MLP, "hidden_hi", 0), (MLP, "mlp_in", 1), (MLP, "hidden_lo", 0),
                 (CROSS, "y1T_out"), (MLP, "hidden_out", 1), (CROSS, "ca_scores"), (LAST, "rstd_c"),
                 (CROSS, "ca_max"), (MLP, "mlp_out", 0), (CROSS, "ca_exps"), (CROSS, "turn_pc"), (MLP, "mlp_in", 2),
                 (SELF, "rstd3"), (CROSS, "pcT_out"), (LAST, "y3_apply"), (MLP, "hidden_hi", 1),
                 (MLP, "hidden_out", 2), (SELF, "y0"), (CROSS, "ca_out"), (SELF, "turn_y"), (MLP, "hidden_lo", 1),
                 (MLP, "y2_bias"), (SELF, "yT_out"), (MLP, "mlp_out", 1), (MLP, "mlp_in", 3), (LAST, "x3"),
                 (MLP, "hidden_out", 3), (CROSS, "residual2"), (MLP, "hidden_hi", 2), (SELF, "sa_scores"),
                 (SELF, "sa_exps"), (MLP, "hidden_lo", 2), (CROSS, "rstd_b"), (CROSS, "y2_apply"), (SELF, "mask"),
                 (MLP, "mlp_out", 2), (MLP, "hidden_hi", 3), (MLP, "hidden_lo", 3), (SELF, "sa_out"),
                 (SELF, "residual1"), (MLP, "mlp_out", 3), (SELF, "rstd_a")]
        block = c.enter_context(nc.Block())

        @block.sync
        def _(sp):
            def load(b):
                reuse(sp, mix_mm, b)
                sp.dma_start(combT[:], at(CT, b)).then_inc(load_in.sem, 16)
                if isinstance(b, int):
                    src = SL[:, :, b, :]
                else:
                    src = SL[:, :, bass.ds(b, 1), :].rearrange("p k a s -> p k (a s)")
                sp.dma_start(slT[:], src).then_inc(load_in.sem, 16)

            def load_ctx(b):
                reuse(sp, cao_mm, b)
                sp.dma_start(ctxT[:, :, 0:L], at(ins["ctxT"].rearrange("b (k p) l -> p b k l", p=P), b)).then_inc(ctx_in.sem, 16)
                sp.dma_start(ctx[:], at2(ins["ctx_1024"].rearrange("b l d -> l b d"), b)).then_inc(ctx_in.sem, 16)

            load(0)
            sp.wait_ge(rows_done.sem, 1)
            load_ctx(0)
            for dst, src in const_loads:
                sp.dma_start(dst, src).then_inc(const_in.sem, 16)
            for n, (src, _, _) in enumerate(stages):
                if n >= 2:
                    sp.wait_ge(wl_done.sem, n - 1)
                if n >= 1:
                    sp.wait_ge(wst_in.sem, 16 * n)
                sp.dma_start(stage(n, src), src).then_inc(wst_in.sem, 16)
            load(1)
            with sp.Fori(1, NB - 1) as b:
                load_ctx(b)
                load(b + 1)
            load_ctx(NB - 1)

        all_const = 16 * len(const_loads)

        @block.gpsimd
        def _(pool):
            pool.memset(cmask[:], 1.0)
            pool.memset(y[:, :, D:D + 1], 1.0)
            pool.memset(y[:, :, D + 1:YW], 0.0)
            pool.memset(ctxT[:], 0.0).then_inc(rows_done.sem, 1)
            pool.wait_ge(rows_done.sem, 1)
            pool.affine_select(out=cmask[:], in_=cmask[:], compare_op=ALU.is_ge, fill=0.0, base=0,
                               pattern=[[1, P]], channel_multiplier=-1).then_inc(rows_done.sem, 1)
            for n, (src, hi, lo) in enumerate(stages):
                pool.wait_ge(wst_in.sem, 16 * (n + 1))
                alone(pool)
                pool.tensor_copy(hi, stage(n, src)).then_inc(wh_done.sem, 1)
                pool.wait_ge(wh_done.sem, n + 1)
                pool.tensor_tensor(lo, stage(n, src), hi.bitcast(F32), ALU.subtract).then_inc(wl_done.sem, 1)
            pool.wait_ge(const_in.sem, all_const)

            def rstd(name, b):
                l = lns[name]
                need(pool, l["mvd"], b)
                alone(pool)
                pool.tensor_scalar(l["rs"][:], l["mv"][:, :, 1], LN_EPS, None, ALU.add).then_inc(l["rss"].sem, 1)
                need(pool, l["rss"], b, 1)
                pool.tensor_tensor(l["rs"][:], l["rs"][:], self.minus_half[:, 0:TT], ALU.pow).then_inc(l["rss"].sem, 1)

            def y2_bias(b):
                need(pool, lns["lb"]["done"], b)
                reuse(pool, r3_done, b)
                pool.tensor_tensor(y2b[:], y2[:], spread(rows[:, 6:7, :], 1, TT), ALU.add).then_inc(y2b_done.sem, 1)

            def hidden_hi(b, q):
                need(pool, h_ev, b, q + 1)
                if q < 2:
                    reuse(pool, f2_mm, b, q + 3)
                else:
                    need(pool, f2_mm, b, q - 1)
                alone(pool)
                pool.tensor_copy(hh[:, q % 2], hf[:, q % 2]).then_inc(hh_done.sem, 1)

            run(pool, order, dict(rstd3=lambda b: rstd("l3", b), rstd_a=lambda b: rstd("la", b), rstd_b=lambda b: rstd("lb", b),
                                  rstd_c=lambda b: rstd("lc", b), y2_bias=y2_bias, hidden_hi=hidden_hi), NB)

        @block.scalar
        def _(act):
            act.wait_ge(const_in.sem, all_const)
            act.wait_ge(bias_done.sem, 1)

            flat = lambda t_: t_[:].rearrange("p k s -> p (k s)")

            def so_out(b):
                need(act, so_mm, b)
                reuse(act, mix_mm, b)
                act.copy(flat(so), psT[:]).then_inc(so_ev.sem, 1)

            def yT_out(b):
                need(act, yt_mm, b)
                reuse(act, sa_mm, b)
                act.copy(flat(yT), psT[:]).then_inc(yt_ev.sem, 1)

            def y1T_out(b):
                need(act, y1t_mm, b)
                reuse(act, ca_mm, b)
                act.copy(flat(y1T), psT2[:]).then_inc(y1t_ev.sem, 1)

            def pcT_out(b):
                need(act, pct_mm, b)
                reuse(act, cao_mm, b)
                act.copy(pcT[:], psT2[0:L, 0:TT * P]).then_inc(pct_ev.sem, 1)

            def y2_hi(b):
                need(act, y2t_mm, b)
                reuse(act, h_mm, b)
                reuse(act, y2l_ev, b)
                act.copy(flat(y2h), psT2[:]).then_inc(y2h_ev.sem, 1)

            def sa_exps(b):
                need(act, sa_mm, b)
                reuse(act, sao_mm, b)
                act.activation(E[:].rearrange("p a q -> p (a q)"), psS[:, 0:3 * P], ACT.Exp, bias=bias16[:, 0:1], scale=ISQ)\
                   .then_inc(sa_exp.sem, 1)

            def ca_exps(b):
                need(act, cm_done, b)
                reuse(act, pct_mm, b)
                reuse(act, crec_done, b)
                for t in range(TT):
                    last = act.activation(pc[:, t, :], psC[:, t * P:t * P + L], ACT.Exp, bias=small["cbias"][:, t:t + 1],
                                          scale=ISQ, accum_out=small["csum"][:, t:t + 1])
                last.then_inc(ca_exp.sem, 1)

            def hidden_out(b, q):
                need(act, h_mm, b, q + 1)
                if q < 2:
                    reuse(act, hl_done, b, q + 3)
                else:
                    need(act, hl_done, b, q - 1)
                for j in range(2):
                    c_ = 2 * q + j
                    last = act.activation(hf[:, q % 2, j, :], psH[:, q % 2, j, :], ACT.Relu, bias=fb1[:, c_:c_ + 1])
                last.then_inc(h_ev.sem, 1)

            run(act, order, dict(so_out=so_out, yT_out=yT_out, y1T_out=y1T_out, pcT_out=pcT_out, y2_hi=y2_hi,
                                 sa_exps=sa_exps, ca_exps=ca_exps, hidden_out=hidden_out), NB)

        @block.vector
        def _(dve):
            dve.memset(bias16[:], -float(D) * ISQ).then_inc(bias_done.sem, 1)
            dve.wait_ge(rows_done.sem, 2)
            dve.wait_ge(const_in.sem, all_const)

            def stats(name, b, src):
                l = lns[name]
                reuse(dve, l["done"], b)
                alone(dve)
                for t in range(TT):
                    last = dve.bn_stats(l["bs"][:, t, :], src[:, t, :])
                last.then_inc(l["st"].sem, 1)
                need(dve, l["st"], b)
                alone(dve)
                for t in range(TT):
                    last = dve.bn_aggr(l["mv"][:, t, :], l["bs"][:, t, :])
                last.then_inc(l["mvd"].sem, 1)

            def apply(name, b, src, dst, g):
                l = lns[name]
                need(dve, l["mvd"], b)
                for t in range(TT):
                    last = dve.scalar_tensor_tensor(out=l["xg"][:, t, :], in0=src[:, t, :], scalar=l["mv"][:, t, 0:1],
                                                    in1=rows[:, g, :], op0=ALU.subtract, op1=ALU.mult)
                last.then_inc(l["xgd"].sem, 1)
                need(dve, l["rss"], b)
                need(dve, l["xgd"], b)
                for t in range(TT):
                    last = dve.scalar_tensor_tensor(out=dst[:, t, :], in0=l["xg"][:, t, :], scalar=l["rs"][:, t:t + 1],
                                                    in1=rows[:, g + 1, :], op0=ALU.mult, op1=ALU.add)
                last.then_inc(l["done"].sem, 1)

            def x2(b):
                need(dve, mix_mm, b)
                x, rc = at(X, b), at2(self.rcomb, b)
                for t in range(TT):
                    last = dve.scalar_tensor_tensor(out=x[:, t, :], in0=psO[:, t * D:(t + 1) * D], scalar=rc[:, t:t + 1],
                                                    in1=x[:, t, :], op0=ALU.mult, op1=ALU.add)
                last.then_inc(x2_done.sem, 1)
                need(dve, x2_done, b)
                stats("l3", b, x)

            def y0(b):
                l, x = lns["l3"], at(X, b)
                need(dve, l["rss"], b)
                reuse(dve, sao_mm, b)
                reuse(dve, r1_done, b)
                for t in range(TT):
                    last = dve.tensor_scalar(y[:, t, 0:D], x[:, t, :], l["mv"][:, t, 0:1], l["rs"][:, t:t + 1],
                                             ALU.subtract, ALU.mult)
                last.then_inc(l["done"].sem, 1)

            def mask(b):
                need(dve, sa_exp, b)
                diag = E[:, 0:3:2, :]
                dve.tensor_tensor(diag, diag, spread(cmask[:].rearrange("p (a q) -> p a q", a=1), 1, 2), ALU.mult)\
                   .then_inc(sa_mask.sem, 1)

            def residual1(b):
                need(dve, sao_mm, b)
                reuse(dve, r1_done, b)
                for t, bank in enumerate((psO, psT)):
                    last = dve.reciprocal(small["srec"][:, t:t + 1], bank[:, D:D + 1])
                last.then_inc(srec_done.sem, 1)
                need(dve, srec_done, b)
                reuse(dve, lns["la"]["done"], b)
                for t, bank in enumerate((psO, psT)):
                    last = dve.scalar_tensor_tensor(out=r1[:, t, :], in0=bank[:, 0:D], scalar=small["srec"][:, t:t + 1],
                                                    in1=y[:, t, 0:D], op0=ALU.mult, op1=ALU.add)
                last.then_inc(r1_done.sem, 1)
                need(dve, r1_done, b)
                stats("la", b, r1)

            def ca_max(b):
                need(dve, ca_mm, b)
                reuse(dve, cm_done, b)
                dve.tensor_reduce(small["cmax"][:], psC[:, 0:2 * P].rearrange("p (t l) -> p t l", t=TT)[:, :, 0:L], AX.X,
                                  ALU.max).then_inc(cm_done.sem, 1)
                need(dve, cm_done, b, 1)
                reuse(dve, ca_exp, b)
                dve.tensor_scalar(small["cbias"][:], small["cmax"][:], -ISQ, None, ALU.mult).then_inc(cm_done.sem, 1)

            def residual2(b):
                need(dve, ca_exp, b)
                reuse(dve, r2_done, b)
                dve.reciprocal(small["crec"][:], small["csum"][:]).then_inc(crec_done.sem, 1)
                need(dve, crec_done, b)
                need(dve, cao_mm, b)
                reuse(dve, lns["lb"]["done"], b)
                for t in range(TT):
                    last = dve.scalar_tensor_tensor(out=r2[:, t, :], in0=psC[:, t * D:(t + 1) * D], scalar=small["crec"][:, t:t + 1],
                                                    in1=y1[:, t, :], op0=ALU.mult, op1=ALU.add)
                last.then_inc(r2_done.sem, 1)
                need(dve, r2_done, b)
                stats("lb", b, r2)

            def y2_lo(b):
                need(dve, y2h_ev, b)
                dve.tensor_tensor(y2l[:].rearrange("p k s -> p (k s)"), psT2[:], y2h[:].bitcast(F32).rearrange("p k s -> p (k s)"),
                                  ALU.subtract).then_inc(y2l_ev.sem, 1)

            def hidden_lo(b, q):
                need(dve, hh_done, b, q + 1)
                dve.tensor_tensor(hl[:, q % 2], hf[:, q % 2], hh[:, q % 2].bitcast(F32), ALU.subtract).then_inc(hl_done.sem, 1)

            def residual3(b):
                need(dve, f2_mm, b)
                need(dve, y2b_done, b)
                reuse(dve, lns["lc"]["done"], b)
                dve.tensor_tensor(r3[:], psF[:], y2b[:], ALU.add).then_inc(r3_done.sem, 1)
                need(dve, r3_done, b)
                stats("lc", b, r3)

            def x3(b):
                x = at(X, b)
                need(dve, lns["lc"]["done"], b)
                for t in range(TT):
                    last = dve.scalar_tensor_tensor(out=x[:, t, :], in0=y3[:, t, :], scalar=self.gates[:, 1:2],
                                                    in1=x[:, t, :], op0=ALU.mult, op1=ALU.add)
                last.then_inc(x3_done.sem, 1)

            def y1_apply(b):
                reuse(dve, y1t_mm, b)
                reuse(dve, r2_done, b)
                apply("la", b, r1, y1, 0)

            def y2_apply(b):
                reuse(dve, y2b_done, b)
                reuse(dve, y2t_mm, b)
                apply("lb", b, r2, y2, 2)

            def y3_apply(b):
                reuse(dve, x3_done, b)
                apply("lc", b, r3, y3, 4)

            run(dve, order, dict(x2=x2, y0=y0, mask=mask, residual1=residual1, y1_apply=y1_apply, ca_max=ca_max,
                                 residual2=residual2, y2_apply=y2_apply, y2_lo=y2_lo, hidden_lo=hidden_lo,
                                 residual3=residual3, y3_apply=y3_apply, x3=x3), NB)

        @block.tensor
        def _(pe):
            def mm(out, lhsT, rhs, start=True, stop=True):
                return pe.matmul(out, lhsT, rhs, start=start, stop=stop)

            def mm3(out, lh, ll, rh, rl, start, stop, shared=False):
                pe.matmul(out, lh, rh, start=start, stop=False, skip_group_check=shared)
                pe.matmul(out, lh, rl, start=False, stop=False, skip_group_check=shared)
                return pe.matmul(out, ll, rh, start=False, stop=stop, skip_group_check=shared)

            def turn4(dst, src):
                for k in range(2):
                    for t in range(2):
                        last = pe.transpose(dst[:, k * S + t * P:k * S + (t + 1) * P], src[:, t, k * P:(k + 1) * P], ident[:])
                return last

            def slot_outputs(b):
                need(pe, load_in, b)
                reuse(pe, r1_done, b)
                turn4(psT, slT).then_inc(so_mm.sem, 1)

            def mix(b):
                need(pe, so_ev, b)
                reuse(pe, r1_done, b)
                for t in range(TT):
                    for k in range(TT):
                        last = mm(psO[:, t * D:(t + 1) * D], combT[:, k, t * P:(t + 1) * P], so[:, k, :], k == 0, k == TT - 1)
                last.then_inc(mix_mm.sem, 1)

            def turn_y(b):
                need(pe, lns["l3"]["done"], b)
                turn4(psT, y).then_inc(yt_mm.sem, 1)

            def sa_scores(b):
                need(pe, yt_ev, b)
                reuse(pe, sa_exp, b)
                for k in range(KD):
                    mm(psS[:, 0:S], yT[:, k, 0:P], yT[:, k, :], k == 0, k == KD - 1)
                for k in range(KD):
                    last = mm(psS[:, S:S + P], yT[:, k, P:S], yT[:, k, P:S], k == 0, k == KD - 1)
                last.then_inc(sa_mm.sem, 1)

            def sa_out(b):
                need(pe, sa_mask, b)
                need(pe, x2_done, b)
                mm(psO[:, 0:YW], E[:, 0, :], y[:, 0, :])
                mm(psT[:, 0:YW], E[:, 1, :], y[:, 0, :], True, False)
                mm(psT[:, 0:YW], E[:, 2, :], y[:, 1, :], False, True).then_inc(sao_mm.sem, 1)

            def turn_y1(b):
                need(pe, lns["la"]["done"], b)
                reuse(pe, y2l_ev, b)
                turn4(psT2, y1).then_inc(y1t_mm.sem, 1)

            def ca_scores(b):
                need(pe, y1t_ev, b)
                need(pe, ctx_in, b)
                reuse(pe, r2_done, b)
                for t in range(TT):
                    for k in range(KD):
                        last = mm(psC[:, t * P:(t + 1) * P], y1T[:, k, t * P:(t + 1) * P], ctxT[:, k, :], k == 0, k == KD - 1)
                last.then_inc(ca_mm.sem, 1)

            def turn_pc(b):
                need(pe, ca_exp, b)
                for t in range(TT):
                    last = pe.transpose(psT2[0:L, t * P:(t + 1) * P], pc[:, t, :], ident[:])
                last.then_inc(pct_mm.sem, 1)

            def ca_out(b):
                need(pe, pct_ev, b)
                for t in range(TT):
                    last = mm(psC[:, t * D:(t + 1) * D], pcT[:, t * P:(t + 1) * P], ctx[:])
                last.then_inc(cao_mm.sem, 1)

            def turn_y2(b):
                need(pe, lns["lb"]["done"], b)
                turn4(psT2, y2).then_inc(y2t_mm.sem, 1)

            def mlp_in(b, q):
                if q == 0:
                    need(pe, y2l_ev, b)
                if q < 2:
                    reuse(pe, h_ev, b, q + 3)
                else:
                    need(pe, h_ev, b, q - 1)
                for j in range(2):
                    cols = slice((2 * q + j) * P, (2 * q + j + 1) * P)
                    for k in range(KD):
                        last = mm3(psH[:, q % 2, j, :], w1h[:, k, cols], w1l[:, k, cols], y2h[:, k, :], y2l[:, k, :],
                                   k == 0, k == KD - 1)
                last.then_inc(h_mm.sem, 1)

            def mlp_out(b, q):
                need(pe, hl_done, b, q + 1)
                if q == 0:
                    reuse(pe, r3_done, b)
                for j in range(2):
                    c_ = 2 * q + j
                    for t in range(TT):
                        cols = slice(t * P, (t + 1) * P)
                        last = mm3(psF[:, t, :], hh[:, q % 2, j, cols], hl[:, q % 2, j, cols], w2h[:, c_, :], w2l[:, c_, :],
                                   c_ == 0 and t == 0, c_ == FC - 1, shared=True)
                last.then_inc(f2_mm.sem, 1)

            pe.wait_ge(wl_done.sem, len(stages))

            run(pe, order, dict(slot_outputs=slot_outputs, mix=mix, turn_y=turn_y, sa_scores=sa_scores, sa_out=sa_out,
                                turn_y1=turn_y1, ca_scores=ca_scores, turn_pc=turn_pc, ca_out=ca_out, turn_y2=turn_y2,
                                mlp_in=mlp_in, mlp_out=mlp_out), NB)

    def phase_d(self, c):
        nc, ins, ident = self.nc, self.ins, self.ident
        sb = lambda n, s, d=F32: self.sb(c, n, s, d)
        sig = lambda n, per=1, step=1: self.sig(c, n, per, step)
        X = self.X[:].rearrange("p (j a) t d -> p j (a t) d", j=NBLK)
        HW = HC * P
        CP = HC // 2 + 1
        Y = self.out.rearrange("(j a) (t p) d -> p j (a t) d", p=P, j=NBLK)

        uph, upl = sb("up_hi", [P, KD, HW], F32R), sb("up_lo", [P, KD, HW], F32R)
        gth, gtl = sb("gate_hi", [P, KD, HW], F32R), sb("gate_lo", [P, KD, HW], F32R)
        dnh, dnl = sb("down_hi", [P, HC, D], F32R), sb("down_lo", [P, HC, D], F32R)
        stage = sb("m_stage", [P, 2, CP * D])
        router = sb("router", [P, KD, P])
        experts = sb("experts", [P, NE1])
        experts_i = sb("experts_i", [P, NE1], mybir.dt.int32)
        zn = sb("m_z", [P, BT, D])
        zf = sb("m_zT", [P, KD, TB])
        zh, zl = sb("m_zT_hi", [P, KD, TB], F32R), sb("m_zT_lo", [P, KD, TB], F32R)
        bs, mv, rs = sb("m_bs", [P, BT, 6]), sb("m_mv", [P, BT, 2]), sb("m_rs", [P, BT])
        top, topd = sb("top", [P, BT, 8]), sb("top_exp", [P, BT, 8])
        idx, idxf = sb("top_idx", [P, BT, 8], U32), sb("top_idx_f", [P, BT, 2])
        tsum, trec = sb("top_sum", [P, BT]), sb("top_rec", [P, BT])
        wtop = sb("top_weight", [P, BT, 2])
        pick = sb("pick", [P, 2, BT, NE1])
        wd = sb("route", [P, P])
        wdT = sb("routeT", [BT * NE1, P])
        wb = sb("route_spread", [P, EC, TB])
        sg = sb("silu", [P, 2, TB])
        hf = sb("m_hidden", [P, 2, TB])
        hh, hl = sb("m_hidden_hi", [P, 3, TB], F32R), sb("m_hidden_lo", [P, 3, TB], F32R)
        o = sb("m_out", [P, BT, D])

        psY = self.ps(c, "m_up", [P, 2, TB])
        psG = self.ps(c, "m_gate", [P, 2, TB])
        psA = self.ps(c, "m_acc", [P, BT, D])
        psT = self.ps(c, "m_turned", [P, TB])
        psR = self.ps(c, "m_router", [P, BT, P])

        fill_done, iota_done, exp_ready = sig("m_fill"), sig("m_iota"), sig("m_experts")
        st_in, hi_done, lo_done = sig("m_stage_in", 1, 16), sig("m_whi"), sig("m_wlo")
        gate_in = sig("m_router_in", 1, 16)
        st, mvd, rss, zn_done = sig("m_st"), sig("m_mvd"), sig("m_rss", 2), sig("m_zn")
        zt_mm, zt_ev, r_mm = sig("m_zt_mm", 2), sig("m_zt_ev", 2), sig("m_r_mm")
        top_done, topd_done, texp, r_step = sig("m_top", 3), sig("m_topd"), sig("m_texp"), sig("m_r_step", 7)
        wdt_mm, wdt_ev, wd_out, wb_in = sig("m_wdt_mm"), sig("m_wdt_ev"), sig("m_wd_out", 1, 16), sig("m_wb_in", 4, 16)
        zh_done, zl_done = sig("m_zh"), sig("m_zl")
        yg_mm, silu_ev, sw_done = sig("m_yg_mm", HC), sig("m_silu", HC), sig("m_sw", EC)
        hf_done, hh_done, hl_done, dn_mm = sig("m_hf", HC), sig("m_hh", HC), sig("m_hl", HC), sig("m_dn_mm", HC)
        o_done, o_out = sig("m_o"), sig("m_o_out", 1, 16)

        upv, gtv = ins["up"].rearrange("(k p) h -> p k h", p=P), ins["gate"].rearrange("(k p) h -> p k h", p=P)
        dnv = ins["down"].rearrange("(c p) d -> p c d", p=P)
        stages = [(upv[:, k], uph[:, k], upl[:, k]) for k in range(KD)] + [(gtv[:, k], gth[:, k], gtl[:, k]) for k in range(KD)] \
            + [(dnv[:, 0:CP], dnh[:, 0:CP], dnl[:, 0:CP]), (dnv[:, CP:HC], dnh[:, CP:HC], dnl[:, CP:HC])]

        def staged(n, src):
            if len(src.shape) == 3:
                return stage[:, n % 2, 0:src.shape[1] * D].rearrange("p (c d) -> p c d", d=D)
            return stage[:, n % 2, 0:HW]

        block = c.enter_context(nc.Block())

        @block.sync
        def _(sp):
            for n, (src, _, _) in enumerate(stages):
                if n >= 2:
                    sp.wait_ge(lo_done.sem, n - 1)
                if n >= 1:
                    sp.wait_ge(st_in.sem, 16 * n)
                sp.dma_start(staged(n, src), src).then_inc(st_in.sem, 16)
                if n == 0:
                    sp.wait_ge(fill_done.sem, 1)
                    sp.dma_start(router[:, :, 0:NE1], ins["gate_wT"].rearrange("(k p) e -> p k e", p=P)).then_inc(gate_in.sem, 16)

            chunks = wb[:].rearrange("p (m r) q -> p m r q", r=3)
            pairs = self.routes.rearrange("(a m two t) q -> a m two (t q)", a=1, two=2, t=BT)

            def schedule(f, k):
                if f is not None:
                    need(sp, wdt_ev, f)
                    sp.dma_start(self.routes, wdT[:]).then_inc(wd_out.sem, 16)
                    need(sp, wd_out, f)
                    reuse(sp, sw_done, f)
                    for r, rows, odd in ((0, slice(0, P), 0), (1, slice(0, P // 2), 0), (1, slice(P // 2, P), 1), (2, slice(0, P), 1)):
                        sp.dma_start(chunks[rows, :, r, :], spread(pairs[:, :, odd, :], 0, P)[rows]).then_inc(wb_in.sem, 16)
                if k is not None:
                    need(sp, o_done, k)
                    sp.dma_start(at(Y, k), o[:]).then_inc(o_out.sem, 16)

            turns(sp, schedule, NBLK)
            need(sp, o_out, NBLK - 1)

        @block.gpsimd
        def _(pool):
            pool.memset(router[:], 0.0)
            pool.memset(wd[:], 0.0)
            pool.iota(experts_i[:], pattern=[[1, NE1]], base=0, channel_multiplier=0).then_inc(fill_done.sem, 1)

            def rstd(b):
                need(pool, mvd, b)
                alone(pool)
                pool.tensor_scalar(rs[:], mv[:, :, 1], LN_EPS, None, ALU.add).then_inc(rss.sem, 1)
                need(pool, rss, b, 1)
                pool.tensor_tensor(rs[:], rs[:], self.minus_half[:, 0:BT], ALU.pow).then_inc(rss.sem, 1)

            def weigh(b, n):
                need(pool, silu_ev, b, n + 1)
                if n == 0:
                    need(pool, wb_in, b)
                if n < 2:
                    reuse(pool, hf_done, b, EC - 1 + n)
                else:
                    need(pool, hf_done, b, n - 1)
                pool.tensor_tensor(sg[:, n % 2, :], sg[:, n % 2, :], wb[:, n, :], ALU.mult).then_inc(sw_done.sem, 1)

            def schedule(f, k):
                if f is not None:
                    rstd(f)
                if k is not None:
                    for n in range(EC):
                        weigh(k, n)

            turns(pool, schedule, NBLK)

        @block.scalar
        def _(act):
            for n, (src, hi, _) in enumerate(stages):
                act.wait_ge(st_in.sem, 16 * (n + 1))
                act.copy(hi, staged(n, src)).then_inc(hi_done.sem, 1)

            def zT_out(b, k):
                need(act, zt_mm, b, k + 1)
                if k == 0:
                    reuse(act, zl_done, b)
                    reuse(act, r_mm, b)
                act.copy(zf[:, k, :], psT[:]).then_inc(zt_ev.sem, 1)

            def top_exp(b):
                need(act, topd_done, b)
                act.activation(topd[:], topd[:], ACT.Exp).then_inc(texp.sem, 1)

            def wdT_out(b):
                need(act, wdt_mm, b)
                reuse(act, wd_out, b)
                act.copy(wdT[:], psR[0:BT * NE1, 0, :]).then_inc(wdt_ev.sem, 1)

            def z_hi(b):
                need(act, zt_ev, b)
                reuse(act, yg_mm, b)
                act.copy(zh[:], zf[:]).then_inc(zh_done.sem, 1)

            def silu(b, n):
                need(act, yg_mm, b, n + 1)
                if n < 2:
                    reuse(act, hf_done, b, HC - 1 + n)
                else:
                    need(act, hf_done, b, n - 1)
                act.activation(sg[:, n % 2, :], psG[:, n % 2, :], ACT.Silu).then_inc(silu_ev.sem, 1)

            def hidden_hi(b, n):
                need(act, hf_done, b, n + 1)
                if n < 3:
                    reuse(act, dn_mm, b, HC - 2 + n)
                else:
                    need(act, dn_mm, b, n - 2)
                act.copy(hh[:, n % 3, :], hf[:, n % 2, :]).then_inc(hh_done.sem, 1)

            prep = {3: lambda b: zT_out(b, 0), 4: lambda b: zT_out(b, 1), 9: top_exp, 12: wdT_out}

            def schedule(f, k):
                for n in range(HC + 1):
                    if f is not None and n in prep:
                        prep[n](f)
                    if k is not None:
                        if n < HC:
                            silu(k, n)
                        if f is not None and n == HC:
                            z_hi(f)
                        if n >= 1:
                            hidden_hi(k, n - 1)
                if f is not None and k is None:
                    z_hi(f)

            turns(act, schedule, NBLK)

        @block.vector
        def _(dve):
            for n, (src, hi, lo) in enumerate(stages):
                dve.wait_ge(hi_done.sem, n + 1)
                dve.tensor_tensor(lo, staged(n, src), hi.bitcast(F32), ALU.subtract).then_inc(lo_done.sem, 1)
            dve.wait_ge(fill_done.sem, 1)
            dve.tensor_copy(experts[:], experts_i[:]).then_inc(exp_ready.sem, 1)
            dve.wait_ge(exp_ready.sem, 1)

            def stats(b):
                x = at(X, b)
                reuse(dve, zn_done, b)
                alone(dve)
                for t in range(BT):
                    last = dve.bn_stats(bs[:, t, :], x[:, t, :])
                last.then_inc(st.sem, 1)
                need(dve, st, b)
                alone(dve)
                for t in range(BT):
                    last = dve.bn_aggr(mv[:, t, :], bs[:, t, :])
                last.then_inc(mvd.sem, 1)

            def apply(b):
                x = at(X, b)
                need(dve, rss, b)
                reuse(dve, zt_mm, b)
                for t in range(BT):
                    last = dve.tensor_scalar(zn[:, t, :], x[:, t, :], mv[:, t, 0:1], rs[:, t:t + 1], ALU.subtract, ALU.mult)
                last.then_inc(zn_done.sem, 1)

            def top_two(b):
                need(dve, r_mm, b)
                alone(dve)
                for t in range(BT):
                    last = dve.max(top[:, t, :], psR[:, t, 0:NE1])
                last.then_inc(top_done.sem, 1)
                need(dve, top_done, b, 1)
                alone(dve)
                for t in range(BT):
                    last = dve.max_index(idx[:, t, :], top[:, t, :], psR[:, t, 0:NE1])
                last.then_inc(top_done.sem, 1)
                need(dve, top_done, b, 2)
                dve.tensor_copy(idxf[:], idx[:, :, 0:2]).then_inc(top_done.sem, 1)
                dve.tensor_tensor(topd[:], top[:], spread(top[:, :, 0:1], 2, 8), ALU.subtract).then_inc(topd_done.sem, 1)

            def route(b):
                need(dve, texp, b)
                dve.tensor_reduce(tsum[:], topd[:], AX.X, ALU.add).then_inc(r_step.sem, 1)
                need(dve, r_step, b, 1)
                dve.reciprocal(trec[:], tsum[:]).then_inc(r_step.sem, 1)
                need(dve, r_step, b, 2)
                dve.tensor_tensor(wtop[:], topd[:, :, 0:2], spread(trec[:].rearrange("p (t a) -> p t a", a=1), 2, 2), ALU.mult)\
                   .then_inc(r_step.sem, 1)
                need(dve, top_done, b)
                need(dve, r_step, b, 3)
                for i in range(2):
                    last = dve.tensor_tensor(pick[:, i], spread(experts[:].rearrange("p (a e) -> p a e", a=1), 1, BT),
                                             spread(idxf[:, :, i:i + 1], 2, NE1), ALU.is_equal)
                last.then_inc(r_step.sem, 1)
                need(dve, r_step, b, 4)
                for i in range(2):
                    last = dve.tensor_tensor(pick[:, i], pick[:, i], spread(wtop[:, :, i:i + 1], 2, NE1), ALU.mult)
                last.then_inc(r_step.sem, 1)
                need(dve, r_step, b, 5)
                reuse(dve, wdt_mm, b)
                dve.tensor_tensor(wd[:, 0:NE1 * BT].rearrange("p (e t) -> p t e", t=BT), pick[:, 0], pick[:, 1], ALU.add)\
                   .then_inc(r_step.sem, 1)
                need(dve, r_step, b, 6)
                dve.tensor_copy(tsum[:], trec[:]).then_inc(r_step.sem, 1)

            def z_lo(b):
                need(dve, zh_done, b)
                dve.tensor_tensor(zl[:], zf[:], zh[:].bitcast(F32), ALU.subtract).then_inc(zl_done.sem, 1)

            def hidden(b, n):
                if n < EC:
                    need(dve, sw_done, b, n + 1)
                else:
                    need(dve, silu_ev, b, n + 1)
                if n < 2:
                    reuse(dve, hl_done, b, HC - 1 + n)
                else:
                    need(dve, hl_done, b, n - 1)
                dve.tensor_tensor(hf[:, n % 2, :], psY[:, n % 2, :], sg[:, n % 2, :], ALU.mult).then_inc(hf_done.sem, 1)

            def hidden_lo(b, n):
                need(dve, hh_done, b, n + 1)
                dve.tensor_tensor(hl[:, n % 3, :], hf[:, n % 2, :], hh[:, n % 3, :].bitcast(F32), ALU.subtract)\
                   .then_inc(hl_done.sem, 1)

            def result(b):
                x = at(X, b)
                need(dve, dn_mm, b)
                reuse(dve, o_out, b)
                for h in range(2):
                    tiles = slice(2 * h, 2 * h + 2)
                    last = dve.scalar_tensor_tensor(out=o[:, tiles, :], in0=psA[:, tiles, :], scalar=self.gates[:, 3:4],
                                                    in1=x[:, tiles, :], op0=ALU.mult, op1=ALU.add)
                last.then_inc(o_done.sem, 1)

            prep = {0: stats, 1: apply, 7: top_two, 10: route}

            def schedule(f, k):
                for n in range(HC + 1):
                    if f is not None and n in prep:
                        prep[n](f)
                    if k is not None:
                        if n < HC:
                            hidden(k, n)
                        if f is not None and n == HC:
                            z_lo(f)
                        if n >= 1:
                            hidden_lo(k, n - 1)
                if f is not None and k is None:
                    z_lo(f)
                if k is not None:
                    result(k)

            turns(dve, schedule, NBLK)

        @block.tensor
        def _(pe):
            pe.wait_ge(lo_done.sem, len(stages))
            pe.wait_ge(gate_in.sem, 16)

            def mm3(out, lh, ll, rh, rl, start, stop, shared=False):
                pe.matmul(out, lh, rh, start=start, stop=False, skip_group_check=shared)
                pe.matmul(out, lh, rl, start=False, stop=False, skip_group_check=shared)
                return pe.matmul(out, ll, rh, start=False, stop=stop, skip_group_check=shared)

            def turn_z(b, k):
                if k == 0:
                    need(pe, zn_done, b)
                    reuse(pe, zt_ev, b)
                else:
                    need(pe, zt_ev, b, 1)
                for t in range(BT):
                    last = pe.transpose(psT[:, t * P:(t + 1) * P], zn[:, t, k * P:(k + 1) * P], ident[:])
                last.then_inc(zt_mm.sem, 1)

            def route(b):
                need(pe, zt_ev, b)
                reuse(pe, wdt_ev, b)
                for t in range(BT):
                    for k in range(KD):
                        last = pe.matmul(psR[:, t, :], zf[:, k, t * P:(t + 1) * P], router[:, k, :], start=(k == 0), stop=(k == KD - 1))
                last.then_inc(r_mm.sem, 1)

            def turn_w(b):
                need(pe, r_step, b, 6)
                need(pe, top_done, b)
                pe.transpose(psR[:, 0, :], wd[:], ident[:]).then_inc(wdt_mm.sem, 1)

            def up(b, n):
                if n == 0:
                    need(pe, zl_done, b)
                if n < 2:
                    reuse(pe, hf_done, b, HC - 1 + n)
                else:
                    need(pe, hf_done, b, n - 1)
                cols = slice(n * P, (n + 1) * P)
                for ps_, wh, wl in ((psG, gth, gtl), (psY, uph, upl)):
                    for k in range(KD):
                        last = mm3(ps_[:, n % 2, :], wh[:, k, cols], wl[:, k, cols], zh[:, k, :], zl[:, k, :], k == 0, k == KD - 1)
                last.then_inc(yg_mm.sem, 1)

            def down(b, n):
                need(pe, hl_done, b, n + 1)
                if n == 0:
                    reuse(pe, o_done, b)
                for t in range(BT):
                    cols = slice(t * P, (t + 1) * P)
                    last = mm3(psA[:, t, :], hh[:, n % 3, cols], hl[:, n % 3, cols], dnh[:, n, :], dnl[:, n, :],
                               n == 0 and t % 2 == 0, n == HC - 1, shared=True)
                last.then_inc(dn_mm.sem, 1)

            prep = {2: lambda b: turn_z(b, 0), 3: lambda b: turn_z(b, 1), 6: route, 11: turn_w}

            def schedule(f, k):
                for n in range(HC + 2):
                    if f is not None and n in prep:
                        prep[n](f)
                    if k is not None:
                        if n < HC:
                            up(k, n)
                        if n >= 2:
                            down(k, n - 2)

            turns(pe, schedule, NBLK)


def spread(ap, dim, n):
    shape = list(ap.shape)
    shape[dim] = n
    return ap.broadcast_to(shape)


def at2(tensor, b):
    if isinstance(b, int):
        return tensor[:, b, :]
    return tensor[:, bass.ds(b, 1), :].rearrange("p a n -> p (a n)")


def layout(inputs):
    import numpy as np

    d = {k: np.asarray(v) for k, v in inputs.items()}

    def columns(v):
        return v.reshape(-1, P).T

    d["wk8"] = np.tile(d.pop("L0_xattn_Wk"), (1, UG))
    d["bk8"] = np.tile(d.pop("L0_xattn_bk"), UG)
    d["bq_cols"] = columns(d.pop("L0_xattn_bq"))
    d["ctxT"] = d["ctx_1024"].transpose(0, 2, 1)
    d["w1_pairs"] = d.pop("L0_ffn_w1").transpose(1, 0, 2).reshape(D, NE0 * H0)
    d["b1_cols"] = columns(d.pop("L0_ffn_b1").reshape(-1))
    d["b2_cols"] = d.pop("L0_ffn_b2").T.reshape(KD, P, NE0).transpose(1, 0, 2)
    d["fb1_cols"] = columns(d.pop("L1_xattn_b1"))
    w1, ws1, hs = d.pop("L1_ffn_W1"), d.pop("L1_ffn_Ws1"), SH
    d["up"] = np.concatenate([w1[:, :H1].reshape(-1, D), ws1[:hs]]).T
    d["gate"] = np.concatenate([w1[:, H1:].reshape(-1, D), ws1[hs:]]).T
    d["down"] = np.concatenate([d.pop("L1_ffn_W2").transpose(0, 2, 1).reshape(-1, D), d.pop("L1_ffn_Ws2").T])
    d["gate_wT"] = d.pop("L1_ffn_gate_w").T
    return {k: np.ascontiguousarray(v) for k, v in d.items()}


def kernel(**inputs):
    from concourse import bacc
    from concourse.bass_utils import run_bass_kernel_spmd

    nc = bacc.Bacc("TRN2", target_bir_lowering=False, num_devices=1)
    arrays = layout(inputs)
    ins = {name: nc.dram_tensor(name, a.shape, mybir.dt.from_np(a.dtype), kind="ExternalInput").ap()
           for name, a in arrays.items()}
    out = nc.dram_tensor("out", (NB, S, D), F32, kind="ExternalOutput").ap()
    Kernel(nc, ins, out).build()
    return run_bass_kernel_spmd(nc, [arrays], core_ids=[0]).results[0]["out"]
```

```python
from contextlib import ExitStack

import concourse.bass as bass
from concourse import mybir

F32 = mybir.dt.float32
F32R = mybir.dt.float32r
F16 = mybir.dt.float16
BF16 = mybir.dt.bfloat16
U32 = mybir.dt.uint32
ALU = mybir.AluOpType
ACT = mybir.ActivationFunctionType
AX = mybir.AxisListType

P = 128
NB, S, D = 16, 256, 256
TT = S // P
KD = D // P
L = 77
G, HD = 16, 16
UG = 8
NE0, NS0, H0 = 16, 16, 64
SLOTS = NE0 * NS0
FF = 1024
FC = FF // P
NE1, H1 = 8, 192
SH = 384
HC = (NE1 * H1 + SH) // P
EC = NE1 * H1 // P
E0 = SH // P - 1
CW = 2 * D + D
AHEAD = 2
SLOT = 5
TB = 512
NBLK = NB * S // TB
BT = TB // P
LN_EPS = 1e-5
L2_EPS = 1e-12


class Signal:

    def __init__(self, sem, per=1, step=1):
        self.sem, self.per, self.step = sem, per, step


def need(eng, sig, b, count=None):
    count = sig.per if count is None else count
    eng.wait_ge(sig.sem, (b * sig.per + count) * sig.step)


def alone(eng):
    eng.nop(nofuse=True)


def reuse(eng, sig, b, count=None):
    if isinstance(b, int) and b == 0:
        return
    count = sig.per if count is None else count
    eng.wait_ge(sig.sem, (b * sig.per + (count - sig.per)) * sig.step)


def at(tensor, b):
    if isinstance(b, int):
        return tensor[:, b]
    part = tensor[:, bass.ds(b, 1)]
    names = " ".join("wxyz"[: len(part.shape) - 2])
    first = names.split()[0]
    return part.rearrange(f"p a {names} -> p (a {first}) {names[2:]}")


def reuse2(eng, sig, b, count=None):
    if isinstance(b, int) and b < 2:
        return
    count = sig.per if count is None else count
    eng.wait_ge(sig.sem, (b * sig.per + (count - 2 * sig.per)) * sig.step)


def run(eng, order, steps, n):
    behind = max(step[0] for step in order)

    def turn(first):
        for stage, name, *part in order:
            b = first - stage
            if name in steps and not (isinstance(b, int) and (b < 0 or b >= n)):
                steps[name](b, *part)

    for t in range(behind + 1):
        turn(t)
    with eng.Fori(behind, n - 1) as i:
        turn(i + 1)
    for t in range(n, n + behind):
        turn(t)


def turns(eng, schedule, n):
    schedule(0, None)
    schedule(1, 0)
    with eng.Fori(1, n - 1) as i:
        schedule(i + 1, i)
    schedule(None, n - 1)


class Kernel:
    def __init__(self, nc, ins, out):
        self.nc, self.ins, self.out = nc, ins, out
        self.used = []

    def sb(self, ctx, name, shape, dt=F32):
        return ctx.enter_context(self.nc.sbuf_tensor(name, shape, dt))

    def ps(self, ctx, name, shape, dt=F32):
        return ctx.enter_context(self.nc.psum_tensor(name, shape, dt))

    def sig(self, ctx, name, per=1, step=1):
        sem = ctx.enter_context(self.nc.semaphore(name))
        self.used.append(sem.num)
        return Signal(sem, per, step)

    def clear_signals(self):
        used, self.used = sorted(set(self.used)), []
        starts = [n for n in used if n - 1 not in used]
        ends = [n + 1 for n in used if n + 1 not in used]
        with self.nc.Block() as block:
            @block.gpsimd
            def _(pool):
                for a, b in zip(starts, ends):
                    pool.sem_clear(range(a, b))

    def build(self):
        nc = self.nc
        self.routes = nc.dram_tensor("routes", [NE1 * BT, P], F32, kind="Internal").ap()
        with ExitStack() as whole:
            self.X = self.sb(whole, "x_all", [P, NB, TT, D])
            self.ident = self.sb(whole, "ident", [P, P])
            self.gates = self.sb(whole, "gates", [P, 4])
            self.minus_half = self.sb(whole, "minus_half", [P, 4])
            self.early = self.sb(whole, "early_weights", [P, NE0 * D])
            with ExitStack() as moe:
                self.CT = self.sb(moe, "combineT_all", [P, NB, TT, S])
                self.SL = self.sb(moe, "slots_all", [P, KD, NB, SLOTS])
                self.rcomb = self.sb(moe, "combine_scale_all", [P, NB, TT])
                self.b1 = self.sb(moe, "e_b1", [P, NE0 // 2])
                self.b2 = self.sb(moe, "e_b2", [P, KD, NE0])
                half = self.early.shape[1] // 2
                self.w1 = self.early[:, 0:half].rearrange("p (k q h) -> p k q h", k=KD, h=P)
                self.w2 = self.early[:, half:2 * half].rearrange("p (q d) -> p q d", d=D)
                with ExitStack() as c:
                    self.phase_a(c)
                self.clear_signals()
                with ExitStack() as mlp:
                    self.f1h = self.sb(mlp, "f_w1_hi", [P, KD, FF], F32R)
                    self.f1l = self.sb(mlp, "f_w1_lo", [P, KD, FF], F32R)
                    self.f2h = self.sb(mlp, "f_w2_hi", [P, FC, D], F32R)
                    self.f2l = self.sb(mlp, "f_w2_lo", [P, FC, D], F32R)
                    self.fb1 = self.sb(mlp, "f_b1", [P, FC])
                    self.rows = self.sb(mlp, "f_rows", [P, 7, D])
                    with ExitStack() as c:
                        self.phase_b(c)
                    with ExitStack() as c:
                        self.phase_c(c)
            self.clear_signals()
            with ExitStack() as c:
                self.phase_d(c)

    def stage_slot(self, n):
        return self.early[:, (n % SLOT) * CW:(n % SLOT + 1) * CW]

    def phase_a(self, c):
        nc, ins = self.nc, self.ins
        X, CT, SL, ident = self.X, self.CT, self.SL, self.ident
        sb = lambda n, s, d=F32: self.sb(c, n, s, d)
        sig = lambda n, per=1, step=1: self.sig(c, n, per, step)

        wq = sb("wq", [P, KD, D])
        wk = sb("wk", [P, KD, P])
        wv = sb("wv", [P, KD, P])
        bq = sb("bq", [P, KD])
        bk = sb("bk", [P, 1])
        bvt = sb("bv_gated", [P, G, HD])
        scale0 = sb("scale0", [P, 1])
        gam0 = sb("gamma0", [P, D])
        bet0 = sb("beta0", [P, D])
        ones = sb("ones", [P, P])
        gmask = sb("group_mask", [P, UG])
        mu = sb("mu", [P, KD, SLOTS])
        mu_sq = sb("mu_sq", [P, KD, SLOTS])
        mu_ss = sb("mu_ss", [P, KD])
        mu_rn = sb("mu_rn", [P, KD])
        mu_diag = sb("mu_diag", [P, KD, P])
        mu_unit = sb("mu_unit", [P, KD, SLOTS])
        ctxT = sb("ctx_turned", [P, KD, P])
        kT = sb("kT", [P, L])
        kblock = sb("kblock", [P, UG, L])
        vpart = sb("vpart_all", [L, NB, 3, HD + 1], BF16)
        vres = sb("vres", [L, 3, HD])
        z = sb("z", [P, TT, D])
        zT = sb("zT", [P, KD, S])
        qT = sb("qT", [P, KD, S])
        mx = sb("mx", [P, UG])
        prob = sb("prob", [P, 2, UG, L])
        prob2 = sb("prob_lo_hi", [P, 2, UG, L, 2], F16)
        probT = sb("probT", [L, G, G, G])
        exp_bias = sb("exp_bias", [P, 1])
        osum = sb("osum", [P, TT, G, HD + 1])
        orec = sb("orec", [P, TT, G])
        oprod = sb("oprod", [P, TT, G, HD])
        mv1 = sb("mv1", [P, TT, 2])
        bs1 = sb("bs1", [P, TT, 6])
        rs1 = sb("rs1", [P, TT])
        bs2 = sb("bs2", [P, TT, 6])
        mv2 = sb("mv2", [P, TT, 2])
        rs2 = sb("rs2", [P, TT])
        xg = sb("xg", [P, TT, D])
        xn = sb("xn", [P, TT, D])
        sq = sb("sq", [P, TT, D])
        ss = sb("ss", [P, TT])
        ru = sb("ru", [P, TT])
        xu = sb("xu", [P, TT, D])
        xuT = sb("xuT", [P, KD, S])
        negmax = sb("negmax", [P, 2, TT])
        esum = sb("esum", [P, 2, TT])
        erec = sb("erec", [P, 2, TT])
        comb = sb("comb", [P, TT, SLOTS])
        dispT = sb("dispT", [P, TT, S])
        disp = sb("disp", [P, TT, SLOTS])

        psA = self.ps(c, "ps_small_a", [P, 512])
        psS = self.ps(c, "ps_scores", [P, 2, 512])
        psT = self.ps(c, "ps_probT", [P, UG, P])
        psB = psT[:, UG // 2:UG, :].rearrange("p g q -> p (g q)")
        psR = self.ps(c, "ps_turned", [P, 512])
        psL = self.ps(c, "ps_logits", [P, 2, 256])
        psM = self.ps(c, "ps_logitsT", [P, 2, 256])

        const_in, mu_in, experts_in = sig("const_in", 1, 16), sig("mu_in", 1, 16), sig("experts_in", 1, 16)
        x_in, ctx_in = sig("x_in", 1, 16), sig("ctx_in", 1, 16)
        filled, id_done, gate_done, bv_done = sig("filled"), sig("id_done"), sig("gate_done"), sig("bv_done")
        mu_sq_done, mu_ss_mm, mu_ss_ev, mu_rn_done = sig("mu_sq_done"), sig("mu_ss_mm"), sig("mu_ss_ev"), sig("mu_rn_done")
        mu_diag_done, mu_bc_mm, mu_done = sig("mu_diag_done"), sig("mu_bc_mm"), sig("mu_done")
        v_out, kv_mm, kb_done, v_step = sig("v_out"), sig("kv_mm"), sig("kb_done"), sig("v_step", 5)
        st1, mv1_done, rs1_step, z_done = sig("st1"), sig("mv1_done"), sig("rs1_step", 2), sig("z_done")
        zt_mm, zt_ev, q_mm, q_ev = sig("zt_mm"), sig("zt_ev"), sig("q_mm"), sig("q_ev")
        sc_mm, mx_done, sub_done, exp_done = sig("sc_mm", 4), sig("mx_done", 4), sig("sub_done", 4), sig("exp_done", 4)
        hi_done, lo_done, pt_mm, pt_ev = sig("hi_done", 4), sig("lo_done", 4), sig("pt_mm", 4), sig("pt_ev", 4)
        pv_mm, osum_done = sig("pv_mm", 4), sig("osum_done", 4)
        xb_done, o_step, x1_done = sig("xb_done"), sig("o_step", 2), sig("x1_done")
        st2, mv2_done, rs2_step, xg_done, xn_done = sig("st2"), sig("mv2_done"), sig("rs2_step", 2), sig("xg_done"), sig("xn_done")
        ss_done, ru_step, xu_done = sig("ss_done"), sig("ru_step", 2), sig("xu_done")
        xut_mm, xut_ev, lg_mm, lt_mm = sig("xut_mm"), sig("xut_ev"), sig("lg_mm"), sig("lt_mm")
        nm_done, ce_done, de_done = sig("nm_done", 2), sig("ce_done"), sig("de_done")
        rec_done, dn_done = sig("rec_done", 2), sig("dn_done")
        ct_mm, ct_ev, dt_mm, dt_ev, sl_mm, sl_ev = sig("ct_mm"), sig("ct_ev"), sig("dt_mm"), sig("dt_ev"), sig("sl_mm"), sig("sl_ev")

        row = lambda ap, n: spread(ap.rearrange("(a d) -> a d", a=1), 0, n)
        const_loads = [
            (wq[:], ins["L0_xattn_Wq"].rearrange("(k p) f -> p k f", p=P)),
            (wk[:], ins["wk8"].rearrange("(k p) f -> p k f", p=P)),
            (wv[:, :, 0:HD], ins["L0_xattn_Wv"].rearrange("(k p) f -> p k f", p=P)),
            (bq[:], ins["bq_cols"]),
            (bk[:], ins["bk8"].rearrange("(p a) -> p a", a=1)),
            (bvt[:], spread(spread(ins["L0_xattn_bv"].rearrange("(a b d) -> a b d", a=1, b=1), 0, P), 1, G)),
            (scale0[:], row(ins["L0_ffn_scale"], P)),
            (gam0[:], row(ins["L0_ffn_ln_gamma"], P)),
            (bet0[:], row(ins["L0_ffn_ln_beta"], P)),
            (self.gates[:, 0:2], row(ins["g_xattn"], P)),
            (self.gates[:, 2:4], row(ins["g_ffn"], P)),
        ]
        expert_loads = [(self.w1, ins["w1_pairs"].rearrange("(k p) (q h) -> p k q h", p=P, h=P)),
                        (self.w2, ins["L0_ffn_w2"].rearrange("(q j) h d -> (j h) q d", j=2)),
                        (self.b1[:], ins["b1_cols"]), (self.b2[:], ins["b2_cols"])]
        block = c.enter_context(nc.Block())
        PRE, MID, OUT, MIX = range(4)

        def unit_steps(u):
            return [(MID, "scores_out", u), (MID, "exps", u), (MID, "high_part", u), (MID, "low_part", u)]

        order = [(MID, "scores", 0), (OUT, "turn_p", 3), (MID, "row_max", 0), (OUT, "probT_act", 3),
                 (MID, "scores_out", 0), (PRE, "ln1_stats"), (MIX, "turn_xu"), (PRE, "ln1_mean"), (MID, "scores", 1),
                 (MID, "row_max", 1), (OUT, "values", 0), (MIX, "xuT_out"), (MIX, "logits"), (PRE, "rstd1"),
                 (OUT, "values", 1), (MIX, "logitsT"), (OUT, "out_sum", 0), (OUT, "values", 2), (MID, "exps", 0),
                 (MID, "scores_out", 1), (MID, "high_part", 0), (MIX, "neg_max"), (OUT, "out_sum", 1),
                 (PRE, "ln1_apply"), (MIX, "neg_maxT"), (MID, "exps", 1), (OUT, "values", 3), (OUT, "out_sum", 2),
                 (MIX, "combine"), (OUT, "out_sum", 3), (MID, "high_part", 1), (MIX, "turn_comb"), (MIX, "dispatch"),
                 (MID, "scores", 2), (OUT, "out_rec"), (MIX, "normalise"), (MIX, "combineT_out"), (PRE, "kv"),
                 (MID, "low_part", 0), (MIX, "disp_scale"), (MID, "turn_p", 0), (MID, "row_max", 2),
                 (MIX, "turn_disp"), (OUT, "out_scale"), (MID, "low_part", 1), (MID, "scores_out", 2),
                 (PRE, "kv_move"), (MID, "probT_out", 0), (PRE, "turn_z"), (MIX, "disp_out"), (MID, "exps", 2),
                 (PRE, "zT_out"), (OUT, "x1"), (MID, "scores", 3), (OUT, "ln2_stats"), (MID, "high_part", 2),
                 (MID, "low_part", 2), (MID, "turn_p", 1), (MID, "row_max", 3), (OUT, "ln2_mean"),
                 (MIX, "slot_inputs"), (PRE, "queries"), (MID, "probT_act", 1), (MID, "scores_out", 3),
                 (MID, "exps", 3), (OUT, "ln2_center"), (PRE, "kv_out"), (MID, "high_part", 3), (OUT, "rstd2"),
                 (MID, "low_part", 3), (MID, "turn_p", 2), (PRE, "q_out"), (OUT, "ln2_scale"), (MIX, "comb_scale"),
                 (OUT, "squares"), (OUT, "runit"), (PRE, "add_bv"), (MID, "probT_out", 2), (MIX, "slots_out"),
                 (OUT, "unit"), (PRE, "v_parts")]

        @block.sync
        def _(sp):
            def load_x(b):
                sp.dma_start(at(X, b), ins["x"].rearrange("b (t p) d -> p b t d", p=P)[:, b] if isinstance(b, int)
                             else at(ins["x"].rearrange("b (t p) d -> p b t d", p=P), b)).then_inc(x_in.sem, 16)

            def load_ctx(b):
                reuse(sp, kv_mm, b)
                src = ins["ctxT"].rearrange("b (k p) l -> p b k l", p=P)
                sp.dma_start(ctxT[:, :, 0:L], at(src, b)).then_inc(ctx_in.sem, 16)

            sp.dma_start(mu[:], ins["L0_ffn_mu"].rearrange("(k p) e s -> p k (e s)", p=P)).then_inc(mu_in.sem, 16)
            load_x(0)
            sp.wait_ge(filled.sem, 1)
            load_ctx(0)
            for dst, src in const_loads[:len(const_loads) // 2]:
                sp.dma_start(dst, src).then_inc(const_in.sem, 16)
            with sp.Fori(1, NB) as b:
                sp.wait_ge(x_in.sem, b * 16)
                load_x(b)
                load_ctx(b)
            for dst, src in expert_loads:
                sp.dma_start(dst, src).then_inc(experts_in.sem, 16)
            sp.wait_ge(experts_in.sem, 16 * len(expert_loads))

        all_const = 16 * len(const_loads)

        def probT_part(eng, copy, b, u):
            need(eng, pt_mm, b, u + 1)
            if u < 2:
                reuse(eng, pv_mm, b)
            tile, g0 = u // 2, (u % 2) * UG
            dst = probT[:, tile * UG:(tile + 1) * UG, :, g0:g0 + UG].rearrange("k h t g -> k (h t) g")
            copy(dst, psT[0:L].rearrange("k g q -> k q g")).then_inc(pt_ev.sem, 1)

        @block.gpsimd
        def _(pool):
            pool.memset(ident[:], 0.0)
            pool.memset(gmask[:], 1.0)
            pool.memset(ones[:], 1.0)
            pool.memset(exp_bias[:], 6.0)
            pool.memset(self.minus_half[:], -0.5)
            pool.memset(wv[:, :, HD:P], 0.0)
            pool.memset(vpart[:, :, 0, HD:HD + 1], 1.0)
            pool.memset(vpart[:, :, 1:3, HD:HD + 1], 0.0)
            pool.memset(ctxT[:], 0.0).then_inc(filled.sem, 1)
            pool.wait_ge(filled.sem, 1)
            pool.affine_select(out=ident[:], in_=ident[:], compare_op=ALU.not_equal, fill=1.0, base=0,
                               pattern=[[-1, P]], channel_multiplier=1).then_inc(id_done.sem, 1)
            pool.affine_select(out=gmask[:], in_=gmask[:], compare_op=ALU.is_ge, fill=0.0, base=0,
                               pattern=[[-HD, UG]], channel_multiplier=1).then_inc(id_done.sem, 1)
            pool.wait_ge(id_done.sem, 2)
            pool.affine_select(out=gmask[:], in_=gmask[:], compare_op=ALU.is_ge, fill=0.0, base=HD - 1,
                               pattern=[[HD, UG]], channel_multiplier=-1).then_inc(id_done.sem, 1)
            pool.wait_ge(mu_ss_ev.sem, 1)
            pool.tensor_tensor(mu_rn[:], mu_ss[:], self.minus_half[:, 0:KD], ALU.pow).then_inc(mu_rn_done.sem, 1)
            pool.wait_ge(gate_done.sem, 1)
            pool.wait_ge(const_in.sem, all_const)
            alone(pool)
            pool.tensor_scalar(bvt[:], bvt[:], self.gates[:, 0:1], None, ALU.mult).then_inc(bv_done.sem, 1)
            pool.wait_ge(bv_done.sem, 1)

            def rstd1(b):
                need(pool, mv1_done, b)
                alone(pool)
                pool.tensor_scalar(rs1[:], mv1[:, :, 1], LN_EPS, None, ALU.add).then_inc(rs1_step.sem, 1)
                need(pool, rs1_step, b, 1)
                pool.tensor_tensor(rs1[:], rs1[:], self.minus_half[:, 0:TT], ALU.pow).then_inc(rs1_step.sem, 1)

            def add_bv(b):
                need(pool, z_done, b)
                alone(pool)
                pool.tensor_tensor(at(X, b), at(X, b), spread(bvt[:].rearrange("p (a g) d -> p a (g d)", a=1), 1, TT),
                                   ALU.add).then_inc(xb_done.sem, 1)

            def low_part(b, u):
                need(pool, hi_done, b, u + 1)
                pool.tensor_tensor(prob2[:, u % 2, :, :, 0], prob[:, u % 2], prob2[:, u % 2, :, :, 1],
                                   ALU.subtract).then_inc(lo_done.sem, 1)

            def v_parts(b):
                v = at(vpart, b)
                need(pool, v_out, b)
                alone(pool)
                pool.tensor_copy(v[:, 0, 0:HD], vres[:, 0, :]).then_inc(v_step.sem, 1)
                need(pool, v_step, b, 1)
                alone(pool)
                pool.tensor_tensor(vres[:, 1, :], vres[:, 0, :], v[:, 0, 0:HD], ALU.subtract).then_inc(v_step.sem, 1)
                need(pool, v_step, b, 2)
                alone(pool)
                pool.tensor_copy(v[:, 1, 0:HD], vres[:, 1, :]).then_inc(v_step.sem, 1)
                need(pool, v_step, b, 3)
                alone(pool)
                pool.tensor_tensor(vres[:, 2, :], vres[:, 1, :], v[:, 1, 0:HD], ALU.subtract).then_inc(v_step.sem, 1)
                need(pool, v_step, b, 4)
                alone(pool)
                pool.tensor_copy(v[:, 2, 0:HD], vres[:, 2, :]).then_inc(v_step.sem, 1)

            def rstd2(b):
                need(pool, mv2_done, b)
                alone(pool)
                pool.tensor_scalar(rs2[:], mv2[:, :, 1], 1.0 + LN_EPS, LN_EPS * LN_EPS, ALU.mult, ALU.add)\
                    .then_inc(rs2_step.sem, 1)
                need(pool, rs2_step, b, 1)
                pool.tensor_tensor(rs2[:], rs2[:], self.minus_half[:, 0:TT], ALU.pow).then_inc(rs2_step.sem, 1)

            def runit(b):
                need(pool, ss_done, b)
                reuse(pool, xu_done, b)
                alone(pool)
                pool.tensor_scalar(ru[:], ss[:], L2_EPS * L2_EPS, None, ALU.max).then_inc(ru_step.sem, 1)
                need(pool, ru_step, b, 1)
                pool.tensor_tensor(ru[:], ru[:], self.minus_half[:, 0:TT], ALU.pow).then_inc(ru_step.sem, 1)

            run(pool, order, dict(rstd1=rstd1, add_bv=add_bv, low_part=low_part, v_parts=v_parts, rstd2=rstd2, runit=runit), NB)

        @block.scalar
        def _(act):
            for dst, src in const_loads[len(const_loads) // 2:]:
                nc.scalar.dma_start(dst, src).then_inc(const_in.sem, 16)
            act.wait_ge(const_in.sem, all_const)
            act.activation(self.gates[:], self.gates[:], ACT.Tanh).then_inc(gate_done.sem, 1)

            act.wait_ge(filled.sem, 1)

            def zT_out(b):
                need(act, zt_mm, b)
                reuse(act, q_mm, b)
                act.copy(zT[:].rearrange("p k s -> p (k s)"), psA[:]).then_inc(zt_ev.sem, 1)

            def q_out(b):
                need(act, q_mm, b)
                reuse(act, sc_mm, b)
                for k in range(KD):
                    ins_ = act.activation(qT[:, k, :], psA[:, k * S:(k + 1) * S], ACT.Identity, bias=bq[:, k:k + 1])
                ins_.then_inc(q_ev.sem, 1)

            def kv_move(b):
                need(act, kv_mm, b)
                reuse(act, v_step, b)
                reuse(act, kb_done, b)
                act.copy(kT[:], psA[:, 0:L])
                act.copy(vres[:, 0, :], psA[0:L, P:P + HD]).then_inc(v_out.sem, 1)

            def high_part(b, u):
                need(act, exp_done, b, u + 1)
                if u < 2:
                    reuse(act, pt_mm, b, 3 + u)
                else:
                    need(act, pt_mm, b, u - 1)
                act.copy(prob2[:, u % 2, :, :, 1], prob[:, u % 2]).then_inc(hi_done.sem, 1)

            def probT_act(b, u):
                probT_part(act, act.copy, b, u)

            def unit(b):
                need(act, ru_step, b)
                reuse(act, xut_mm, b)
                for t in range(TT):
                    ins_ = act.mul(xu[:, t, :], xn[:, t, :], ru[:, t:t + 1])
                ins_.then_inc(xu_done.sem, 1)

            def disp_scale(b):
                need(act, rec_done, b)
                need(act, de_done, b)
                for t in range(TT):
                    ins_ = act.mul(dispT[:, t, :], dispT[:, t, :], erec[:, 1, t:t + 1])
                ins_.then_inc(dn_done.sem, 1)

            def exps(b, u):
                need(act, sub_done, b, u + 1)
                act.activation(prob[:, u % 2], prob[:, u % 2], ACT.Exp, scale=float(D) ** -0.5,
                               bias=exp_bias[:, 0:1]).then_inc(exp_done.sem, 1)

            def squares(b):
                need(act, xn_done, b)
                reuse(act, ss_done, b)
                reuse(act, ru_step, b, 1)
                for t in range(TT):
                    ins_ = act.activation(sq[:, t, :], xn[:, t, :], ACT.Square, accum_out=ss[:, t:t + 1])
                ins_.then_inc(ss_done.sem, 1)

            def xuT_out(b):
                need(act, xut_mm, b)
                reuse(act, lt_mm, b)
                act.copy(xuT[:].rearrange("p k s -> p (k s)"), psR[:]).then_inc(xut_ev.sem, 1)

            def combine(b):
                need(act, nm_done, b, 1)
                reuse(act, ct_mm, b)
                reuse(act, rec_done, b, 1)
                for t in range(TT):
                    ins_ = act.activation(comb[:, t, :], psL[:, t, :], ACT.Exp, bias=negmax[:, 0, t:t + 1],
                                          accum_out=esum[:, 0, t:t + 1])
                ins_.then_inc(ce_done.sem, 1)

            def dispatch(b):
                need(act, nm_done, b, 2)
                reuse(act, dt_mm, b)
                reuse(act, rec_done, b, 2)
                for t in range(TT):
                    ins_ = act.activation(dispT[:, t, :], psM[:, t, :], ACT.Exp, bias=negmax[:, 1, t:t + 1],
                                          accum_out=esum[:, 1, t:t + 1])
                ins_.then_inc(de_done.sem, 1)

            def combineT_out(b):
                need(act, ct_mm, b)
                act.copy(at(CT, b), psR[:].rearrange("p (k s) -> p k s", k=TT)).then_inc(ct_ev.sem, 1)

            def disp_out(b):
                need(act, dt_mm, b)
                reuse(act, sl_mm, b)
                act.copy(disp[:].rearrange("p k s -> p (k s)"), psR[:]).then_inc(dt_ev.sem, 1)

            def slots_out(b):
                need(act, sl_mm, b)
                for k in range(KD):
                    dst = SL[:, k, b, :] if isinstance(b, int) else SL[:, k, bass.ds(b, 1), :].rearrange("p a s -> p (a s)")
                    ins_ = act.copy(dst, psL[:, k, :])
                ins_.then_inc(sl_ev.sem, 1)

            run(act, order, dict(kv_move=kv_move, zT_out=zT_out, q_out=q_out, exps=exps, probT_act=probT_act, unit=unit, disp_scale=disp_scale,
                                 high_part=high_part, squares=squares,
                                 xuT_out=xuT_out, combine=combine, dispatch=dispatch, combineT_out=combineT_out,
                                 disp_out=disp_out, slots_out=slots_out), NB)

        @block.vector
        def _(dve):
            dve.wait_ge(mu_in.sem, 16)
            dve.tensor_tensor(mu_sq[:], mu[:], mu[:], ALU.mult).then_inc(mu_sq_done.sem, 1)
            dve.wait_ge(mu_ss_mm.sem, 1)
            dve.tensor_scalar(mu_ss[:], psA[:].rearrange("p (k s) -> p k s", k=KD)[:, :, 0], L2_EPS * L2_EPS, None, ALU.max)\
               .then_inc(mu_ss_ev.sem, 1)
            dve.wait_ge(mu_rn_done.sem, 1)
            dve.wait_ge(id_done.sem, 3)
            for k in range(KD):
                last = dve.tensor_scalar(mu_diag[:, k, :], ident[:], mu_rn[:, k:k + 1], None, ALU.mult)
            last.then_inc(mu_diag_done.sem, 1)
            dve.wait_ge(mu_bc_mm.sem, 1)
            dve.wait_ge(const_in.sem, all_const)
            dve.scalar_tensor_tensor(out=mu_unit[:], in0=mu[:], scalar=scale0[:, 0:1],
                                     in1=spread(psB[:, 0:SLOTS].rearrange("p (a s) -> p a s", a=1), 1, KD), op0=ALU.mult, op1=ALU.mult)\
               .then_inc(mu_done.sem, 1)


            def kv_out(b):
                need(dve, v_out, b)
                reuse(dve, sc_mm, b)
                dve.scalar_tensor_tensor(out=kblock[:], in0=spread(kT[:].rearrange("p (a l) -> p a l", a=1), 1, UG),
                                         scalar=bk[:, 0:1], in1=spread(gmask[:].rearrange("p (g a) -> p g a", a=1), 2, L),
                                         op0=ALU.add, op1=ALU.mult).then_inc(kb_done.sem, 1)

            def stats(b, src, bs, st, readers):
                reuse(dve, readers, b)
                alone(dve)
                for t in range(TT):
                    last = dve.bn_stats(bs[:, t, :], src[:, t, :])
                last.then_inc(st.sem, 1)

            def aggregate(b, bs, mv, st, done):
                need(dve, st, b)
                alone(dve)
                for t in range(TT):
                    last = dve.bn_aggr(mv[:, t, :], bs[:, t, :])
                last.then_inc(done.sem, 1)

            def ln1_stats(b):
                need(dve, x_in, b)
                stats(b, at(X, b), bs1, st1, z_done)

            def ln1_mean(b):
                aggregate(b, bs1, mv1, st1, mv1_done)

            def ln1_apply(b):
                need(dve, rs1_step, b)
                reuse(dve, zt_mm, b)
                x = at(X, b)
                for t in range(TT):
                    last = dve.tensor_scalar(z[:, t, :], x[:, t, :], mv1[:, t, 0:1], rs1[:, t:t + 1], ALU.subtract, ALU.mult)
                last.then_inc(z_done.sem, 1)

            score_groups = psS[:, :, 0:UG // 2 * L].rearrange("p c (g l) -> p c g l", l=L)

            def row_max(b, u):
                need(dve, sc_mm, b, u + 1)
                dve.tensor_reduce(mx[:].rearrange("p (c g) -> p c g", c=2), score_groups, AX.X, ALU.max)\
                   .then_inc(mx_done.sem, 1)

            def scores_out(b, u):
                need(dve, mx_done, b, u + 1)
                if u < 2:
                    reuse(dve, lo_done, b, 3 + u)
                else:
                    need(dve, lo_done, b, u - 1)
                dve.tensor_tensor(prob[:, u % 2].rearrange("p (c g) l -> p c g l", c=2), score_groups,
                                  spread(mx[:].rearrange("p (c g a) -> p c g a", c=2, a=1), 3, L),
                                  ALU.subtract).then_inc(sub_done.sem, 1)

            def probT_out(b, u):
                probT_part(dve, dve.tensor_copy, b, u)

            def out_sum(b, w):
                need(dve, pv_mm, b, w + 1)
                bank = (psA, psB)[w % 2]
                dve.tensor_reduce(osum[:, w // 2, (w % 2) * 8:(w % 2) * 8 + 8, :],
                                  bank[:, 0:8 * 3 * (HD + 1)].rearrange("p (h c d) -> p h d c", h=8, c=3),
                                  AX.X, ALU.add).then_inc(osum_done.sem, 1)

            def out_rec(b):
                need(dve, osum_done, b)
                dve.reciprocal(orec[:], osum[:, :, :, HD]).then_inc(o_step.sem, 1)

            def out_scale(b):
                need(dve, o_step, b, 1)
                dve.scalar_tensor_tensor(out=oprod[:].rearrange("p t g d -> p (t g) d"),
                                         in0=osum[:, :, :, 0:HD].rearrange("p t g d -> p (t g) d"), scalar=self.gates[:, 0:1],
                                         in1=spread(orec[:].rearrange("p t (g a) -> p (t g) a", a=1), 2, HD),
                                         op0=ALU.mult, op1=ALU.mult).then_inc(o_step.sem, 1)

            def x1(b):
                need(dve, o_step, b, 2)
                need(dve, xb_done, b)
                dve.tensor_tensor(at(X, b), at(X, b), oprod[:].rearrange("p t g d -> p t (g d)"), ALU.add).then_inc(x1_done.sem, 1)

            def ln2_stats(b):
                need(dve, x1_done, b)
                stats(b, at(X, b), bs2, st2, xn_done)

            def ln2_mean(b):
                aggregate(b, bs2, mv2, st2, mv2_done)

            def ln2_center(b):
                x = at(X, b)
                need(dve, mv2_done, b)
                for t in range(TT):
                    last = dve.scalar_tensor_tensor(out=xg[:, t, :], in0=x[:, t, :], scalar=mv2[:, t, 0:1], in1=gam0[:],
                                                    op0=ALU.subtract, op1=ALU.mult)
                last.then_inc(xg_done.sem, 1)

            def ln2_scale(b):
                need(dve, rs2_step, b)
                need(dve, xg_done, b)
                reuse(dve, sl_mm, b)
                reuse(dve, ss_done, b)
                for t in range(TT):
                    last = dve.scalar_tensor_tensor(out=xn[:, t, :], in0=xg[:, t, :], scalar=rs2[:, t:t + 1], in1=bet0[:],
                                                    op0=ALU.mult, op1=ALU.add)
                last.then_inc(xn_done.sem, 1)

            def neg_max(b):
                need(dve, lg_mm, b)
                reuse(dve, ce_done, b)
                dve.tensor_reduce(negmax[:, 0, :], psL[:], AX.X, ALU.max, negate=True).then_inc(nm_done.sem, 1)

            def neg_maxT(b):
                need(dve, lt_mm, b)
                reuse(dve, de_done, b)
                dve.tensor_reduce(negmax[:, 1, :], psM[:], AX.X, ALU.max, negate=True).then_inc(nm_done.sem, 1)

            def normalise(b):
                need(dve, ce_done, b)
                dve.reciprocal(erec[:, 0, :], esum[:, 0, :]).then_inc(rec_done.sem, 1)
                need(dve, de_done, b)
                dve.reciprocal(erec[:, 1, :], esum[:, 1, :]).then_inc(rec_done.sem, 1)

            def comb_scale(b):
                need(dve, rec_done, b)
                dve.tensor_scalar(at2(self.rcomb, b), erec[:, 0, :], self.gates[:, 2:3], None, ALU.mult)

            run(dve, order, dict(kv_out=kv_out, ln1_stats=ln1_stats, ln1_apply=ln1_apply, row_max=row_max, scores_out=scores_out,
                                 probT_out=probT_out, out_sum=out_sum, x1=x1, out_rec=out_rec, out_scale=out_scale, ln1_mean=ln1_mean, ln2_mean=ln2_mean,
                                 neg_maxT=neg_maxT, comb_scale=comb_scale, ln2_stats=ln2_stats, ln2_center=ln2_center, ln2_scale=ln2_scale,
                                 neg_max=neg_max, normalise=normalise), NB)

        @block.tensor
        def _(pe):
            def mm(out, lhsT, rhs, start=True, stop=True):
                return pe.matmul(out, lhsT, rhs, start=start, stop=stop)

            pe.wait_ge(filled.sem, 1)
            pe.wait_ge(mu_sq_done.sem, 1)
            for h in range(KD):
                for k in range(KD):
                    last = mm(psA[:, h * 256:h * 256 + P], mu_sq[:, k, h * P:(h + 1) * P], ones[:], k == 0, k == KD - 1)
            last.then_inc(mu_ss_mm.sem, 1)
            pe.wait_ge(mu_diag_done.sem, 1)
            for h in range(KD):
                last = mm(psB[:, h * P:(h + 1) * P], ones[:], mu_diag[:, h, :])
            last.then_inc(mu_bc_mm.sem, 1)
            pe.wait_ge(mu_done.sem, 1)
            pe.wait_ge(const_in.sem, all_const)

            def turn4(dst, src):
                for k in range(2):
                    for t in range(2):
                        last = pe.transpose(dst[:, k * S + t * P:k * S + (t + 1) * P], src[:, t, k * P:(k + 1) * P], ident[:])
                return last

            def kv(b):
                need(pe, ctx_in, b)
                reuse2(pe, osum_done, b)
                for k in range(KD):
                    mm(psA[:, 0:P], wk[:, k, :], ctxT[:, k, :], k == 0, k == KD - 1)
                for k in range(KD):
                    last = mm(psA[:, P:2 * P], ctxT[:, k, :], wv[:, k, :], k == 0, k == KD - 1)
                last.then_inc(kv_mm.sem, 1)

            def turn_z(b):
                need(pe, z_done, b)
                need(pe, v_out, b)
                turn4(psA, z).then_inc(zt_mm.sem, 1)

            def queries(b):
                need(pe, zt_ev, b)
                for m in range(KD):
                    for k in range(KD):
                        last = mm(psA[:, m * S:(m + 1) * S], wq[:, k, m * P:(m + 1) * P], zT[:, k, :], k == 0, k == KD - 1)
                last.then_inc(q_mm.sem, 1)

            def scores(b, u):
                tile, chunk = u // 2, u % 2
                if u == 0:
                    need(pe, q_ev, b)
                    need(pe, kb_done, b)
                    reuse(pe, sub_done, b)
                else:
                    need(pe, sub_done, b, u)
                for h in range(2):
                    last = mm(psS[:, h, 0:UG // 2 * L], qT[:, chunk, tile * P:(tile + 1) * P],
                              kblock[:, h * UG // 2:(h + 1) * UG // 2, :].rearrange("p g l -> p (g l)"))
                last.then_inc(sc_mm.sem, 1)

            def turn_p(b, u):
                need(pe, lo_done, b, u + 1)
                if u == 0:
                    reuse(pe, pt_ev, b)
                    reuse(pe, osum_done, b)
                else:
                    need(pe, pt_ev, b, u)
                pairs = prob2[:, u % 2].rearrange("p g l two -> p g (l two)").bitcast(F32)
                for g in range(UG):
                    last = pe.transpose(psT[0:L, g, :], pairs[:, g, :], ident[:])
                last.then_inc(pt_mm.sem, 1)

            def values(b, w):
                tile, half = w // 2, w % 2
                bank = (psA, psB)[half]
                if w == 0:
                    need(pe, pt_ev, b)
                    need(pe, v_step, b)
                if w >= 2:
                    need(pe, osum_done, b, w - 1)
                both = probT[:].rearrange("k h t g -> k h (t g)").bitcast(F16)\
                               .rearrange("k h (q two) -> k h q two", two=2)
                W = 3 * (HD + 1)
                rhs = at(vpart, b).rearrange("k c d -> k (c d)")
                for h in range(8):
                    for part in (1, 0):
                        last = mm(bank[:, h * W:(h + 1) * W], both[:, half * 8 + h, tile * P:(tile + 1) * P, part], rhs,
                                  part == 1, part == 0)
                last.then_inc(pv_mm.sem, 1)

            def turn_xu(b):
                need(pe, xu_done, b)
                reuse(pe, dt_ev, b)
                turn4(psR, xu).then_inc(xut_mm.sem, 1)

            def logits(b):
                need(pe, xut_ev, b)
                reuse(pe, sl_ev, b)
                for t in range(TT):
                    for k in range(KD):
                        last = mm(psL[:, t, :], xuT[:, k, t * P:(t + 1) * P], mu_unit[:, k, :], k == 0, k == KD - 1)
                last.then_inc(lg_mm.sem, 1)

            def logitsT(b):
                need(pe, xut_ev, b)
                reuse(pe, de_done, b)
                for h in range(2):
                    for k in range(KD):
                        last = mm(psM[:, h, :], mu_unit[:, k, h * P:(h + 1) * P], xuT[:, k, :], k == 0, k == KD - 1)
                last.then_inc(lt_mm.sem, 1)

            def turn_comb(b):
                need(pe, ce_done, b)
                turn4(psR, comb).then_inc(ct_mm.sem, 1)

            def turn_disp(b):
                need(pe, dn_done, b)
                need(pe, ct_ev, b)
                turn4(psR, dispT).then_inc(dt_mm.sem, 1)

            def slot_inputs(b):
                need(pe, dt_ev, b)
                need(pe, ce_done, b)
                for k in range(KD):
                    for t in range(TT):
                        last = mm(psL[:, k, :], xn[:, t, k * P:(k + 1) * P], disp[:, t, :], t == 0, t == TT - 1)
                last.then_inc(sl_mm.sem, 1)

            run(pe, order, dict(kv=kv, turn_z=turn_z, queries=queries, scores=scores, turn_p=turn_p, values=values,
                                turn_xu=turn_xu, logits=logits, logitsT=logitsT, turn_comb=turn_comb, turn_disp=turn_disp,
                                slot_inputs=slot_inputs), NB)

    def phase_b(self, c):
        nc, ins, SL = self.nc, self.ins, self.SL
        sb = lambda n, s, d=F32: self.sb(c, n, s, d)
        sig = lambda n, per=1, step=1: self.sig(c, n, per, step)
        w1, w2, b1, b2 = self.w1, self.w2, self.b1, self.b2
        wst = sb("f_w_stage", [P, 2, FF])
        hT = [sb(f"e_hT{j}", [P, NB * NS0]) for j in range(2)]
        psH = [self.ps(c, f"ps_hidden{j}", [P, 512]) for j in range(2)]
        psO = [self.ps(c, f"ps_slot_out{j}", [P, KD, NB, NS0]) for j in range(2)]
        zero_done = sig("e_zero_done")
        wst_in, wh_done, wl_done, rows_in = sig("wst_in", 1, 16), sig("wh_done"), sig("wl_done"), sig("rows_in", 1, 16)
        h_mm, h_ev, o_mm, o_ev = sig("e_h_mm"), sig("e_h_ev"), sig("e_o_mm"), sig("e_o_ev")
        row = lambda ap: spread(ap.rearrange("(a d) -> a d", a=1), 0, P)
        names = ["L1_xattn_g1", "L1_xattn_beta1", "L1_xattn_g2", "L1_xattn_beta2", "L1_xattn_g3", "L1_xattn_beta3", "L1_xattn_b2"]
        row_loads = [(self.rows[:, n, :], row(ins[name])) for n, name in enumerate(names)] + [(self.fb1[:], ins["fb1_cols"])]
        w1v = ins["L1_xattn_w1"].rearrange("(k p) f -> p k f", p=P)
        w2v = ins["L1_xattn_w2"].rearrange("(c p) d -> p c d", p=P)
        stages = [(w1v[:, k], self.f1h[:, k], self.f1l[:, k]) for k in range(KD)] \
            + [(w2v[:, h:h + FC // 2], self.f2h[:, h:h + FC // 2], self.f2l[:, h:h + FC // 2]) for h in (0, FC // 2)]

        def stage(n, src):
            view = wst[:, n % 2]
            return view.rearrange("p (c d) -> p c d", d=D) if len(src.shape) == 3 else view

        block = c.enter_context(nc.Block())

        @block.sync
        def _(sp):
            for n, (src, _, _) in enumerate(stages):
                if n >= 2:
                    sp.wait_ge(wl_done.sem, n - 1)
                if n >= 1:
                    sp.wait_ge(wst_in.sem, 16 * n)
                sp.dma_start(stage(n, src), src).then_inc(wst_in.sem, 16)
            for dst, src in row_loads:
                sp.dma_start(dst, src).then_inc(rows_in.sem, 16)
            sp.wait_ge(rows_in.sem, 16 * len(row_loads))

        @block.scalar
        def _(act):
            for e in range(NE0):
                if e % 4 == 2:
                    n = e // 4
                    act.wait_ge(wst_in.sem, 16 * (n + 1))
                    act.copy(stages[n][1], stage(n, stages[n][0])).then_inc(wh_done.sem, 1)
                j, rows = e % 2, slice(e % 2 * H0, e % 2 * H0 + H0)
                if e < 2:
                    act.wait_ge(zero_done.sem, 1)
                else:
                    act.wait_ge(o_mm.sem, e - 1)
                act.wait_ge(h_mm.sem, e + 1)
                act.activation(hT[j][rows, :], psH[j][rows, 0:NB * NS0], ACT.Gelu, bias=b1[rows, e // 2:e // 2 + 1])\
                   .then_inc(h_ev.sem, 1)

        @block.vector
        def _(dve):
            dve.memset(hT[0][:], 0.0)
            dve.memset(hT[1][:], 0.0).then_inc(zero_done.sem, 1)
            for e in range(NE0):
                if e % 4 == 2:
                    src, hi, lo = stages[e // 4]
                    dve.wait_ge(wh_done.sem, e // 4 + 1)
                    dve.tensor_tensor(lo, stage(e // 4, src), hi.bitcast(F32), ALU.subtract).then_inc(wl_done.sem, 1)
                dve.wait_ge(o_mm.sem, e + 1)
                for k in range(KD):
                    last = dve.tensor_scalar(SL[:, k, :, e * NS0:(e + 1) * NS0], psO[e % 2][:, k], b2[:, k, e:e + 1],
                                             None, ALU.add)
                last.then_inc(o_ev.sem, 1)

        @block.tensor
        def _(pe):
            def hidden(e):
                if e >= 2:
                    pe.wait_ge(h_ev.sem, e - 1)
                for k in range(KD):
                    last = pe.matmul(psH[e % 2][:, 0:NB * NS0], w1[:, k, e // 2, :], SL[:, k, :, e * NS0:(e + 1) * NS0],
                                     start=(k == 0), stop=(k == KD - 1))
                last.then_inc(h_mm.sem, 1)

            def outputs(e):
                pe.wait_ge(h_ev.sem, e + 1)
                if e >= 2:
                    pe.wait_ge(o_ev.sem, e - 1)
                for k in range(KD):
                    last = pe.matmul(psO[e % 2][:, k].rearrange("p b s -> p (b s)"), w2[:, e // 2, k * P:(k + 1) * P],
                                     hT[e % 2][:], start=True, stop=True)
                last.then_inc(o_mm.sem, 1)

            hidden(0)
            for e in range(1, NE0):
                hidden(e)
                outputs(e - 1)
            outputs(NE0 - 1)

    def phase_c(self, c):
        nc, ins = self.nc, self.ins
        X, CT, SL, ident = self.X, self.CT, self.SL, self.ident
        sb = lambda n, s, d=F32: self.sb(c, n, s, d)
        sig = lambda n, per=1, step=1: self.sig(c, n, per, step)
        ISQ = float(D) ** -0.5
        YW = D + 2

        w1h, w1l, w2h, w2l, fb1, rows = self.f1h, self.f1l, self.f2h, self.f2l, self.fb1, self.rows
        cmask = sb("causal", [P, P])
        nmr = sb("minus_mean_rstd", [P, TT])
        bias16 = sb("minus_top_score", [P, 1])
        combT = sb("combT", [P, TT, S])
        slT = sb("slT", [P, KD, SLOTS])
        so = sb("so", [P, TT, D])
        ctxT = sb("c_ctxT", [P, KD, P])
        ctx = sb("c_ctx", [L, D])
        y = sb("y", [P, TT, YW])
        yT = sb("yT", [P, KD, S])
        E = sb("sa_exp", [P, 3, P])
        r1, y1 = sb("r1", [P, TT, D]), sb("y1", [P, TT, D])
        y1T = sb("y1T", [P, KD, S])
        pc = sb("ca_prob", [P, TT, L])
        pcT = sb("ca_probT", [L, TT * P])
        r2, y2, y2b = sb("r2", [P, TT, D]), sb("y2", [P, TT, D]), sb("y2b", [P, TT, D])
        y2h, y2l = sb("y2T_hi", [P, KD, S], F32R), sb("y2T_lo", [P, KD, S], F32R)
        hf = sb("f_hidden", [P, 2, 2, S])
        hh, hl = sb("f_hidden_hi", [P, 2, 2, S], F32R), sb("f_hidden_lo", [P, 2, 2, S], F32R)
        r3, y3 = sb("r3", [P, TT, D]), sb("y3", [P, TT, D])
        small = {n: sb(f"c_small_{n}", [P, TT]) for n in ("srec", "cmax", "cbias", "csum", "crec")}
        lns = {}
        for n in ("l3", "la", "lb", "lc"):
            lns[n] = dict(bs=sb(f"bs_{n}", [P, TT, 6]), mv=sb(f"mv_{n}", [P, TT, 2]), rs=sb(f"rs_{n}", [P, TT]),
                          xg=sb(f"xg_{n}", [P, TT, D]) if n != "l3" else None,
                          st=sig(f"st_{n}"), mvd=sig(f"mvd_{n}"), rss=sig(f"rss_{n}", 2), xgd=sig(f"xgd_{n}"),
                          done=sig(f"done_{n}"))

        psT = self.ps(c, "c_turned", [P, 512])
        psO = self.ps(c, "c_out", [P, 512])
        psS = self.ps(c, "c_scores", [P, 512])
        psT2 = self.ps(c, "c_turned2", [P, 512])
        psC = self.ps(c, "c_cross", [P, 512])
        psH = self.ps(c, "c_hidden", [P, 2, 2, S])
        psF = self.ps(c, "c_mlp", [P, TT, D])

        fill_done = sig("c_fill_done", 2)
        bias_done, nmr_done = sig("top_score_done"), sig("nmr_done", 2)
        load_in, chunk_in = sig("c_load_in", 2, 16), sig("c_chunk_in", 1, 16)
        ctx_in = sig("c_ctx_in", 2, 16)
        so_mm, so_ev, mix_mm, x2_done = sig("so_mm"), sig("so_ev"), sig("mix_mm"), sig("x2_done")
        yt_mm, yt_ev, sa_mm, sa_exp, sa_mask = sig("yt_mm"), sig("yt_ev"), sig("sa_mm"), sig("sa_exp_done"), sig("sa_mask")
        sao_mm, srec_done, r1_done = sig("sao_mm"), sig("srec_done"), sig("r1_done")
        y1t_mm, y1t_ev, ca_mm, cm_done, ca_exp = sig("y1t_mm"), sig("y1t_ev"), sig("ca_mm"), sig("cm_done", 2), sig("ca_exp")
        pct_mm, pct_ev, cao_mm, crec_done, r2_done = sig("pct_mm"), sig("pct_ev"), sig("cao_mm"), sig("crec_done"), sig("r2_done")
        y2b_done, y2t_mm, y2h_ev, y2l_ev = sig("y2b_done"), sig("y2t_mm"), sig("y2h_ev"), sig("y2l_ev")
        h_mm, h_ev, hh_done, hl_done, f2_mm = sig("c_h_mm", 4), sig("c_h_ev", 4), sig("hh_done", 4), sig("hl_done", 4), sig("f2_mm", 4)
        r3_done, x3_done = sig("r3_done"), sig("x3_done")

        SELF, CROSS, MLP, LAST = range(4)
        order = [(SELF, "slot_outputs"), (MLP, "mlp_in", 0), (SELF, "so_out"), (CROSS, "y1_center"), (SELF, "mix"),
                 (CROSS, "y1_scale"), (LAST, "residual3"), (CROSS, "turn_y1"), (MLP, "hidden_out", 0),
                 (CROSS, "y1T_out"), (LAST, "stats_c"), (MLP, "mlp_in", 1), (CROSS, "ca_scores"), (SELF, "x2"),
                 (MLP, "hidden_hi", 0), (LAST, "mean_c"), (LAST, "rstd_c"), (MLP, "hidden_lo", 0), (CROSS, "ca_max"),
                 (CROSS, "ca_bias"), (MLP, "hidden_out", 1), (MLP, "mlp_out", 0), (CROSS, "ca_exps"),
                 (SELF, "stats_3"), (CROSS, "turn_pc"), (MLP, "mlp_in", 2), (SELF, "mean_3"), (LAST, "y3_center"),
                 (CROSS, "sums2"), (MLP, "hidden_hi", 1), (SELF, "rstd3"), (CROSS, "pcT_out"), (SELF, "shift3"),
                 (CROSS, "ca_out"), (MLP, "y2_bias"), (MLP, "hidden_out", 2), (SELF, "y0"), (MLP, "hidden_lo", 1),
                 (LAST, "y3_scale"), (MLP, "mlp_out", 1), (SELF, "turn_y"), (CROSS, "residual2"), (SELF, "yT_out"),
                 (MLP, "hidden_hi", 2), (CROSS, "stats_b"), (MLP, "mlp_in", 3), (CROSS, "mean_b"),
                 (CROSS, "y2_center"), (MLP, "hidden_lo", 2), (CROSS, "rstd_b"), (CROSS, "y2_scale"),
                 (MLP, "hidden_out", 3), (SELF, "sa_scores"), (MLP, "mlp_out", 2), (CROSS, "turn_y2"),
                 (SELF, "sa_exps"), (SELF, "mask"), (MLP, "hidden_hi", 3), (CROSS, "y2_hi"), (SELF, "sa_out"),
                 (LAST, "x3"), (MLP, "hidden_lo", 3), (CROSS, "y2_lo"), (SELF, "sums1"), (MLP, "mlp_out", 3),
                 (SELF, "residual1"), (SELF, "stats_a"), (SELF, "mean_a"), (SELF, "rstd_a")]
        block = c.enter_context(nc.Block())

        @block.sync
        def _(sp):
            def load(b):
                reuse(sp, mix_mm, b)
                reuse(sp, load_in, b)
                sp.dma_start(combT[:], at(CT, b)).then_inc(load_in.sem, 16)
                if isinstance(b, int):
                    src = SL[:, :, b, :]
                else:
                    src = SL[:, :, bass.ds(b, 1), :].rearrange("p k a s -> p k (a s)")
                sp.dma_start(slT[:], src).then_inc(load_in.sem, 16)

            def load_ctx(b):
                reuse(sp, cao_mm, b)
                sp.dma_start(ctxT[:, :, 0:L], at(ins["ctxT"].rearrange("b (k p) l -> p b k l", p=P), b)).then_inc(ctx_in.sem, 16)
                sp.dma_start(ctx[:], at2(ins["ctx_1024"].rearrange("b l d -> l b d"), b)).then_inc(ctx_in.sem, 16)

            load(0)
            sp.wait_ge(fill_done.sem, 1)
            load_ctx(0)
            load(1)
            with sp.Fori(1, NB - 1) as b:
                load_ctx(b)
                load(b + 1)
            load_ctx(NB - 1)
            for n in range(SLOT):
                sp.dma_start(self.stage_slot(n), ins["mlp_chunks"][:, n]).then_inc(chunk_in.sem, 16)
            sp.wait_ge(chunk_in.sem, 16 * SLOT)

        @block.gpsimd
        def _(pool):
            pool.memset(cmask[:], 1.0)
            pool.memset(y[:, :, D:D + 1], 1.0)
            pool.memset(y[:, :, D + 1:YW], 0.0)
            pool.memset(ctxT[:], 0.0).then_inc(fill_done.sem, 1)
            pool.wait_ge(fill_done.sem, 1)
            pool.affine_select(out=cmask[:], in_=cmask[:], compare_op=ALU.is_ge, fill=0.0, base=0,
                               pattern=[[1, P]], channel_multiplier=-1).then_inc(fill_done.sem, 1)
            def rstd(name, b):
                l = lns[name]
                need(pool, l["mvd"], b)
                alone(pool)
                pool.tensor_scalar(l["rs"][:], l["mv"][:, :, 1], LN_EPS, None, ALU.add).then_inc(l["rss"].sem, 1)
                need(pool, l["rss"], b, 1)
                pool.tensor_tensor(l["rs"][:], l["rs"][:], self.minus_half[:, 0:TT], ALU.pow).then_inc(l["rss"].sem, 1)

            def shift3(b):
                l = lns["l3"]
                need(pool, l["rss"], b)
                reuse(pool, l["done"], b)
                alone(pool)
                pool.tensor_tensor(nmr[:], l["mv"][:, :, 0], l["rs"][:], ALU.mult).then_inc(nmr_done.sem, 1)
                need(pool, nmr_done, b, 1)
                alone(pool)
                pool.tensor_scalar(nmr[:], nmr[:], -1.0, None, ALU.mult).then_inc(nmr_done.sem, 1)

            def y2_bias(b):
                need(pool, lns["lb"]["done"], b)
                reuse(pool, r3_done, b)
                pool.tensor_tensor(y2b[:], y2[:], spread(rows[:, 6:7, :], 1, TT), ALU.add).then_inc(y2b_done.sem, 1)

            def hidden_hi(b, q):
                need(pool, h_ev, b, q + 1)
                if q < 2:
                    reuse(pool, f2_mm, b, q + 3)
                else:
                    need(pool, f2_mm, b, q - 1)
                alone(pool)
                pool.tensor_copy(hh[:, q % 2], hf[:, q % 2]).then_inc(hh_done.sem, 1)

            run(pool, order, dict(rstd3=lambda b: rstd("l3", b), shift3=shift3, rstd_a=lambda b: rstd("la", b), rstd_b=lambda b: rstd("lb", b),
                                  rstd_c=lambda b: rstd("lc", b), y2_bias=y2_bias, hidden_hi=hidden_hi), NB)

        @block.scalar
        def _(act):
            act.wait_ge(bias_done.sem, 1)

            flat = lambda t_: t_[:].rearrange("p k s -> p (k s)")

            def so_out(b):
                need(act, so_mm, b)
                reuse(act, mix_mm, b)
                act.copy(flat(so), psT[:]).then_inc(so_ev.sem, 1)

            def yT_out(b):
                need(act, yt_mm, b)
                reuse(act, sa_mm, b)
                act.copy(flat(yT), psT[:]).then_inc(yt_ev.sem, 1)

            def y1T_out(b):
                need(act, y1t_mm, b)
                reuse(act, ca_mm, b)
                act.copy(flat(y1T), psT2[:]).then_inc(y1t_ev.sem, 1)

            def pcT_out(b):
                need(act, pct_mm, b)
                reuse(act, cao_mm, b)
                act.copy(pcT[:], psT2[0:L, 0:TT * P]).then_inc(pct_ev.sem, 1)

            def y2_hi(b):
                need(act, y2t_mm, b)
                reuse(act, h_mm, b)
                reuse(act, y2l_ev, b)
                act.copy(flat(y2h), psT2[:]).then_inc(y2h_ev.sem, 1)

            def y0(b):
                l, x = lns["l3"], at(X, b)
                need(act, nmr_done, b)
                reuse(act, sao_mm, b)
                reuse(act, r1_done, b)
                for t in range(TT):
                    last = act.activation(y[:, t, 0:D], x[:, t, :], ACT.Identity, bias=nmr[:, t:t + 1], scale=l["rs"][:, t:t + 1])
                last.then_inc(l["done"].sem, 1)

            def sa_exps(b):
                need(act, sa_mm, b)
                reuse(act, sao_mm, b)
                act.activation(E[:].rearrange("p a q -> p (a q)"), psS[:, 0:3 * P], ACT.Exp, bias=bias16[:, 0:1], scale=ISQ)\
                   .then_inc(sa_exp.sem, 1)

            def ca_exps(b):
                need(act, cm_done, b)
                reuse(act, pct_mm, b)
                reuse(act, crec_done, b)
                for t in range(TT):
                    last = act.activation(pc[:, t, :], psC[:, t * P:t * P + L], ACT.Exp, bias=small["cbias"][:, t:t + 1],
                                          scale=ISQ, accum_out=small["csum"][:, t:t + 1])
                last.then_inc(ca_exp.sem, 1)

            def hidden_out(b, q):
                need(act, h_mm, b, q + 1)
                if q < 2:
                    reuse(act, hl_done, b, q + 3)
                else:
                    need(act, hl_done, b, q - 1)
                for j in range(2):
                    c_ = 2 * q + j
                    last = act.activation(hf[:, q % 2, j, :], psH[:, q % 2, j, :], ACT.Relu, bias=fb1[:, c_:c_ + 1])
                last.then_inc(h_ev.sem, 1)

            run(act, order, dict(so_out=so_out, yT_out=yT_out, y1T_out=y1T_out, pcT_out=pcT_out, y2_hi=y2_hi,
                                 sa_exps=sa_exps, y0=y0, ca_exps=ca_exps, hidden_out=hidden_out), NB)

        @block.vector
        def _(dve):
            dve.memset(bias16[:], -float(D) * ISQ).then_inc(bias_done.sem, 1)
            dve.wait_ge(fill_done.sem, 2)

            def stats(name, b, src):
                l = lns[name]
                reuse(dve, l["done"], b)
                alone(dve)
                for t in range(TT):
                    last = dve.bn_stats(l["bs"][:, t, :], src[:, t, :])
                last.then_inc(l["st"].sem, 1)

            def mean(name, b):
                l = lns[name]
                need(dve, l["st"], b)
                alone(dve)
                for t in range(TT):
                    last = dve.bn_aggr(l["mv"][:, t, :], l["bs"][:, t, :])
                last.then_inc(l["mvd"].sem, 1)

            def center(name, b, src, g):
                l = lns[name]
                need(dve, l["mvd"], b)
                for t in range(TT):
                    last = dve.scalar_tensor_tensor(out=l["xg"][:, t, :], in0=src[:, t, :], scalar=l["mv"][:, t, 0:1],
                                                    in1=rows[:, g, :], op0=ALU.subtract, op1=ALU.mult)
                last.then_inc(l["xgd"].sem, 1)

            def scale(name, b, dst, g):
                l = lns[name]
                need(dve, l["rss"], b)
                need(dve, l["xgd"], b)
                for t in range(TT):
                    last = dve.scalar_tensor_tensor(out=dst[:, t, :], in0=l["xg"][:, t, :], scalar=l["rs"][:, t:t + 1],
                                                    in1=rows[:, g + 1, :], op0=ALU.mult, op1=ALU.add)
                last.then_inc(l["done"].sem, 1)

            def x2(b):
                need(dve, mix_mm, b)
                x, rc = at(X, b), at2(self.rcomb, b)
                for t in range(TT):
                    last = dve.scalar_tensor_tensor(out=x[:, t, :], in0=psO[:, t * D:(t + 1) * D], scalar=rc[:, t:t + 1],
                                                    in1=x[:, t, :], op0=ALU.mult, op1=ALU.add)
                last.then_inc(x2_done.sem, 1)

            def stats_3(b):
                need(dve, x2_done, b)
                stats("l3", b, at(X, b))

            def mask(b):
                need(dve, sa_exp, b)
                diag = E[:, 0:3:2, :]
                dve.tensor_tensor(diag, diag, spread(cmask[:].rearrange("p (a q) -> p a q", a=1), 1, 2), ALU.mult)\
                   .then_inc(sa_mask.sem, 1)

            def sums1(b):
                need(dve, sao_mm, b)
                reuse(dve, r1_done, b)
                for t, bank in enumerate((psO, psT)):
                    last = dve.reciprocal(small["srec"][:, t:t + 1], bank[:, D:D + 1])
                last.then_inc(srec_done.sem, 1)

            def residual1(b):
                need(dve, srec_done, b)
                reuse(dve, lns["la"]["done"], b)
                for t, bank in enumerate((psO, psT)):
                    last = dve.scalar_tensor_tensor(out=r1[:, t, :], in0=bank[:, 0:D], scalar=small["srec"][:, t:t + 1],
                                                    in1=y[:, t, 0:D], op0=ALU.mult, op1=ALU.add)
                last.then_inc(r1_done.sem, 1)

            def stats_a(b):
                need(dve, r1_done, b)
                stats("la", b, r1)

            def ca_max(b):
                need(dve, ca_mm, b)
                reuse(dve, cm_done, b)
                dve.tensor_reduce(small["cmax"][:], psC[:, 0:2 * P].rearrange("p (t l) -> p t l", t=TT)[:, :, 0:L], AX.X,
                                  ALU.max).then_inc(cm_done.sem, 1)

            def ca_bias(b):
                need(dve, cm_done, b, 1)
                reuse(dve, ca_exp, b)
                dve.tensor_scalar(small["cbias"][:], small["cmax"][:], -ISQ, None, ALU.mult).then_inc(cm_done.sem, 1)

            def sums2(b):
                need(dve, ca_exp, b)
                reuse(dve, r2_done, b)
                dve.reciprocal(small["crec"][:], small["csum"][:]).then_inc(crec_done.sem, 1)

            def residual2(b):
                need(dve, crec_done, b)
                need(dve, cao_mm, b)
                reuse(dve, lns["lb"]["done"], b)
                for t in range(TT):
                    last = dve.scalar_tensor_tensor(out=r2[:, t, :], in0=psC[:, t * D:(t + 1) * D], scalar=small["crec"][:, t:t + 1],
                                                    in1=y1[:, t, :], op0=ALU.mult, op1=ALU.add)
                last.then_inc(r2_done.sem, 1)

            def stats_b(b):
                need(dve, r2_done, b)
                stats("lb", b, r2)

            def y2_lo(b):
                need(dve, y2h_ev, b)
                dve.tensor_tensor(y2l[:].rearrange("p k s -> p (k s)"), psT2[:], y2h[:].bitcast(F32).rearrange("p k s -> p (k s)"),
                                  ALU.subtract).then_inc(y2l_ev.sem, 1)

            def hidden_lo(b, q):
                need(dve, hh_done, b, q + 1)
                dve.tensor_tensor(hl[:, q % 2], hf[:, q % 2], hh[:, q % 2].bitcast(F32), ALU.subtract).then_inc(hl_done.sem, 1)

            def residual3(b):
                need(dve, f2_mm, b)
                need(dve, y2b_done, b)
                reuse(dve, lns["lc"]["done"], b)
                dve.tensor_tensor(r3[:], psF[:], y2b[:], ALU.add).then_inc(r3_done.sem, 1)

            def stats_c(b):
                need(dve, r3_done, b)
                stats("lc", b, r3)

            def x3(b):
                x = at(X, b)
                need(dve, lns["lc"]["done"], b)
                for t in range(TT):
                    last = dve.scalar_tensor_tensor(out=x[:, t, :], in0=y3[:, t, :], scalar=self.gates[:, 1:2],
                                                    in1=x[:, t, :], op0=ALU.mult, op1=ALU.add)
                last.then_inc(x3_done.sem, 1)

            def y1_scale(b):
                reuse(dve, y1t_mm, b)
                reuse(dve, r2_done, b)
                scale("la", b, y1, 0)

            def y2_scale(b):
                reuse(dve, y2b_done, b)
                reuse(dve, y2t_mm, b)
                scale("lb", b, y2, 2)

            def y3_scale(b):
                reuse(dve, x3_done, b)
                scale("lc", b, y3, 4)

            def mean_3(b):
                mean("l3", b)

            def mean_a(b):
                mean("la", b)

            def mean_b(b):
                mean("lb", b)

            def mean_c(b):
                mean("lc", b)

            def y1_center(b):
                center("la", b, r1, 0)

            def y2_center(b):
                center("lb", b, r2, 2)

            def y3_center(b):
                center("lc", b, r3, 4)

            run(dve, order, dict(x2=x2, stats_3=stats_3, mean_3=mean_3, mask=mask, sums1=sums1,
                                 residual1=residual1, stats_a=stats_a, mean_a=mean_a, y1_center=y1_center, y1_scale=y1_scale,
                                 ca_max=ca_max, ca_bias=ca_bias, sums2=sums2, residual2=residual2, stats_b=stats_b,
                                 mean_b=mean_b, y2_center=y2_center, y2_scale=y2_scale, y2_lo=y2_lo, hidden_lo=hidden_lo,
                                 residual3=residual3, stats_c=stats_c, mean_c=mean_c, y3_center=y3_center,
                                 y3_scale=y3_scale, x3=x3), NB)

        @block.tensor
        def _(pe):
            def mm(out, lhsT, rhs, start=True, stop=True):
                return pe.matmul(out, lhsT, rhs, start=start, stop=stop)

            def mm3(out, lh, ll, rh, rl, start, stop, shared=False):
                pe.matmul(out, lh, rh, start=start, stop=False, skip_group_check=shared)
                pe.matmul(out, lh, rl, start=False, stop=False, skip_group_check=shared)
                return pe.matmul(out, ll, rh, start=False, stop=stop, skip_group_check=shared)

            def turn4(dst, src):
                for k in range(2):
                    for t in range(2):
                        last = pe.transpose(dst[:, k * S + t * P:k * S + (t + 1) * P], src[:, t, k * P:(k + 1) * P], ident[:])
                return last

            def slot_outputs(b):
                if not isinstance(b, int):
                    need(pe, load_in, b)
                reuse(pe, r1_done, b)
                turn4(psT, SL[:, :, b, :] if isinstance(b, int) else slT).then_inc(so_mm.sem, 1)

            def mix(b):
                need(pe, so_ev, b)
                reuse(pe, r1_done, b)
                weights = CT[:, b] if isinstance(b, int) else combT
                for t in range(TT):
                    for k in range(TT):
                        last = mm(psO[:, t * D:(t + 1) * D], weights[:, k, t * P:(t + 1) * P], so[:, k, :], k == 0, k == TT - 1)
                last.then_inc(mix_mm.sem, 1)

            def turn_y(b):
                need(pe, lns["l3"]["done"], b)
                turn4(psT, y).then_inc(yt_mm.sem, 1)

            def sa_scores(b):
                need(pe, yt_ev, b)
                reuse(pe, sa_exp, b)
                for k in range(KD):
                    mm(psS[:, 0:S], yT[:, k, 0:P], yT[:, k, :], k == 0, k == KD - 1)
                for k in range(KD):
                    last = mm(psS[:, S:S + P], yT[:, k, P:S], yT[:, k, P:S], k == 0, k == KD - 1)
                last.then_inc(sa_mm.sem, 1)

            def sa_out(b):
                need(pe, sa_mask, b)
                need(pe, x2_done, b)
                mm(psO[:, 0:YW], E[:, 0, :], y[:, 0, :])
                mm(psT[:, 0:YW], E[:, 1, :], y[:, 0, :], True, False)
                mm(psT[:, 0:YW], E[:, 2, :], y[:, 1, :], False, True).then_inc(sao_mm.sem, 1)

            def turn_y1(b):
                need(pe, lns["la"]["done"], b)
                reuse(pe, y2l_ev, b)
                turn4(psT2, y1).then_inc(y1t_mm.sem, 1)

            def ca_scores(b):
                need(pe, y1t_ev, b)
                need(pe, ctx_in, b)
                reuse(pe, r2_done, b)
                for t in range(TT):
                    for k in range(KD):
                        last = mm(psC[:, t * P:(t + 1) * P], y1T[:, k, t * P:(t + 1) * P], ctxT[:, k, :], k == 0, k == KD - 1)
                last.then_inc(ca_mm.sem, 1)

            def turn_pc(b):
                need(pe, ca_exp, b)
                for t in range(TT):
                    last = pe.transpose(psT2[0:L, t * P:(t + 1) * P], pc[:, t, :], ident[:])
                last.then_inc(pct_mm.sem, 1)

            def ca_out(b):
                need(pe, pct_ev, b)
                for t in range(TT):
                    last = mm(psC[:, t * D:(t + 1) * D], pcT[:, t * P:(t + 1) * P], ctx[:])
                last.then_inc(cao_mm.sem, 1)

            def turn_y2(b):
                need(pe, lns["lb"]["done"], b)
                turn4(psT2, y2).then_inc(y2t_mm.sem, 1)

            def mlp_in(b, q):
                if q == 0:
                    need(pe, y2l_ev, b)
                if q < 2:
                    reuse(pe, h_ev, b, q + 3)
                else:
                    need(pe, h_ev, b, q - 1)
                for j in range(2):
                    cols = slice((2 * q + j) * P, (2 * q + j + 1) * P)
                    for k in range(KD):
                        last = mm3(psH[:, q % 2, j, :], w1h[:, k, cols], w1l[:, k, cols], y2h[:, k, :], y2l[:, k, :],
                                   k == 0, k == KD - 1)
                last.then_inc(h_mm.sem, 1)

            def mlp_out(b, q):
                need(pe, hl_done, b, q + 1)
                if q == 0:
                    reuse(pe, r3_done, b)
                for j in range(2):
                    c_ = 2 * q + j
                    for t in range(TT):
                        cols = slice(t * P, (t + 1) * P)
                        last = mm3(psF[:, t, :], hh[:, q % 2, j, cols], hl[:, q % 2, j, cols], w2h[:, c_, :], w2l[:, c_, :],
                                   c_ == 0 and t == 0, c_ == FC - 1, shared=True)
                last.then_inc(f2_mm.sem, 1)

            run(pe, order, dict(slot_outputs=slot_outputs, mix=mix, turn_y=turn_y, sa_scores=sa_scores, sa_out=sa_out,
                                turn_y1=turn_y1, ca_scores=ca_scores, turn_pc=turn_pc, ca_out=ca_out, turn_y2=turn_y2,
                                mlp_in=mlp_in, mlp_out=mlp_out), NB)

    def phase_d(self, c):
        nc, ins, ident = self.nc, self.ins, self.ident
        sb = lambda n, s, d=F32: self.sb(c, n, s, d)
        sig = lambda n, per=1, step=1: self.sig(c, n, per, step)
        X = self.X[:].rearrange("p (j a) t d -> p j (a t) d", j=NBLK)
        Y = self.out.rearrange("(j a) (t p) d -> p j (a t) d", p=P, j=NBLK)

        wh, wl = sb("m_weights_hi", [P, HC, CW], F32R), sb("m_weights_lo", [P, HC, CW], F32R)
        router = sb("router", [P, KD, P])
        experts = sb("experts", [P, NE1])
        experts_i = sb("experts_i", [P, NE1], mybir.dt.int32)
        zn = sb("m_z", [P, BT, D])
        zf = sb("m_zT", [P, KD, TB])
        zh, zl = sb("m_zT_hi", [P, KD, TB], F32R), sb("m_zT_lo", [P, KD, TB], F32R)
        bs, mv, rs = sb("m_bs", [P, BT, 6]), sb("m_mv", [P, BT, 2]), sb("m_rs", [P, BT])
        top, topd = sb("top", [P, BT, 8]), sb("top_exp", [P, BT, 8])
        idx, idxf = sb("top_idx", [P, BT, 8], U32), sb("top_idx_f", [P, BT, 2])
        tsum, trec = sb("top_sum", [P, BT]), sb("top_rec", [P, BT])
        wtop = sb("top_weight", [P, BT, 2])
        pick = sb("pick", [P, 2, BT, NE1])
        wd = sb("route", [P, P])
        wdT = sb("routeT", [BT * NE1, P])
        wb = sb("route_spread", [P, EC, TB])
        sg = sb("silu", [P, 2, TB])
        hf = sb("m_hidden", [P, 2, TB])
        hh, hl = sb("m_hidden_hi", [P, 3, TB], F32R), sb("m_hidden_lo", [P, 3, TB], F32R)
        o = sb("m_out", [P, BT, D])

        psY = self.ps(c, "m_up", [P, 2, TB])
        psG = self.ps(c, "m_gate", [P, 2, TB])
        psA = self.ps(c, "m_acc", [P, BT, D])
        psT = self.ps(c, "m_turned", [P, TB])
        psR = self.ps(c, "m_router", [P, BT, P])

        fill_done, exp_ready = sig("m_fill"), sig("m_experts")
        st_in, hi_done, lo_done = [sig(f"m_stage_in{j}", 1, 16) for j in range(2)], sig("m_whi"), sig("m_wlo")
        gate_in = sig("m_router_in", 1, 16)
        st, mvd, rss, zn_done = sig("m_st"), sig("m_mvd"), sig("m_rss", 2), sig("m_zn")
        zt_mm, zt_ev, r_mm = sig("m_zt_mm", 2), sig("m_zt_ev", 2), sig("m_r_mm")
        top_done, topd_done, texp, r_step = sig("m_top", 3), sig("m_topd"), sig("m_texp"), sig("m_r_step", 6)
        wdt_mm, wdt_ev, wd_out, wb_in = sig("m_wdt_mm"), sig("m_wdt_ev"), sig("m_wd_out", 1, 16), [sig(f"m_wb_in{r}", 1 + r % 2, 16) for r in range(3)]
        zh_done, zl_done = sig("m_zh"), sig("m_zl")
        yg_mm, silu_ev, sw_done = sig("m_yg_mm", HC), sig("m_silu", HC), sig("m_sw", EC)
        hf_done, hh_done, hl_done, dn_mm = sig("m_hf", HC), sig("m_hh", HC), sig("m_hl", HC), sig("m_dn_mm", HC)
        o_done, o_out = sig("m_o"), sig("m_o_out", 1, 16)

        block = c.enter_context(nc.Block())

        @block.sync
        def _(sp):
            sp.wait_ge(fill_done.sem, 1)
            sp.dma_start(router[:, :, 0:NE1], ins["gate_wT"].rearrange("(k p) e -> p k e", p=P)).then_inc(gate_in.sem, 16)

            chunks = wb[:].rearrange("p (r m) q -> p r m q", r=3)
            pairs = self.routes.rearrange("(a m two t) q -> a m two (t q)", a=1, two=2, t=BT)

            def schedule(f, k):
                if f is not None:
                    need(sp, wdt_ev, f)
                    sp.dma_start(self.routes, wdT[:]).then_inc(wd_out.sem, 16)
                    need(sp, wd_out, f)
                    reuse(sp, sw_done, f)
                    for r, rows, odd in ((0, slice(0, P), 0), (1, slice(0, P // 2), 0), (1, slice(P // 2, P), 1), (2, slice(0, P), 1)):
                        sp.dma_start(chunks[rows, r], spread(pairs[:, :, odd, :], 0, P)[rows]).then_inc(wb_in[r].sem, 16)
                if k is not None:
                    need(sp, o_done, k)
                    sp.dma_start(at(Y, k), o[:]).then_inc(o_out.sem, 16)

            turns(sp, schedule, NBLK)
            need(sp, o_out, NBLK - 1)

        @block.gpsimd
        def _(pool):
            pool.memset(router[:], 0.0)
            pool.memset(wd[:], 0.0)
            pool.iota(experts_i[:], pattern=[[1, NE1]], base=0, channel_multiplier=0).then_inc(fill_done.sem, 1)

            def rstd(b):
                need(pool, mvd, b)
                alone(pool)
                pool.tensor_scalar(rs[:], mv[:, :, 1], LN_EPS, None, ALU.add).then_inc(rss.sem, 1)
                need(pool, rss, b, 1)
                pool.tensor_tensor(rs[:], rs[:], self.minus_half[:, 0:BT], ALU.pow).then_inc(rss.sem, 1)

            def weigh(b, n):
                need(pool, silu_ev, b, n + 1)
                if (n - E0) % (EC // 3) == 0:
                    need(pool, wb_in[(n - E0) // (EC // 3)], b)
                pool.tensor_tensor(sg[:, n % 2, :], sg[:, n % 2, :], wb[:, n - E0, :], ALU.mult).then_inc(sw_done.sem, 1)

            def schedule(f, k):
                if f is not None:
                    rstd(f)
                if k is not None:
                    for n in range(E0, E0 + EC):
                        weigh(k, n)

            turns(pool, schedule, NBLK)

        @block.scalar
        def _(act):
            def load_chunk(n):
                act.wait_ge(lo_done.sem, n - SLOT + 1)
                if n >= SLOT + 2:
                    act.wait_ge(st_in[(n - SLOT) % 2].sem, (n - SLOT) // 2 * 16)
                nc.scalar.dma_start(self.stage_slot(n), ins["mlp_chunks"][:, n]).then_inc(st_in[(n - SLOT) % 2].sem, 16)

            def weights_hi(n):
                if n >= SLOT:
                    act.wait_ge(st_in[(n - SLOT) % 2].sem, ((n - SLOT) // 2 + 1) * 16)
                act.copy(wh[:, n, :], self.stage_slot(n)).then_inc(hi_done.sem, 1)

            def zT_out(b, k):
                need(act, zt_mm, b, k + 1)
                if k == 0:
                    reuse(act, zl_done, b)
                    reuse(act, r_mm, b)
                act.copy(zf[:, k, :], psT[:]).then_inc(zt_ev.sem, 1)

            def top_exp(b):
                need(act, topd_done, b)
                act.activation(topd[:], topd[:], ACT.Exp).then_inc(texp.sem, 1)

            def wdT_out(b):
                need(act, wdt_mm, b)
                reuse(act, wd_out, b)
                act.copy(wdT[:], psR[0:BT * NE1, 0, :]).then_inc(wdt_ev.sem, 1)

            def z_hi(b):
                need(act, zt_ev, b)
                reuse(act, yg_mm, b)
                act.copy(zh[:], zf[:]).then_inc(zh_done.sem, 1)

            def silu(b, n):
                need(act, yg_mm, b, n + 1)
                if n < 2:
                    reuse(act, hf_done, b, HC - 1 + n)
                else:
                    need(act, hf_done, b, n - 1)
                act.activation(sg[:, n % 2, :], psG[:, n % 2, :], ACT.Silu).then_inc(silu_ev.sem, 1)

            def hidden_hi(b, n):
                need(act, hf_done, b, n + 1)
                if n < 3:
                    reuse(act, dn_mm, b, HC - 2 + n)
                else:
                    need(act, dn_mm, b, n - 2)
                act.copy(hh[:, n % 3, :], hf[:, n % 2, :]).then_inc(hh_done.sem, 1)

            prep = {4: lambda b: zT_out(b, 0), 6: lambda b: zT_out(b, 1), 9: top_exp, 12: wdT_out}
            first_prep = {1: top_exp, 2: wdT_out}

            def schedule(f, k):
                first = isinstance(k, int) and k == 0
                for n in range(HC + 1):
                    if first:
                        if n in first_prep:
                            first_prep[n](0)
                        if n + AHEAD < HC:
                            weights_hi(n + AHEAD)
                        if n + AHEAD - 1 + SLOT < HC:
                            load_chunk(n + AHEAD - 1 + SLOT)
                    if f is not None and n in prep and (k is not None or n in (4, 6)):
                        prep[n](f)
                    if k is None and f is not None and n < AHEAD:
                        weights_hi(n)
                    if k is None and n == AHEAD:
                        load_chunk(SLOT)
                    if k is not None:
                        if n >= 1:
                            hidden_hi(k, n - 1)
                        if n < HC:
                            silu(k, n)
                        if f is not None and n == HC:
                            z_hi(f)
                if f is not None and k is None:
                    z_hi(f)

            turns(act, schedule, NBLK)

        @block.vector
        def _(dve):
            def weights_lo(n):
                dve.wait_ge(hi_done.sem, n + 1)
                dve.tensor_tensor(wl[:, n, :], self.stage_slot(n), wh[:, n, :].bitcast(F32), ALU.subtract).then_inc(lo_done.sem, 1)

            dve.wait_ge(fill_done.sem, 1)
            dve.tensor_copy(experts[:], experts_i[:]).then_inc(exp_ready.sem, 1)
            dve.wait_ge(exp_ready.sem, 1)

            def stats(b):
                x = at(X, b)
                reuse(dve, zn_done, b)
                alone(dve)
                for t in range(BT):
                    last = dve.bn_stats(bs[:, t, :], x[:, t, :])
                last.then_inc(st.sem, 1)
                need(dve, st, b)
                alone(dve)
                for t in range(BT):
                    last = dve.bn_aggr(mv[:, t, :], bs[:, t, :])
                last.then_inc(mvd.sem, 1)

            def apply(b):
                x = at(X, b)
                need(dve, rss, b)
                reuse(dve, zt_mm, b)
                for t in range(BT):
                    last = dve.tensor_scalar(zn[:, t, :], x[:, t, :], mv[:, t, 0:1], rs[:, t:t + 1], ALU.subtract, ALU.mult)
                last.then_inc(zn_done.sem, 1)

            def top_two(b):
                need(dve, r_mm, b)
                alone(dve)
                for t in range(BT):
                    last = dve.max(top[:, t, :], psR[:, t, 0:NE1])
                last.then_inc(top_done.sem, 1)
                need(dve, top_done, b, 1)
                alone(dve)
                for t in range(BT):
                    last = dve.max_index(idx[:, t, :], top[:, t, :], psR[:, t, 0:NE1])
                last.then_inc(top_done.sem, 1)
                need(dve, top_done, b, 2)
                dve.tensor_copy(idxf[:], idx[:, :, 0:2]).then_inc(top_done.sem, 1)
                dve.tensor_tensor(topd[:], top[:], spread(top[:, :, 0:1], 2, 8), ALU.subtract).then_inc(topd_done.sem, 1)

            def route(b):
                need(dve, texp, b)
                dve.tensor_reduce(tsum[:], topd[:], AX.X, ALU.add).then_inc(r_step.sem, 1)
                need(dve, r_step, b, 1)
                dve.reciprocal(trec[:], tsum[:]).then_inc(r_step.sem, 1)
                need(dve, r_step, b, 2)
                dve.tensor_tensor(wtop[:], topd[:, :, 0:2], spread(trec[:].rearrange("p (t a) -> p t a", a=1), 2, 2), ALU.mult)\
                   .then_inc(r_step.sem, 1)
                need(dve, top_done, b)
                need(dve, r_step, b, 3)
                for i in range(2):
                    last = dve.tensor_tensor(pick[:, i], spread(experts[:].rearrange("p (a e) -> p a e", a=1), 1, BT),
                                             spread(idxf[:, :, i:i + 1], 2, NE1), ALU.is_equal)
                last.then_inc(r_step.sem, 1)
                need(dve, r_step, b, 4)
                for i in range(2):
                    last = dve.tensor_tensor(pick[:, i], pick[:, i], spread(wtop[:, :, i:i + 1], 2, NE1), ALU.mult)
                last.then_inc(r_step.sem, 1)
                need(dve, r_step, b, 5)
                reuse(dve, wdt_mm, b)
                dve.tensor_tensor(wd[:, 0:NE1 * BT].rearrange("p (e t) -> p t e", t=BT), pick[:, 0], pick[:, 1], ALU.add)\
                   .then_inc(r_step.sem, 1)

            def z_lo(b):
                need(dve, zh_done, b)
                dve.tensor_tensor(zl[:], zf[:], zh[:].bitcast(F32), ALU.subtract).then_inc(zl_done.sem, 1)

            def hidden(b, n):
                if E0 <= n < E0 + EC:
                    need(dve, sw_done, b, n - E0 + 1)
                else:
                    need(dve, silu_ev, b, n + 1)
                if n < 2:
                    reuse(dve, hl_done, b, HC - 1 + n)
                else:
                    need(dve, hl_done, b, n - 1)
                dve.tensor_tensor(hf[:, n % 2, :], psY[:, n % 2, :], sg[:, n % 2, :], ALU.mult).then_inc(hf_done.sem, 1)

            def hidden_lo(b, n):
                need(dve, hh_done, b, n + 1)
                dve.tensor_tensor(hl[:, n % 3, :], hf[:, n % 2, :], hh[:, n % 3, :].bitcast(F32), ALU.subtract)\
                   .then_inc(hl_done.sem, 1)

            def result(b):
                x = at(X, b)
                need(dve, dn_mm, b)
                reuse(dve, o_out, b)
                for h in range(2):
                    tiles = slice(2 * h, 2 * h + 2)
                    last = dve.scalar_tensor_tensor(out=o[:, tiles, :], in0=psA[:, tiles, :], scalar=self.gates[:, 3:4],
                                                    in1=x[:, tiles, :], op0=ALU.mult, op1=ALU.add)
                last.then_inc(o_done.sem, 1)

            prep = {0: stats, 1: apply, 8: top_two, 10: route}
            first_prep = {0: top_two, 1: route}

            def schedule(f, k):
                first = isinstance(k, int) and k == 0
                for n in range(HC + 1):
                    if first:
                        if n in first_prep:
                            first_prep[n](0)
                        if n + AHEAD < HC:
                            weights_lo(n + AHEAD)
                    if f is not None and n in prep and (k is not None or n < 2):
                        prep[n](f)
                    if k is None and n < AHEAD:
                        weights_lo(n)
                    if k is not None:
                        if n >= 1:
                            hidden_lo(k, n - 1)
                        if n < HC:
                            hidden(k, n)
                        if f is not None and n == HC:
                            z_lo(f)
                if f is not None and k is None:
                    z_lo(f)
                if k is not None:
                    result(k)

            turns(dve, schedule, NBLK)

        @block.tensor
        def _(pe):
            pe.wait_ge(gate_in.sem, 16)

            def mm3(out, lh, ll, rh, rl, start, stop, shared=False):
                pe.matmul(out, lh, rh, start=start, stop=False, skip_group_check=shared)
                pe.matmul(out, lh, rl, start=False, stop=False, skip_group_check=shared)
                return pe.matmul(out, ll, rh, start=False, stop=stop, skip_group_check=shared)

            def turn_z(b, k):
                if k == 0:
                    need(pe, zn_done, b)
                    reuse(pe, zt_ev, b)
                else:
                    need(pe, zt_ev, b, 1)
                for t in range(BT):
                    last = pe.transpose(psT[:, t * P:(t + 1) * P], zn[:, t, k * P:(k + 1) * P], ident[:])
                last.then_inc(zt_mm.sem, 1)

            def route(b):
                need(pe, zt_ev, b)
                reuse(pe, wdt_ev, b)
                for t in range(BT):
                    for k in range(KD):
                        last = pe.matmul(psR[:, t, :], zf[:, k, t * P:(t + 1) * P], router[:, k, :], start=(k == 0), stop=(k == KD - 1))
                last.then_inc(r_mm.sem, 1)

            def turn_w(b):
                need(pe, r_step, b, 6)
                need(pe, top_done, b)
                pe.transpose(psR[:, 0, :], wd[:], ident[:]).then_inc(wdt_mm.sem, 1)

            def up(b, n):
                if n == 0:
                    need(pe, zl_done, b)
                if n < 2:
                    reuse(pe, hf_done, b, HC - 1 + n)
                else:
                    need(pe, hf_done, b, n - 1)
                if isinstance(b, int) and b == 0:
                    pe.wait_ge(lo_done.sem, n + 1)
                for ps_, first_col in ((psG, D), (psY, 0)):
                    for k in range(KD):
                        cols = slice(first_col + k * P, first_col + (k + 1) * P)
                        last = mm3(ps_[:, n % 2, :], wh[:, n, cols], wl[:, n, cols], zh[:, k, :], zl[:, k, :], k == 0, k == KD - 1)
                last.then_inc(yg_mm.sem, 1)

            def down(b, n):
                need(pe, hl_done, b, n + 1)
                if n == 0:
                    reuse(pe, o_done, b)
                for t in range(BT):
                    cols = slice(t * P, (t + 1) * P)
                    last = mm3(psA[:, t, :], hh[:, n % 3, cols], hl[:, n % 3, cols], wh[:, n, 2 * D:CW], wl[:, n, 2 * D:CW],
                               n == 0 and t % 2 == 0, n == HC - 1, shared=True)
                last.then_inc(dn_mm.sem, 1)

            prep = {3: lambda b: turn_z(b, 0), 5: lambda b: turn_z(b, 1), 7: route, 11: turn_w}
            first_prep = {0: route, 2: turn_w}

            def schedule(f, k):
                first = isinstance(k, int) and k == 0
                for n in range(HC + 2):
                    if first and n in first_prep:
                        first_prep[n](0)
                    if f is not None and n in prep and (k is not None or n < 6):
                        prep[n](f)
                    if k is not None:
                        if n < HC:
                            up(k, n)
                        if n >= 2:
                            down(k, n - 2)

            turns(pe, schedule, NBLK)


def spread(ap, dim, n):
    shape = list(ap.shape)
    shape[dim] = n
    return ap.broadcast_to(shape)


def at2(tensor, b):
    if isinstance(b, int):
        return tensor[:, b, :]
    return tensor[:, bass.ds(b, 1), :].rearrange("p a n -> p (a n)")


def layout(inputs):
    import numpy as np

    d = {k: np.asarray(v) for k, v in inputs.items()}

    def columns(v):
        return v.reshape(-1, P).T

    d["wk8"] = np.tile(d.pop("L0_xattn_Wk"), (1, UG))
    d["bk8"] = np.tile(d.pop("L0_xattn_bk"), UG)
    d["bq_cols"] = columns(d.pop("L0_xattn_bq"))
    d["ctxT"] = d["ctx_1024"].transpose(0, 2, 1)
    d["w1_pairs"] = d.pop("L0_ffn_w1").transpose(1, 0, 2).reshape(D, NE0 * H0)
    d["b1_cols"] = columns(d.pop("L0_ffn_b1").reshape(-1))
    d["b2_cols"] = d.pop("L0_ffn_b2").T.reshape(KD, P, NE0).transpose(1, 0, 2)
    d["fb1_cols"] = columns(d.pop("L1_xattn_b1"))
    w1, ws1, hs = d.pop("L1_ffn_W1"), d.pop("L1_ffn_Ws1"), SH
    def chunked(shared, experts):
        experts = experts.reshape(EC // 3, 3, P, D).transpose(1, 0, 2, 3).reshape(-1, D)
        return np.concatenate([shared[:E0 * P], experts, shared[E0 * P:]])

    def by_features(m):
        return m.T.reshape(KD, P, HC, P).transpose(1, 2, 0, 3).reshape(P, HC, D)

    up, gate = by_features(chunked(ws1[:hs], w1[:, :H1])), by_features(chunked(ws1[hs:], w1[:, H1:]))
    down = chunked(d.pop("L1_ffn_Ws2").T, d.pop("L1_ffn_W2").transpose(0, 2, 1)).reshape(HC, P, D).transpose(1, 0, 2)
    d["mlp_chunks"] = np.concatenate([up, gate, down], axis=2)
    d["gate_wT"] = d.pop("L1_ffn_gate_w").T
    return {k: np.ascontiguousarray(v) for k, v in d.items()}


def kernel(**inputs):
    from concourse import bacc
    from concourse.bass_utils import run_bass_kernel_spmd

    nc = bacc.Bacc("TRN2", target_bir_lowering=False, num_devices=1)
    arrays = layout(inputs)
    ins = {name: nc.dram_tensor(name, a.shape, mybir.dt.from_np(a.dtype), kind="ExternalInput").ap()
           for name, a in arrays.items()}
    out = nc.dram_tensor("out", (NB, S, D), F32, kind="ExternalOutput").ap()
    Kernel(nc, ins, out).build()
    return run_bass_kernel_spmd(nc, [arrays], core_ids=[0]).results[0]["out"]
```
